# Optimizing a Trainium2 kernel written in Bass

```python
import numpy as np
import jax
import jax.numpy as jnp

def _softmax(x, axis=-1):
    return jax.nn.softmax(x, axis=axis)

def _gelu(x):
    return jax.nn.gelu(x, approximate=True)

def _silu(x):
    return jax.nn.silu(x)

def _sigmoid(x):
    return jax.nn.sigmoid(x)

def _layernorm(x, axis=-1, eps=1e-05):
    m = jnp.mean(x, axis=axis, keepdims=True)
    v = jnp.var(x, axis=axis, keepdims=True)
    return (x - m) / jnp.sqrt(v + eps)

def _scatter_add(tgt, idx, src, axis=0):
    return tgt.at[idx].add(src)

def _segment_sum(src, seg, n):
    return jax.ops.segment_sum(src, seg, n)
kernel_name = 'mk_gnn_preln_d4_gnn_r8_d1b5dc'

def setup_inputs(seed: int=0):
    np.random.seed(seed)
    _w = jnp.asarray

    def _rec_inputs():
        import jax
        import jax.numpy as jnp
        _gk = jax.random.key(seed)
        x = -0.0005963 + 1.001 * jax.random.normal(jax.random.fold_in(_gk, 1), (384, 1024), jnp.float32)
        src = jax.random.randint(jax.random.fold_in(_gk, 2), (6144,), 0, 384, jnp.int32)
        dst = jnp.minimum((384 * jax.random.uniform(jax.random.fold_in(_gk, 3), (6144,)) ** 2.0).astype(jnp.int32), 3071)
        _o = jnp.argsort(dst, stable=True)
        src = src[_o]
        dst = dst[_o]
        edge_type_5 = jax.random.randint(jax.random.fold_in(_gk, 13), (6144,), 0, 5, jnp.int32)
        edge_type_8 = jax.random.randint(jax.random.fold_in(_gk, 14), (6144,), 0, 8, jnp.int32)
        edge_weight = -0.000130211 + 0.031236 * jax.random.normal(jax.random.fold_in(_gk, 15), (6144,), jnp.float32)
        return (x, src, dst, edge_type_5, edge_type_8, edge_weight)
    x, src, dst, edge_type_5, edge_type_8, edge_weight = _rec_inputs()

    def _L0_gnn_setup():
        import jax, jax.numpy as jnp
        import numpy as np
        N = 384
        E = 12288
        IN_F = 1024
        OUT_F = 1024
        H = 16
        D = OUT_F // H
        NUM_ETYPES = 4

        def _build_mask(edge_index, edge_type, edge_type_weights, dtype):
            src, dst = (edge_index[0], edge_index[1])
            w = jax.nn.softplus(edge_type_weights)
            mask = jnp.full((N, N), -jnp.inf, dtype=dtype)
            mask = mask.at[src, dst].set(w[edge_type - 1])
            diag = jnp.diagonal(mask)
            idx = jnp.arange(N)
            mask = mask.at[idx, idx].set(jnp.where(jnp.isneginf(diag), w[3], diag))
            return mask
        key = jax.random.key(seed)
        ks = jax.random.split(key, 20)
        p = lambda k, shape: jax.random.normal(k, shape, dtype=jnp.float32) * 0.02
        return {'x': jax.random.normal(ks[0], (N, IN_F), dtype=jnp.float32), 'edge_index': jax.random.randint(ks[1], (2, E), 0, N), 'edge_type': jax.random.randint(ks[2], (E,), 1, NUM_ETYPES + 1), 'edge_type_weights': jnp.ones((NUM_ETYPES,), jnp.float32) + 0.1 * jax.random.normal(ks[3], (NUM_ETYPES,), dtype=jnp.float32), 'wq': p(ks[4], (OUT_F, IN_F)), 'bq': p(ks[5], (OUT_F,)), 'wk': p(ks[6], (OUT_F, IN_F)), 'bk': p(ks[7], (OUT_F,)), 'wv': p(ks[8], (OUT_F, IN_F)), 'bv': p(ks[9], (OUT_F,)), 'wiq': p(ks[10], (OUT_F, OUT_F)), 'biq': p(ks[11], (OUT_F,)), 'wik': p(ks[12], (OUT_F, OUT_F)), 'bik': p(ks[13], (OUT_F,)), 'wiv': p(ks[14], (OUT_F, OUT_F)), 'biv': p(ks[15], (OUT_F,)), 'wo': p(ks[16], (OUT_F, OUT_F)), 'bo': p(ks[17], (OUT_F,))}
    _L0_gnn_all = _L0_gnn_setup()
    _L0_gnn_in = {k: v for k, v in _L0_gnn_all.items() if k in ('edge_type_weights', 'wq', 'bq', 'wk', 'bk', 'wv', 'bv', 'wiq', 'biq', 'wik', 'bik', 'wiv', 'biv', 'wo', 'bo')}
    del _L0_gnn_all

    def _L1_gnn_setup():
        import jax, jax.numpy as jnp
        import numpy as np
        N, D, R, E = (1250, 1024, 8, 10000)

        def _rgcn(x, edge_index, edge_type, weight, root, bias):
            src, dst = (edge_index[0], edge_index[1])
            msgs = x[src]
            out = x @ root + bias
            n = x.shape[0]
            for r in range(weight.shape[0]):
                mask = (edge_type == r).astype(x.dtype)
                sums = jax.ops.segment_sum(msgs * mask[:, None], dst, num_segments=n)
                cnt = jax.ops.segment_sum(mask, dst, num_segments=n)
                mean = sums / jnp.maximum(cnt, 1.0)[:, None]
                out = out + mean @ weight[r]
            return out
        key = jax.random.key(seed)
        ks = jax.random.split(key, 8)
        s = 1.0 / np.sqrt(D)
        x = jax.random.normal(ks[0], (N, D), dtype=jnp.float32)
        edge_index = jax.random.randint(ks[1], (2, E), 0, N, dtype=jnp.int64)
        edge_type = jax.random.randint(ks[2], (E,), 0, R, dtype=jnp.int64)
        weight = jax.random.normal(ks[3], (R, D, D), dtype=jnp.float32) * s
        root = jax.random.normal(ks[4], (D, D), dtype=jnp.float32) * s
        bias = jnp.zeros((D,), dtype=jnp.float32)
        w_gate = jax.random.normal(ks[5], (2 * D, D), dtype=jnp.float32) * (1.0 / np.sqrt(2 * D))
        b_gate = jnp.zeros((D,), dtype=jnp.float32)
        return {'x': x, 'edge_index': edge_index, 'edge_type': edge_type, 'weight': weight, 'root': root, 'bias': bias, 'w_gate': w_gate, 'b_gate': b_gate}
    _L1_gnn_all = _L1_gnn_setup()
    _L1_gnn_in = {k: v for k, v in _L1_gnn_all.items() if k in ('weight', 'root', 'bias', 'w_gate', 'b_gate')}
    del _L1_gnn_all

    def _L2_gnn_setup():
        import jax, jax.numpy as jnp
        import numpy as np
        N_NODES = 3125
        N_EDGES = 50000
        D = 1024

        def _sage_layer(h, edge_src, edge_dst, deg_inv, W_self, W_neigh, b):
            msg = h[edge_src]
            agg = jax.ops.segment_sum(msg, edge_dst, num_segments=h.shape[0])
            mean = agg * deg_inv[:, None]
            return h @ W_self + mean @ W_neigh + b
        key = jax.random.key(seed)
        ks = jax.random.split(key, 8)
        s = 1.0 / np.sqrt(D)
        return {'x': jax.random.normal(ks[0], (N_NODES, D), dtype=jnp.float32), 'edge_src': jax.random.randint(ks[1], (N_EDGES,), 0, N_NODES, dtype=jnp.int32), 'edge_dst': jax.random.randint(ks[2], (N_EDGES,), 0, N_NODES, dtype=jnp.int32), 'W_self0': jax.random.normal(ks[3], (D, D), dtype=jnp.float32) * s, 'W_neigh0': jax.random.normal(ks[4], (D, D), dtype=jnp.float32) * s, 'b0': jnp.zeros((D,), dtype=jnp.float32), 'W_self1': jax.random.normal(ks[5], (D, D), dtype=jnp.float32) * s, 'W_neigh1': jax.random.normal(ks[6], (D, D), dtype=jnp.float32) * s, 'b1': jnp.zeros((D,), dtype=jnp.float32)}
    _L2_gnn_all = _L2_gnn_setup()
    _L2_gnn_in = {k: v for k, v in _L2_gnn_all.items() if k in ('W_self0', 'W_neigh0', 'b0', 'W_self1', 'W_neigh1', 'b1')}
    del _L2_gnn_all

    def _L3_gnn_setup():
        import jax, jax.numpy as jnp
        import numpy as np
        INDIM = 1024
        OUTDIM = 1024
        NNZ = 8192
        N = 6250
        key = jax.random.key(seed)
        k1, k2, k3, k4, k5 = jax.random.split(key, 5)
        x = jax.random.normal(k1, (N, INDIM), dtype=jnp.float32)
        stdv = np.sqrt(6.0 / (INDIM + OUTDIM))
        nnz_weight = jax.random.uniform(k2, (NNZ,), dtype=jnp.float32, minval=-stdv, maxval=stdv)
        bias = jax.random.normal(k3, (OUTDIM,), dtype=jnp.float32) * 0.02
        row = jax.random.randint(k4, (NNZ,), 0, OUTDIM, dtype=jnp.int64)
        col = jax.random.randint(k5, (NNZ,), 0, INDIM, dtype=jnp.int64)
        edge_index = jnp.stack([row, col])
        return {'x': x, 'nnz_weight': nnz_weight, 'bias': bias, 'edge_index': edge_index}
    _L3_gnn_all = _L3_gnn_setup()
    _L3_gnn_in = {k: v for k, v in _L3_gnn_all.items() if k in ('bias',)}
    del _L3_gnn_all
    return {'x': x, 'src': src, 'dst': dst, 'edge_type_5': edge_type_5, 'edge_type_8': edge_type_8, 'edge_weight': edge_weight, 'L0_gnn_edge_type_weights': _L0_gnn_in['edge_type_weights'], 'L0_gnn_wq': _L0_gnn_in['wq'], 'L0_gnn_bq': _L0_gnn_in['bq'], 'L0_gnn_wk': _L0_gnn_in['wk'], 'L0_gnn_bk': _L0_gnn_in['bk'], 'L0_gnn_wv': _L0_gnn_in['wv'], 'L0_gnn_bv': _L0_gnn_in['bv'], 'L0_gnn_wiq': _L0_gnn_in['wiq'], 'L0_gnn_biq': _L0_gnn_in['biq'], 'L0_gnn_wik': _L0_gnn_in['wik'], 'L0_gnn_bik': _L0_gnn_in['bik'], 'L0_gnn_wiv': _L0_gnn_in['wiv'], 'L0_gnn_biv': _L0_gnn_in['biv'], 'L0_gnn_wo': _L0_gnn_in['wo'], 'L0_gnn_bo': _L0_gnn_in['bo'], 'L1_gnn_weight': _L1_gnn_in['weight'], 'L1_gnn_root': _L1_gnn_in['root'], 'L1_gnn_bias': _L1_gnn_in['bias'], 'L1_gnn_w_gate': _L1_gnn_in['w_gate'], 'L1_gnn_b_gate': _L1_gnn_in['b_gate'], 'L2_gnn_W_self0': _L2_gnn_in['W_self0'], 'L2_gnn_W_neigh0': _L2_gnn_in['W_neigh0'], 'L2_gnn_b0': _L2_gnn_in['b0'], 'L2_gnn_W_self1': _L2_gnn_in['W_self1'], 'L2_gnn_W_neigh1': _L2_gnn_in['W_neigh1'], 'L2_gnn_b1': _L2_gnn_in['b1'], 'L3_gnn_bias': _L3_gnn_in['bias']}

def reference(x, src, dst, edge_type_5, edge_type_8, edge_weight, L0_gnn_edge_type_weights, L0_gnn_wq, L0_gnn_bq, L0_gnn_wk, L0_gnn_bk, L0_gnn_wv, L0_gnn_bv, L0_gnn_wiq, L0_gnn_biq, L0_gnn_wik, L0_gnn_bik, L0_gnn_wiv, L0_gnn_biv, L0_gnn_wo, L0_gnn_bo, L1_gnn_weight, L1_gnn_root, L1_gnn_bias, L1_gnn_w_gate, L1_gnn_b_gate, L2_gnn_W_self0, L2_gnn_W_neigh0, L2_gnn_b0, L2_gnn_W_self1, L2_gnn_W_neigh1, L2_gnn_b1, L3_gnn_bias):
    import jax
    import jax.numpy as jnp

    def _L0_gnn_ref(x, edge_index, edge_type, edge_type_weights, wq, bq, wk, bk, wv, bv, wiq, biq, wik, bik, wiv, biv, wo, bo):
        import jax, jax.numpy as jnp
        import numpy as np
        N = 384
        E = 12288
        IN_F = 1024
        OUT_F = 1024
        H = 16
        D = OUT_F // H
        NUM_ETYPES = 4

        def _build_mask(edge_index, edge_type, edge_type_weights, dtype):
            src, dst = (edge_index[0], edge_index[1])
            w = jax.nn.softplus(edge_type_weights)
            mask = jnp.full((N, N), -jnp.inf, dtype=dtype)
            mask = mask.at[src, dst].set(w[edge_type - 1])
            diag = jnp.diagonal(mask)
            idx = jnp.arange(N)
            mask = mask.at[idx, idx].set(jnp.where(jnp.isneginf(diag), w[3], diag))
            return mask
        q = x @ wq.T + bq
        k = x @ wk.T + bk
        v = x @ wv.T + bv
        q2 = (q @ wiq.T + biq).reshape(N, H, D).transpose(1, 0, 2)
        k2 = (k @ wik.T + bik).reshape(N, H, D).transpose(1, 0, 2)
        v2 = (v @ wiv.T + biv).reshape(N, H, D).transpose(1, 0, 2)
        mask = _build_mask(edge_index, edge_type, edge_type_weights, x.dtype)
        scale = 1.0 / np.sqrt(D).astype(np.float32)
        scores = jnp.einsum('hnd,hmd->hnm', q2, k2) * scale + mask[None]
        attn = jax.nn.softmax(scores, axis=-1)
        out = jnp.einsum('hnm,hmd->hnd', attn, v2)
        out = out.transpose(1, 0, 2).reshape(N, OUT_F)
        return out @ wo.T + bo

    def _L1_gnn_ref(x, edge_index, edge_type, weight, root, bias, w_gate, b_gate):
        import jax, jax.numpy as jnp
        import numpy as np
        N, D, R, E = (1250, 1024, 8, 10000)

        def _rgcn(x, edge_index, edge_type, weight, root, bias):
            src, dst = (edge_index[0], edge_index[1])
            msgs = x[src]
            out = x @ root + bias
            n = x.shape[0]
            for r in range(weight.shape[0]):
                mask = (edge_type == r).astype(x.dtype)
                sums = jax.ops.segment_sum(msgs * mask[:, None], dst, num_segments=n)
                cnt = jax.ops.segment_sum(mask, dst, num_segments=n)
                mean = sums / jnp.maximum(cnt, 1.0)[:, None]
                out = out + mean @ weight[r]
            return out
        u = _rgcn(x, edge_index, edge_type, weight, root, bias)
        z = jnp.concatenate([u, x], axis=1) @ w_gate + b_gate
        h = jnp.tanh(u) * z + x * (1.0 - z)
        return h

    def _L2_gnn_ref(x, edge_src, edge_dst, W_self0, W_neigh0, b0, W_self1, W_neigh1, b1):
        import jax, jax.numpy as jnp
        import numpy as np
        N_NODES = 3125
        N_EDGES = 50000
        D = 1024

        def _sage_layer(h, edge_src, edge_dst, deg_inv, W_self, W_neigh, b):
            msg = h[edge_src]
            agg = jax.ops.segment_sum(msg, edge_dst, num_segments=h.shape[0])
            mean = agg * deg_inv[:, None]
            return h @ W_self + mean @ W_neigh + b
        N = x.shape[0]
        deg = jax.ops.segment_sum(jnp.ones_like(edge_dst, dtype=x.dtype), edge_dst, num_segments=N)
        deg_inv = 1.0 / jnp.maximum(deg, 1.0)
        h = jax.nn.relu(_sage_layer(x, edge_src, edge_dst, deg_inv, W_self0, W_neigh0, b0))
        out = _sage_layer(h, edge_src, edge_dst, deg_inv, W_self1, W_neigh1, b1)
        return out

    def _L3_gnn_ref(x, nnz_weight, bias, edge_index):
        import jax, jax.numpy as jnp
        import numpy as np
        INDIM = 1024
        OUTDIM = 1024
        NNZ = 8192
        N = 6250
        row, col = (edge_index[0], edge_index[1])
        W = jnp.zeros((OUTDIM, INDIM), dtype=nnz_weight.dtype).at[row, col].add(nnz_weight)
        return x @ W.T + bias
    edge_index = jnp.stack([src, dst])
    h = jnp.maximum(_layernorm(x, axis=-1), 0.0)
    x = x + _L0_gnn_ref(h, edge_index, edge_type_5, L0_gnn_edge_type_weights, L0_gnn_wq, L0_gnn_bq, L0_gnn_wk, L0_gnn_bk, L0_gnn_wv, L0_gnn_bv, L0_gnn_wiq, L0_gnn_biq, L0_gnn_wik, L0_gnn_bik, L0_gnn_wiv, L0_gnn_biv, L0_gnn_wo, L0_gnn_bo)
    h = jnp.maximum(_layernorm(x, axis=-1), 0.0)
    x = x + _L1_gnn_ref(h, edge_index, edge_type_8, L1_gnn_weight, L1_gnn_root, L1_gnn_bias, L1_gnn_w_gate, L1_gnn_b_gate)
    h = jnp.maximum(_layernorm(x, axis=-1), 0.0)
    x = x + _L2_gnn_ref(h, src, dst, L2_gnn_W_self0, L2_gnn_W_neigh0, L2_gnn_b0, L2_gnn_W_self1, L2_gnn_W_neigh1, L2_gnn_b1)
    h = jnp.maximum(_layernorm(x, axis=-1), 0.0)
    x = x + _L3_gnn_ref(h, edge_weight, L3_gnn_bias, edge_index)
    return x

_drawn_inputs = setup_inputs


def setup_inputs(seed=0):
    import zlib

    import numpy as np

    out = dict(_drawn_inputs(seed))
    spreads = {'L1_gnn_bias': (0.0, 0.1),
     'L1_gnn_b_gate': (0.0, 0.1),
     'L2_gnn_b0': (0.0, 0.1),
     'L2_gnn_b1': (0.0, 0.1)}
    factors = {'L0_gnn_edge_type_weights': 64.0,
     'L0_gnn_wq': 8.0,
     'L0_gnn_bq': 8.0,
     'L0_gnn_wk': 8.0,
     'L0_gnn_bk': 64.0,
     'L0_gnn_bv': 5.904,
     'L0_gnn_wiq': 8.0,
     'L0_gnn_biq': 29.95,
     'L0_gnn_wik': 8.0,
     'L0_gnn_bik': 64.0,
     'L0_gnn_biv': 3.66,
     'L3_gnn_bias': 6.182}
    for name, (base, spread) in spreads.items():
        noise = np.random.default_rng([zlib.crc32(name.encode()), seed]).standard_normal(out[name].shape)
        drawn = base * np.exp(spread * noise) if base else spread * noise
        out[name] = jnp.asarray(drawn.astype(out[name].dtype))
    for name, factor in factors.items():
        out[name] = (out[name] * factor).astype(out[name].dtype)
    return out
```

```python
from contextlib import ExitStack

import concourse.bass as bass
from concourse import mybir

ALU = mybir.AluOpType
ACT = mybir.ActivationFunctionType
AX = mybir.AxisListType
F32 = mybir.dt.float32
F32R = mybir.dt.float32r
BF16 = mybir.dt.bfloat16
I32 = mybir.dt.int32
I16 = mybir.dt.int16
U16 = mybir.dt.uint16

P = 128
RING = 4
EPS = 1e-5
MASKED = -1e30


def need(eng, sem, value):
    if not (isinstance(value, int) and value <= 0):
        eng.wait_ge(sem, value)


class Chain:

    def __init__(self, eng, sem):
        self.eng, self.sem, self.n = eng, sem, 0

    def __call__(self, instruction):
        self.n = self.n + 1
        instruction.then_inc(self.sem, 1)
        self.eng.wait_ge(self.sem, self.n)


def build(nc, x, src, dst, et5, et8, ew, etw, wq, bq, wk, bk, wv, bv, wiq, biq, wik, bik, wiv, biv,
          wo, bo, rel_w, root, bias1, w_gate, b_gate, w_self0, w_neigh0, b0, w_self1, w_neigh1, b1,
          bias3, out):
    N, D = x.shape
    E = src.shape[0]
    R = rel_w.shape[0]
    H = 16
    DH = D // H
    NT = N // P
    KT = D // P
    EC = E // P
    HALF = D // 2
    SCALE = float(DH) ** -0.5
    CELLS = R * NT
    PASS = 8
    NPASS = CELLS // PASS
    EXP_STEP, EXP_BASE = 5, -120
    assert N == NT * P and D == KT * P and E == EC * P and DH == 64 and CELLS % PASS == 0
    assert EXP_BASE + EXP_STEP * EC <= 127

    ctx = ExitStack()
    with ctx:
        def sb(name, shape, dt, scope=ctx):
            return scope.enter_context(nc.sbuf_tensor(name, shape, dt))

        def sem(name):
            return ctx.enter_context(nc.semaphore(name))

        xres = sb("xres", [P, NT, D], F32)
        ident = sb("ident", [P, P], F32)
        ones_r = sb("ones_r", [P, P], F32R)
        counts16 = sb("counts16", [P, CELLS, N], U16)
        total_r = sb("total_r", [P, NT, N], F32R)
        sparse_w = sb("sparse_w", [P, NT, N], F32)
        mask = sb("mask", [P, NT, N], F32)
        brow = sb("brow", [P, D], F32)
        bcol = sb("bcol", [P, 7 * KT], F32)
        b_in = sb("b_in", [7 * KT, P], F32)
        stats = sb("stats", [P, NT, 2, 6], F32)
        mv = sb("mv", [P, NT, 2], F32)
        std = sb("std", [P, NT, 1], F32)
        rstd = sb("rstd", [P, NT, 1], F32)
        shift = sb("shift", [P, NT, 1], F32)
        epsc = sb("epsc", [P, 1], F32)
        raw = [sb(f"raw{i}", [P, D], F32) for i in range(RING)]
        whi = [sb(f"whi{i}", [P, KT, P], F32R) for i in range(RING)]
        wlo = [sb(f"wlo{i}", [P, KT, P], F32R) for i in range(RING)]
        whi_row = [w[:, :, :].rearrange("p k n -> p (k n)") for w in whi]
        wlo_row = [w[:, :, :].rearrange("p k n -> p (k n)") for w in wlo]

        graph_base = nc.sbuf_base
        with ExitStack() as scope:
            hot_dst = sb("hot_dst", [P, EC, N], BF16, scope)
            hot_rs = sb("hot_rs", [P, 4, PASS * P], BF16, scope)
            hot_val = sb("hot_val", [P, 2, N], BF16, scope)
            hot_w = sb("hot_w", [P, 2, 3, N], BF16, scope)
            e_in = sb("e_in", [EC, 4, P], I32, scope)
            e_w = sb("e_w", [EC, P], F32, scope)
            e_row = sb("e_row", [EC, 6, P], F32, scope)
            e_col = sb("e_col", [P, 6, EC], F32, scope)
            later = sb("later", [P, P], F32, scope)
            same = sb("same", [P, 4, P], F32, scope)
            dup = sb("dup", [P, EC], F32, scope)
            live = sb("live", [P, EC], F32, scope)
            chunk_exp = sb("chunk_exp", [P, EC], I32, scope)
            chunk_val = sb("chunk_val", [P, EC], I32, scope)
            edge_val = sb("edge_val", [P, EC], F32, scope)
            w_bf = sb("w_bf", [P, 3, EC], BF16, scope)
            w_part = sb("w_part", [P, 3, EC], F32, scope)
            w_rest = sb("w_rest", [P, 2, EC], F32, scope)
            etw_b = sb("etw_b", [P, 4], F32, scope)
            h0 = sb("h0", [P, NT, D], F32, scope)
            spare = 3 * 2 * KT * N * 4 - (nc.sbuf_base - graph_base)
            if spare > 0:
                sb("spare", [P, spare // 4 + 8], F32, scope)
            iota = sb("iota", [P, R * N], I16, scope)
            key_i = sb("key_i", [P, 2, E // 4], I32, scope)
            key_row = sb("key_row", [P, E // 4], F32, scope)
            sp = sb("sp", [P, 6, 4], F32, scope)

        with ExitStack() as scope:
            acts = sb("acts", [P, 4, 2, KT, N], F32R, scope)
        with ExitStack() as scope:
            sb("places_0_1", [P, 2, 2, KT, N], F32R, scope)
            pt = [sb(f"pt_{s}", [P, 2, NT, N], F32R, scope) for s in ("hi", "lo")]
            q_st = [sb(f"q_st_{s}", [P, 2, N], F32R, scope) for s in ("hi", "lo")]
            sb("place_3", [P, 2, KT, N], F32R, scope)
            v_st = [sb(f"v_st_{s}", [P, 2, NT, P], F32R, scope) for s in ("hi", "lo")]
            rmax = sb("rmax", [P, 2, NT], F32, scope)
            nmax = sb("nmax", [P, 2, NT], F32, scope)
            rsum = sb("rsum", [P, 2, NT], F32, scope)
            rinv = sb("rinv", [P, 2, NT], F32, scope)
        v_rows = acts[:, 3, :, :, :].rearrange("p s k n -> p s (k n)").rearrange(
            "p s (t d) -> p s t d", t=NT)
        sc = xres[:, :, :].rearrange("p t d -> p (t d)")[:, 0:2 * NT * N].rearrange(
            "p (b t n) -> p b t n", b=2, t=NT)
        y_t = brow[:, 0:2 * N].rearrange("p (b n) -> p b n", b=2)

        with ExitStack() as scope:
            h = sb("h", [P, NT, D], F32, scope)
            h_row = [sb(f"h_row_{s}", [P, NT, D], F32R, scope) for s in ("hi", "lo")]
            h_t = [sb(f"h_t_{s}", [P, KT, N], F32R, scope) for s in ("hi", "lo")]
            mean_f = sb("mean_f", [P, 2, N], F32, scope)
            mean = [sb(f"mean_{s}", [P, 2, N], F32R, scope) for s in ("hi", "lo")]
            rel_r = sb("rel_r", [P, NT, N], F32R, scope)
            cnt = sb("cnt", [P, N], F32, scope)
            inv = sb("inv", [P, N], F32, scope)
            u = sb("u", [P, NT, D], F32, scope)
            w3 = [sb(f"w3_{s}", [P, NT, N], F32R, scope) for s in ("hi", "lo")]
        u_t = [a[:, :, :].rearrange("p t d -> p (t d)").rearrange("p (k n) -> p k n", k=KT)
               for a in h_row]

        ps = ctx.enter_context(nc.psum_tensor("ps", [P, 8, 512], F32))

        names = """x_in edges_in key_rows_in etw_in bcol_in brow_in out_stored
            iota_made ident_made later_made exp_made ones_made
            edge_rows edges_turned edge_cols keys_read hot_dst_made hot_rs_made hot_rs_used
            counts_by_vec counts_by_act edge_vals_made hot_m_made hot_m_used mask_decoded
            sparse_kept sp_max sp_exp sp_ln mask_made total_made
            var_ready std_ready shift_ready h_ready
            turned turn_hi turn_lo
            weight_turned w_hi w_lo w_used out_hi out_lo
            v_turned v_hi v_lo
            q_staged v_staged scores_ready scores_read max_ready exp_ready sum_inverted
            probs_ready probs_turned pt_hi pt_lo pv_done head_hi head_lo
            y_evacuated y_turned y_added
            row_hi row_lo rel_ready agg_ready agg_read mean_hi mean_lo
            u_ready u_tanh gate_sum gate_product x_gated
            mid_ready x_based x_done w3_hi w3_lo out_based out_psum out_done
            vec_chain pool_chain act_chain sum_ready inv_made sp_made dup_found held_vec held_pool""".split()
        S = {n: sem(n) for n in names}
        raw_in = [sem(f"raw_in{i}") for i in range(RING)]

        T_WO = 6 * KT
        T_ROOT = 7 * KT
        T_REL = T_ROOT + KT
        T_GX = T_REL + R * KT
        T_GU = T_GX + KT
        T_S0 = T_GU + KT
        T_N0 = T_S0 + KT
        T_S1 = T_N0 + KT
        T_N1 = T_S1 + KT
        T_END = T_N1 + KT
        W_CREDIT = RING
        O_CREDIT = 2
        M_CREDIT = 2
        Y_H0, Y_H1 = 0, KT
        Y_U, Y_H2 = 2 * KT, 3 * KT
        Y_MID, Y_H3 = 4 * KT, 5 * KT
        SRC, DST, KEY, KEY2, TYPE, WEIGHT = range(6)
        QUARTER = EC // 4

        def use_of_slot(g, j):
            return (g * (KT // RING) + (j // RING + 1)) * 16

        def hold(eng):
            eng.sem_inc(S["held_vec"] if eng is nc.vector else S["held_pool"], 1)

        def is_head(i, o, n):
            return isinstance(i, int) and i * 4 + o == n

        block = ctx.enter_context(nc.Block())

        @block.sync
        def _(sp_):
            sp_.dma_start(e_in[:, 0, :], src.rearrange("(c p) -> c p", p=P)).then_inc(S["edges_in"], 16)
            sp_.dma_start(e_in[:, 1, :], dst.rearrange("(c p) -> c p", p=P)).then_inc(S["edges_in"], 16)
            sp_.dma_start(e_in[:, 2, :], et5.rearrange("(c p) -> c p", p=P)).then_inc(S["edges_in"], 16)
            sp_.dma_start(e_in[:, 3, :], et8.rearrange("(c p) -> c p", p=P)).then_inc(S["edges_in"], 16)
            sp_.dma_start(e_w[:, :], ew.rearrange("(c p) -> c p", p=P)).then_inc(S["edges_in"], 16)
            sp_.dma_start(xres[:, :, :], x.rearrange("(t p) d -> p t d", p=P)).then_inc(S["x_in"], 16)

            def load(t0, rows_of, n, looped=True):
                def four(i4, i):
                    for s in range(RING):
                        t = t0 + i4 + s
                        if t0 >= T_ROOT + RING:
                            sp_.wait_ge(S["w_lo"], t - RING + 1)
                        elif t0 >= RING:
                            sp_.wait_ge(S["weight_turned"], t - RING + 1)
                        sp_.dma_start(raw[s][:, :], rows_of(i4 + s)).then_inc(raw_in[s], 16)
                if n == 1 or not looped:
                    for i in range(n):
                        four(RING * i, i)
                else:
                    with sp_.Fori(0, n) as i:
                        four(i * RING, i)

            def rows(w):
                return lambda i: w[bass.ds(i * P, P), :]

            load(0, rows(wq), 1)
            load(RING, lambda i: wq[bass.ds((i + RING) * P, P), :], 1)
            for g, w in enumerate((wk, wv, wiq, wik, wiv, wo)):
                load((g + 1) * KT, rows(w), KT // RING)
            load(T_ROOT, rows(root), 1)
            load(T_ROOT + RING, lambda i: root[bass.ds((i + RING) * P, P), :], 1)
            load(T_REL, rows(rel_w.rearrange("r k n -> (r k) n")), R * KT // RING)
            load(T_GX, lambda i: w_gate[bass.ds(i * P + D, P), :], KT // RING)
            load(T_GU, rows(w_gate), KT // RING)
            for t0, w in ((T_S0, w_self0), (T_N0, w_neigh0), (T_S1, w_self1), (T_N1, w_neigh1)):
                load(t0, rows(w), KT // RING)
            for nt in range(NT):
                sp_.wait_ge(S["out_based"], nt + 1)
                sp_.dma_start(out.rearrange("(t p) d -> p t d", p=P)[:, nt, N:D],
                              u[:, nt, N:D]).then_inc(S["out_stored"], 16)
            for nt in range(NT):
                sp_.wait_ge(S["out_done"], nt + 1)
                sp_.dma_start(out.rearrange("(t p) d -> p t d", p=P)[:, nt, 0:N],
                              u[:, nt, 0:N]).then_inc(S["out_stored"], 16)
            sp_.wait_ge(S["out_stored"], 16 * 2 * NT)

        @block.tensor
        def _(pe):
            pe.wait_ge(S["ident_made"], 2)
            pe.wait_ge(S["edge_rows"], 1)
            for f in range(6):
                mm = pe.transpose(ps[:, 0, EC * f:EC * f + EC], e_row[:, f, :], ident[0:EC, 0:EC])
            mm.then_inc(S["edges_turned"], 1)
            pe.wait_ge(S["bcol_in"], 16 * 7)
            pe.transpose(ps[:, 1, 0:7 * KT], b_in[:, :], ident[0:7 * KT, 0:7 * KT]).then_inc(S["edges_turned"], 1)
            pe.wait_ge(S["edge_cols"], 2)

            pe.wait_ge(S["hot_dst_made"], EC)

            def count_chunks(n0, c0, first, last):
                for j in range(4):
                    n, c = n0 + j, c0 + j
                    pe.wait_ge(S["hot_rs_made"], n + 1)
                    for b in range(PASS):
                        mm = pe.matmul(ps[:, b, 0:N], hot_rs[:, j, P * b:P * b + P], hot_dst[:, c, :],
                                       start=first and j == 0, stop=last and j == 3)
                    mm.then_inc(S["hot_rs_used"], 1)

            with pe.Fori(0, NPASS) as p:
                pe.wait_ge(S["counts_by_vec"], p * (PASS // 2) + 1)
                pe.wait_ge(S["counts_by_act"], p * (PASS // 2) + 1)
                count_chunks(p * EC, 0, True, False)
                with pe.Fori(1, EC // 4 - 1) as c4:
                    count_chunks(p * EC + c4 * 4, c4 * 4, False, False)
                count_chunks(p * EC + (EC - 4), EC - 4, False, True)

            pe.wait_ge(S["counts_by_vec"], NPASS * (PASS // 2) + 1)
            pe.wait_ge(S["counts_by_act"], NPASS * (PASS // 2) + 1)

            def mask_chunks(c0, first, last):
                for j in range(2):
                    c = c0 + j
                    pe.wait_ge(S["hot_m_made"], c + 1)
                    for s in range(NT):
                        pe.matmul(ps[:, s, 0:N], hot_val[:, j, P * s:P * s + P], hot_dst[:, c, :],
                                  start=first and j == 0, stop=last and j == 1)
                        for w in range(3):
                            mm = pe.matmul(ps[:, NT + s, 0:N], hot_dst[:, c, P * s:P * s + P],
                                           hot_w[:, j, w, :], start=first and j == 0 and w == 0,
                                           stop=last and j == 1 and w == 2)
                    mm.then_inc(S["hot_m_used"], 1)

            mask_chunks(0, True, False)
            with pe.Fori(1, EC // 2 - 1) as c2:
                mask_chunks(c2 * 2, False, False)
            mask_chunks(EC - 2, False, True)

            def turn(y, source, f):
                need(pe, S["turn_lo"], y - 1)
                for nt in range(NT):
                    mm = pe.transpose(ps[:, 6 + y % 2, P * nt:P * nt + P],
                                      source[:, nt, P * f:P * f + P], ident[:, :])
                mm.then_inc(S["turned"], 1)

            def turn_weight(g, j):
                pe.wait_ge(raw_in[j % RING], use_of_slot(g, j))
                need(pe, S["w_lo"], g * KT + (j - 1))
                for k in range(KT):
                    mm = pe.transpose(ps[:, 2 + 2 * (j % 2) + k // 4, P * (k % 4):P * (k % 4) + P],
                                      raw[j % RING][:, P * k:P * k + P], ident[:, :])
                mm.then_inc(S["weight_turned"], 1)

            def column_tile(g, j, a):
                pe.wait_ge(S["w_lo"], g * KT + (j + 1))
                i = 0
                for k in range(KT):
                    for stationary, moving in ((whi, 0), (whi, 1), (wlo, 0)):
                        mm = pe.matmul(ps[:, j % 2, 0:N], stationary[j % RING][:, k, :],
                                       acts[:, a, moving, k, :], start=i == 0, stop=i == 3 * KT - 1)
                        i += 1
                mm.then_inc(S["w_used"], 1)

            pe.wait_ge(S["h_ready"], NT)
            pe.wait_ge(S["mask_decoded"], 1)
            pe.wait_ge(S["sparse_kept"], 1)
            for f in range(KT):
                turn(Y_H0 + f, h0, f)
            turn_weight(0, 0)
            turn_weight(0, 1)
            pe.wait_ge(S["turn_lo"], Y_H0 + KT)

            def eight_tiles(g, a):
                for j in range(KT):
                    turn_weight(g, j + 2)
                    pe.wait_ge(S["out_lo"], g * KT + (j - 1 + O_CREDIT))
                    column_tile(g, j, a)

            with pe.Fori(0, 3) as g:
                eight_tiles(g, 0)
            pe.wait_ge(S["out_lo"], O_CREDIT + 3 * KT)
            with pe.Fori(3, 6) as g:
                eight_tiles(g, g - 2)

            pe.wait_ge(S["out_lo"], O_CREDIT + 6 * KT)
            pe.wait_ge(S["w_lo"], T_WO + 2)
            for m in range(NT):
                for s in range(2):
                    need(pe, (S["v_hi"], S["v_lo"])[s], m)
                    for f in range(KT):
                        mm = pe.transpose(ps[:, 2 + 2 * s + f // 4, P * (f % 4):P * (f % 4) + P],
                                          acts[:, 2, s, f, P * m:P * m + P].bitcast(F32), ident[:, :])
                    mm.then_inc(S["v_turned"], 1)
            pe.wait_ge(S["v_hi"], NT)
            pe.wait_ge(S["v_lo"], NT)

            def scores(i, o):
                pe.wait_ge(S["q_staged"], i * 8 + (2 * o + 2))
                for nt in range(NT):
                    need(pe, S["scores_read"], (i * 4 + (o - 1)) * NT + (nt + 1))
                    for n, (a, c) in enumerate(((0, 0), (0, 1), (1, 0))):
                        mm = pe.matmul(ps[:, nt, 0:N], q_st[a][:, o % 2, P * nt:P * nt + P],
                                       acts[:, 1, c, i * 2 + o // 2, :], start=n == 0, stop=n == 2)
                    mm.then_inc(S["scores_ready"], 1)

            def turn_probs(i, o):
                pe.wait_ge(S["probs_ready"], i * 4 + (o + 1))
                for m in range(NT):
                    need(pe, S["pt_lo"], (i * 4 + (o - 1)) * NT + (m + 1))
                    for nt in range(NT):
                        mm = pe.transpose(ps[:, NT + m, P * nt:P * nt + P],
                                          sc[:, o % 2, nt, P * m:P * m + P], ident[:, :])
                    mm.then_inc(S["probs_turned"], 1)

            def weigh_values(i, o):
                pe.wait_ge(S["pt_lo"], (i * 4 + (o + 1)) * NT)
                if o % 2 == 0:
                    pe.wait_ge(S["v_staged"], i * 4 + (o // 2 * 2 + 2))
                pe.wait_ge(S["head_lo"], i * 4 + (o - 1 + O_CREDIT))
                n = 0
                for m in range(NT):
                    for a, c in ((0, 0), (0, 1), (1, 0)):
                        mm = pe.matmul(ps[:, 6 + o % 2, 0:N], v_st[a][:, o // 2 % 2, m, :],
                                       pt[c][:, o % 2, m, :], start=n == 0, stop=n == 3 * NT - 1)
                        n += 1
                mm.then_inc(S["pv_done"], 1)

            def head(i, o):
                if not is_head(i, o, H - 1):
                    scores(i, o + 1)
                turn_probs(i, o)
                if not is_head(i, o, 0):
                    weigh_values(i, o - 1)

            scores(0, 0)
            head(0, 0)
            with pe.Fori(0, 3) as i:
                for o in range(1, 5):
                    head(i, o)
            for o in range(1, 4):
                head(3, o)
            weigh_values(3, 3)

            pe.wait_ge(S["head_lo"], O_CREDIT + H)
            pe.wait_ge(S["scores_read"], H * NT)

            def turn_y(j):
                pe.wait_ge(S["y_evacuated"], j + 1)
                need(pe, S["y_added"], j - 1)
                for nt in range(NT):
                    mm = pe.transpose(ps[:, 6 + j % 2, P * nt:P * nt + P],
                                      y_t[:, j % 2, P * nt:P * nt + P], ident[:, :])
                mm.then_inc(S["y_turned"], 1)

            for j in range(KT):
                if j + 2 < KT:
                    turn_weight(6, j + 2)
                need(pe, S["y_evacuated"], j - 1)
                column_tile(6, j, 0)
                if j:
                    turn_y(j - 1)
            turn_y(KT - 1)

            def row_block(t, slot, stationary, k, first=False, last=False, bank_free=None):
                pe.wait_ge(S["w_lo"], t + 1)
                for nt in range(NT):
                    if bank_free:
                        bank_free(nt)
                    for a, weight in ((0, whi_row), (0, wlo_row), (1, whi_row)):
                        for f in range(2):
                            mm = pe.matmul(ps[:, 2 * nt + f, :], stationary[a][:, k, P * nt:P * nt + P],
                                           weight[slot][:, HALF * f:HALF * f + HALF],
                                           start=first and a == 0 and weight is whi_row,
                                           stop=last and a == 1, skip_group_check=True)
                    if last and nt < NT - 1:
                        mm.then_inc(S["sum_ready"], 1)
                mm.then_inc(S["w_used"], 1)

            def start_relation(q, edges, a6):
                a6()
                for s in range(NT):
                    mm = pe.matmul(ps[:, 6, 0:N], ones_r[:, :], edges[:, s, :], start=s == 0, stop=s == NT - 1)
                mm.then_inc(S["agg_ready"], 1)
                sum_edges(q, edges, 0)

            def sum_edges(q, edges, k):
                if k:
                    pe.wait_ge(S["agg_read"], q * (KT + 1) + k)
                i = 0
                for s in range(NT):
                    for a in range(2):
                        mm = pe.matmul(ps[:, 7 - k % 2, 0:N], h_row[a][:, s, P * k:P * k + P],
                                       edges[:, s, :], start=i == 0, stop=i == 2 * NT - 1)
                        i += 1
                mm.then_inc(S["agg_ready"], 1)

            def aggregated(q, k):
                pe.wait_ge(S["mean_hi"], q * KT + (k + 1))
                pe.wait_ge(S["mean_lo"], q * KT + (k + 2))

            def own_product(t0, y0, source, q, edges, first_free=None):
                for k in range(KT):
                    if k == KT - 1:
                        pe.wait_ge(S["row_lo"], (q - R + 1) * NT + NT if q >= R else NT)
                        if q == 0:
                            pe.wait_ge(S["rel_ready"], 1)
                        start_relation(q, edges, lambda: pe.wait_ge(S["turn_lo"], y0 + KT))
                    pe.wait_ge(S["turn_lo"], y0 + k + 1)
                    row_block(t0 + k, k % RING, h_t, k, first=k == 0,
                              bank_free=first_free if k == 0 else None)
                    if k + 2 < KT:
                        turn(y0 + k + 2, source, k + 2)

            def relation(q, t0, edges, last):
                for k in range(KT):
                    if k < KT - 1:
                        sum_edges(q, edges, k + 1)
                    elif not last:
                        pe.wait_ge(S["rel_ready"], q + 2)
                        start_relation(q + 1, edges, lambda: pe.wait_ge(S["agg_read"], (q + 1) * (KT + 1)))
                    aggregated(q, k)
                    row_block(t0 + k, k % RING, [m_pair(k, a) for a in range(2)], 0, last=last and k == KT - 1)

            def m_pair(k, a):
                return mean[a][:, k % 2:k % 2 + 1, :]

            def begin(q):
                y0 = (Y_H1, Y_H2, Y_MID)[q]
                pe.wait_ge(S["h_ready"], NT * (q + 2))
                if q == 0:
                    pe.wait_ge(S["y_added"], KT)
                else:
                    pe.wait_ge(S["agg_read"], (KT + 1) * (R + q - 1))
                turn(y0, h, 0)
                turn(y0 + 1, h, 1)
                return y0

            y0 = begin(0)
            own_product(T_ROOT, y0, h, 0, rel_r)
            with pe.Fori(0, R - 1) as r:
                relation(r, T_REL + r * KT, rel_r, False)
            relation(R - 1, T_REL + (R - 1) * KT, rel_r, True)

            pe.wait_ge(S["agg_read"], R * (KT + 1))
            for k in range(KT):
                row_block(T_GX + k, k % RING, h_t, k, first=k == 0,
                          bank_free=(lambda nt: pe.wait_ge(S["u_ready"], 2 * nt + 2)) if k == 0 else None)
                turn(Y_U + k, u, k)
            for k in range(KT):
                pe.wait_ge(S["turn_lo"], Y_U + k + 1)
                row_block(T_GU + k, k % RING, u_t, k, last=k == KT - 1)

            y0 = begin(1)
            own_product(T_S0, y0, h, R, total_r)
            relation(R, T_N0, total_r, True)
            y0 = begin(2)
            own_product(T_S1, y0, h, R + 1, total_r)
            relation(R + 1, T_N1, total_r, True)

            pe.wait_ge(S["h_ready"], NT * 5)
            pe.wait_ge(S["agg_read"], (KT + 1) * (R + 2))
            for f in range(NT):
                turn(Y_H3 + f, h, f)
            pe.wait_ge(S["turn_lo"], Y_H3 + NT)
            pe.wait_ge(S["w3_lo"], 1)
            for nt in range(NT):
                i = 0
                for k in range(NT):
                    for a, w in ((0, 0), (0, 1), (1, 0)):
                        mm = pe.matmul(ps[:, nt, 0:N], h_t[a][:, k, P * nt:P * nt + P], w3[w][:, k, :],
                                       start=i == 0, stop=i == 3 * NT - 1)
                        i += 1
                mm.then_inc(S["out_psum"], 1)

        @block.scalar
        def _(act):
            link = Chain(act, S["act_chain"])
            act.dma_start(etw_b[:, :], etw.partition_broadcast(P)).then_inc(S["etw_in"], 16)
            for g, b in enumerate((bq, bk, bv, biq, bik, biv, bo)):
                act.dma_start(b_in[KT * g:KT * g + KT, :], b.rearrange("(j p) -> j p", p=P)).then_inc(S["bcol_in"], 16)

            def key_rows(q):
                act.dma_start(key_i[:, 0, :], src[q * (E // 4):(q + 1) * (E // 4)].partition_broadcast(P))\
                   .then_inc(S["key_rows_in"], 16)
                act.dma_start(key_i[:, 1, :], dst[q * (E // 4):(q + 1) * (E // 4)].partition_broadcast(P))\
                   .then_inc(S["key_rows_in"], 16)

            key_rows(0)
            act.wait_ge(S["sp_max"], 1)
            act.activation(sp[:, 3, :], sp[:, 2, :], ACT.Exp, scale=-1.0).then_inc(S["sp_exp"], 1)
            act.wait_ge(S["sp_exp"], 1)
            act.activation(sp[:, 4, :], sp[:, 3, :], ACT.Ln, bias=1.0).then_inc(S["sp_ln"], 1)

            def layer_norm(n, target):
                for nt in range(NT):
                    act.wait_ge(S["var_ready"], NT * n + nt + 1)
                    act.activation(std[:, nt, :], mv[:, nt, 1:2], ACT.Sqrt, bias=epsc[:, 0:1]).then_inc(S["std_ready"], 1)
                for nt in range(NT):
                    act.wait_ge(S["shift_ready"], NT * n + nt + 1)
                    act.activation(target[:, nt, :], xres[:, nt, :], ACT.Relu, bias=shift[:, nt, :],
                                   scale=rstd[:, nt, :]).then_inc(S["h_ready"], 1)

            layer_norm(0, h0)
            for q in range(1, 4):
                act.wait_ge(S["keys_read"], q)
                key_rows(q)
            with act.Fori(0, NPASS) as p:
                act.wait_ge(S["hot_rs_used"], p * EC + (EC + RING))
                for b in range(PASS // 2, PASS):
                    act.activation(counts16[:, p * PASS + b, :], ps[:, b, 0:N], ACT.Copy)\
                       .then_inc(S["counts_by_act"], 1)
            act.wait_ge(S["hot_m_used"], EC + M_CREDIT)
            act.activation(sparse_w[:, :, :], ps[:, NT:2 * NT, 0:N], ACT.Copy).then_inc(S["sparse_kept"], 1)

            def turned_high(y, target):
                act.wait_ge(S["turned"], y + 1)
                act.activation(target, ps[:, 6 + y % 2, 0:N], ACT.Copy).then_inc(S["turn_hi"], 1)

            def column_high(g, j):
                act.wait_ge(S["weight_turned"], g * KT + (j + 1))
                act.wait_ge(S["w_used"], g * KT + (j + 1))
                b = 2 + 2 * (j % 2)
                act.activation(whi[j % RING][:, :, :],
                               ps[:, b:b + 2, :].rearrange("p b (k n) -> p (b k) n", n=P), ACT.Copy)\
                   .then_inc(S["w_hi"], 1)

            def row_high(t, slot, use):
                act.wait_ge(raw_in[slot], use)
                act.wait_ge(S["w_used"], t + 1)
                act.activation(whi_row[slot], raw[slot][:, :], ACT.Copy).then_inc(S["w_hi"], 1)

            def row_high_at(t):
                row_high(t, t % RING, 16 * (t // RING + 1))

            for f in range(KT):
                turned_high(Y_H0 + f, acts[:, 0, 0, f, :])
            column_high(0, 0)
            column_high(0, 1)

            def eight_tiles(g, a):
                for j in range(KT):
                    column_high(g, j + 2)
                    act.wait_ge(S["w_used"], g * KT + (j + 1 + W_CREDIT))
                    act.activation(acts[:, a, 0, j, :], ps[:, j % 2, 0:N], ACT.Identity,
                                   bias=bcol[:, bass.ds(g * KT + j, 1)]).then_inc(S["out_hi"], 1)

            with act.Fori(0, 3) as g:
                act.wait_ge(S["mask_made"], g // 2 + 1)
                eight_tiles(g, g + 1)
            with act.Fori(3, 6) as g:
                eight_tiles(g, g - 3)
            for m in range(NT):
                act.wait_ge(S["v_turned"], 2 * m + 1)
                act.activation(v_rows[:, 0, m, :], ps[:, 2:4, :].rearrange("p b n -> p (b n)"), ACT.Copy)\
                   .then_inc(S["v_hi"], 1)

            def exps(i, o):
                act.wait_ge(S["max_ready"], i * 4 + (o + 1))
                for nt in range(NT):
                    act.activation(sc[:, o % 2, nt, :], sc[:, o % 2, nt, :], ACT.Exp, bias=nmax[:, o % 2, nt:nt + 1],
                                   accum_out=rsum[:, o % 2, nt:nt + 1]).then_inc(S["exp_ready"], 1)

            def head(i, o):
                if not is_head(i, o, H - 1):
                    exps(i, o + 1)
                for m in range(NT):
                    act.wait_ge(S["probs_turned"], (i * 4 + o) * NT + (m + 1))
                    act.wait_ge(S["pv_done"], i * 4 + (o - 1 + O_CREDIT))
                    act.activation(pt[0][:, o % 2, m, :], ps[:, NT + m, 0:N], ACT.Copy).then_inc(S["pt_hi"], 1)
                if not is_head(i, o, 0):
                    head_out(i, o - 1)

            def head_out(i, o):
                r = DH * (o % 2)
                act.wait_ge(S["pv_done"], i * 4 + (o + 1 + O_CREDIT))
                act.activation(acts[r:r + DH, 0, 0, i * 2 + o // 2, :], ps[r:r + DH, 6 + o % 2, 0:N], ACT.Copy)\
                   .then_inc(S["head_hi"], 1)

            exps(0, 0)
            head(0, 0)
            with act.Fori(0, 3) as i:
                for o in range(1, 5):
                    head(i, o)
            for o in range(1, 4):
                head(3, o)
            act.wait_ge(S["probs_turned"], H * NT)
            act.dma_start(xres[:, :, :], x.rearrange("(t p) d -> p t d", p=P)).then_inc(S["x_in"], 16)
            head_out(3, 3)

            for j in range(KT):
                if j + 2 < KT:
                    column_high(6, j + 2)
                else:
                    row_high_at(T_WO + j + 2)
                act.wait_ge(S["w_used"], T_WO + j + 1 + W_CREDIT)
                need(act, S["y_turned"], j - 1)
                act.activation(y_t[:, j % 2, :], ps[:, j % 2, 0:N], ACT.Identity,
                               bias=bcol[:, T_WO + j:T_WO + j + 1]).then_inc(S["y_evacuated"], 1)

            def bias_row(b, last_use, count):
                act.wait_ge(S[last_use], count)
                act.dma_start(brow[:, :], b.partition_broadcast(P)).then_inc(S["brow_in"], 16)

            def row_parts(n):
                for nt in range(NT):
                    act.wait_ge(S["h_ready"], NT * (n + 2))
                    if n == 1:
                        act.wait_ge(S["w_used"], T_S0 + W_CREDIT)
                    if n == 2:
                        act.wait_ge(S["agg_ready"], (KT + 1) * (R + 1))
                    act.activation(h_row[0][:, nt, :], h[:, nt, :], ACT.Copy).then_inc(S["row_hi"], 1)

            def mean_high(q, k):
                act.wait_ge(S["agg_read"], q * (KT + 1) + (k + 2))
                act.activation(mean[0][:, k % 2, :], mean_f[:, k % 2, :], ACT.Copy).then_inc(S["mean_hi"], 1)

            def relation_edges(r):
                need(act, S["agg_ready"], r * (KT + 1))
                act.activation(rel_r[:, :, :], counts16[:, bass.ds(r * NT, NT), :], ACT.Copy)\
                   .then_inc(S["rel_ready"], 1)

            def own_product(n, t0, q):
                for k in range(KT):
                    row_high_at(t0 + k + 2)
                    if k + 2 < KT:
                        turned_high((Y_H1, Y_H2, Y_MID)[n] + k + 2, h_t[0][:, k + 2, :])
                    if k == 1:
                        row_parts(n)
                    if k == 3 and n == 0:
                        relation_edges(0)
                mean_high(q, 0)

            def relation(q, t0, last, more=True):
                for k in range(KT):
                    if isinstance(t0, int):
                        if t0 + k + 2 < T_END:
                            row_high_at(t0 + k + 2)
                    else:
                        row_high(t0 + (k + 2), (k + 2) % RING, use_of_slot(q + T_REL // KT, k + 2))
                    if k < KT - 1:
                        act.wait_ge(S["w_used"], t0 + (k + W_CREDIT))
                        mean_high(q, k + 1)
                    if k == KT - 2 and not last:
                        act.wait_ge(S["agg_ready"], q * (KT + 1) + (KT + 1))
                        act.activation(rel_r[:, :, :], counts16[:, bass.ds(q * NT + NT, NT), :], ACT.Copy)\
                           .then_inc(S["rel_ready"], 1)
                if not last:
                    act.wait_ge(S["w_used"], t0 + (KT - 1 + W_CREDIT))
                    mean_high(q + 1, 0)

            bias_row(bias1, "y_turned", KT)
            layer_norm(1, h)
            turned_high(Y_H1, h_t[0][:, 0, :])
            turned_high(Y_H1 + 1, h_t[0][:, 1, :])
            own_product(0, T_ROOT, 0)
            with act.Fori(0, R - 1) as r:
                relation(r, T_REL + r * KT, False)
            relation(R - 1, T_REL + (R - 1) * KT, True)
            for k in range(KT):
                row_high_at(T_GX + k + 2)
                turned_high(Y_U + k, u_t[0][:, k, :])
                if k == 1:
                    bias_row(b_gate, "u_ready", 2 * NT)
            for k in range(KT):
                row_high_at(T_GU + k + 2)
                if k < NT:
                    act.wait_ge(S["turned"], Y_U + KT)
                    act.activation(u[:, k, :], u[:, k, :], ACT.Tanh).then_inc(S["u_tanh"], 1)
            bias_row(b0, "gate_sum", NT)
            layer_norm(2, h)
            turned_high(Y_H2, h_t[0][:, 0, :])
            turned_high(Y_H2 + 1, h_t[0][:, 1, :])
            own_product(1, T_S0, R)
            relation(R, T_N0, True)
            for nt in range(NT):
                act.wait_ge(S["mid_ready"], 2 * nt + 2)
                act.activation(h[:, nt, :], h[:, nt, :], ACT.Relu).then_inc(S["h_ready"], 1)
            bias_row(b1, "mid_ready", 2 * NT)
            turned_high(Y_MID, h_t[0][:, 0, :])
            turned_high(Y_MID + 1, h_t[0][:, 1, :])
            own_product(2, T_S1, R + 1)
            act.activation(w3[0][:, :, :], sparse_w[:, :, :], ACT.Copy).then_inc(S["w3_hi"], 1)
            relation(R + 1, T_N1, True)
            bias_row(bias3, "x_based", NT)
            layer_norm(3, h)
            for f in range(NT):
                turned_high(Y_H3 + f, h_t[0][:, f, :])

        @block.vector
        def _(dve):
            link = Chain(dve, S["vec_chain"])
            dve.sem_inc(S["w_used"], W_CREDIT)
            dve.sem_inc(S["out_lo"], O_CREDIT)
            dve.sem_inc(S["head_lo"], O_CREDIT)
            dve.sem_inc(S["pv_done"], O_CREDIT)
            for name in ("counts_by_vec", "counts_by_act", "mask_made", "mean_lo"):
                dve.sem_inc(S[name], 1)
            dve.sem_inc(S["hot_rs_used"], RING)
            dve.sem_inc(S["dup_found"], 4)
            dve.sem_inc(S["hot_m_used"], M_CREDIT)
            dve.memset(epsc[:, :], EPS).then_inc(S["ones_made"], 1)
            dve.memset(same[:, 0, :], 1.0).then_inc(S["ones_made"], 1)
            dve.wait_ge(S["ones_made"], 2)
            dve.tensor_copy(ones_r[:, :], same[:, 0, :]).then_inc(S["ones_made"], 1)

            dve.wait_ge(S["edges_in"], 16 * 5)
            dve.tensor_copy(e_row[:, SRC, :], e_in[:, 0, :])
            dve.tensor_copy(e_row[:, DST, :], e_in[:, 1, :])
            dve.tensor_copy(e_row[:, TYPE, :], e_in[:, 2, :])
            dve.tensor_copy(e_row[:, WEIGHT, :], e_w[:, :])
            dve.scalar_tensor_tensor(e_row[:, KEY, :], e_in[:, 0, :], float(N), e_in[:, 1, :], ALU.mult, ALU.add)
            dve.scalar_tensor_tensor(e_row[:, KEY2, :], e_in[:, 3, :], float(N), e_in[:, 0, :], ALU.mult, ALU.add)\
               .then_inc(S["edge_rows"], 1)
            dve.wait_ge(S["etw_in"], 16)
            link(dve.tensor_scalar(sp[:, 0, :], etw_b[:, :], 0.0, None, ALU.max))
            link(dve.tensor_scalar(sp[:, 1, :], etw_b[:, :], -1.0, None, ALU.mult))
            dve.tensor_tensor(sp[:, 2, :], etw_b[:, :], sp[:, 1, :], ALU.max).then_inc(S["sp_max"], 1)

            def norm_stats(nt):
                for f in range(2):
                    ins = dve.bn_stats(stats[:, nt, f, :], xres[:, nt, HALF * f:HALF * f + HALF])
                    link(ins)
                dve.bn_aggr(mv[:, nt, :], stats[:, nt, :, :].rearrange("p a b -> p (a b)")).then_inc(S["var_ready"], 1)

            def norm_shift(n, nt):
                dve.wait_ge(S["std_ready"], NT * n + nt + 1)
                link(dve.reciprocal(rstd[:, nt, :], std[:, nt, :]))
                dve.scalar_tensor_tensor(shift[:, nt, :], mv[:, nt, 0:1], -1.0, rstd[:, nt, :], ALU.mult, ALU.mult)\
                   .then_inc(S["shift_ready"], 1)

            dve.wait_ge(S["x_in"], 16)
            for nt in range(NT):
                norm_stats(nt)
            dve.wait_ge(S["edges_turned"], 2)
            dve.tensor_copy(e_col[:, :, :], ps[:, 0, 0:6 * EC].rearrange("p (f c) -> p f c", f=6))\
               .then_inc(S["edge_cols"], 1)
            dve.tensor_copy(bcol[:, :], ps[:, 1, 0:7 * KT]).then_inc(S["edge_cols"], 1)
            dve.wait_ge(S["edge_cols"], 2)
            dve.wait_ge(S["iota_made"], 1)
            with dve.Fori(0, EC // 4) as c4:
                for j in range(4):
                    dve.tensor_scalar(hot_dst[:, c4 * 4 + j, :], iota[:, 0:N], e_col[:, DST, bass.ds(c4 * 4 + j, 1)],
                                      None, ALU.is_equal).then_inc(S["hot_dst_made"], 1)
            for nt in range(NT):
                norm_shift(0, nt)

            dve.wait_ge(S["later_made"], 2)
            with dve.Fori(0, 4) as q:
                dve.wait_ge(S["key_rows_in"], q * 32 + 32)
                dve.scalar_tensor_tensor(key_row[:, :], key_i[:, 0, :], float(N), key_i[:, 1, :], ALU.mult, ALU.add)\
                   .then_inc(S["keys_read"], 1)
                dve.wait_ge(S["keys_read"], q + 1)
                hold(dve)
                with dve.Fori(0, QUARTER // 4) as c4:
                    for j in range(4):
                        dve.wait_ge(S["dup_found"], q * QUARTER + (c4 * 4 + (j + 1)))
                        dve.scalar_tensor_tensor(same[:, j, :], key_row[:, bass.ds((c4 * 4 + j) * P, P)],
                                                 e_col[:, KEY, bass.ds(q * QUARTER + (c4 * 4 + j), 1)],
                                                 later[:, :], ALU.is_equal, ALU.mult,
                                                 accum_out=dup[:, bass.ds(q * QUARTER + (c4 * 4 + j), 1)])\
                           .then_inc(S["dup_found"], 1)
                dve.wait_ge(S["dup_found"], q * QUARTER + (QUARTER + 4))
            dve.wait_ge(S["exp_made"], 1)
            dve.wait_ge(S["dup_found"], EC + 4)
            link(dve.tensor_scalar(live[:, :], dup[:, :], 0.0, None, ALU.is_equal))
            link(dve.tensor_scalar(chunk_val[:, :], chunk_exp[:, :], 23, None, ALU.logical_shift_left))
            link(dve.tensor_scalar(edge_val[:, :], e_col[:, TYPE, :], 0.125, 1.0, ALU.mult, ALU.add))
            link(dve.tensor_tensor(edge_val[:, :], edge_val[:, :], live[:, :], ALU.mult))
            link(dve.tensor_tensor(edge_val[:, :], edge_val[:, :], chunk_val[:, :].bitcast(F32), ALU.mult))
            left = e_col[:, WEIGHT, :]
            for w in range(3):
                link(dve.tensor_copy(w_bf[:, w, :], left))
                link(dve.tensor_copy(w_part[:, w, :], w_bf[:, w, :]))
                if w < 2:
                    link(dve.tensor_tensor(w_rest[:, w, :], left, w_part[:, w, :], ALU.subtract))
                    left = w_rest[:, w, :]

            with dve.Fori(0, NPASS) as p:
                with dve.Fori(0, EC // 4) as c4:
                    for j in range(4):
                        dve.wait_ge(S["hot_rs_used"], p * EC + (c4 * 4 + (j + 1)))
                        dve.tensor_scalar(hot_rs[:, j, :], iota[:, bass.ds(p * (PASS * P), PASS * P)],
                                          e_col[:, KEY2, bass.ds(c4 * 4 + j, 1)], None, ALU.is_equal)\
                           .then_inc(S["hot_rs_made"], 1)
                dve.wait_ge(S["hot_rs_used"], p * EC + (EC + RING))
                for b in range(PASS // 2):
                    dve.tensor_copy(counts16[:, p * PASS + b, :], ps[:, b, 0:N]).then_inc(S["counts_by_vec"], 1)
            with dve.Fori(0, EC // 2) as c2:
                for j in range(2):
                    dve.wait_ge(S["hot_m_used"], c2 * 2 + (j + 1))
                    col = bass.ds(c2 * 2 + j, 1)
                    for w in range(3):
                        dve.tensor_scalar(hot_w[:, j, w, :], iota[:, 0:N], e_col[:, SRC, col],
                                          w_part[:, w, col], ALU.is_equal, ALU.mult)
                    dve.tensor_scalar(hot_val[:, j, :], iota[:, 0:N], e_col[:, SRC, col], edge_val[:, col],
                                      ALU.is_equal, ALU.mult).then_inc(S["hot_m_made"], 1)
            dve.wait_ge(S["hot_m_used"], EC + M_CREDIT)
            packed = key_i[:, 1, 0:NT * N]
            types = key_i[:, 0, 0:NT * N]
            dve.tensor_copy(packed.bitcast(F32).rearrange("p (t n) -> p t n", t=NT), ps[:, 0:NT, 0:N])\
               .then_inc(S["mask_decoded"], 1)
            dve.wait_ge(S["mask_decoded"], 1)
            link(dve.tensor_scalar(types, packed, 20, 7, ALU.logical_shift_right, ALU.bitwise_and))
            dve.tensor_copy(key_row[:, 0:NT * N], types).then_inc(S["mask_decoded"], 1)
            dve.wait_ge(S["sp_ln"], 1)
            dve.tensor_tensor(sp[:, 5, :], sp[:, 0, :], sp[:, 4, :], ALU.add).then_inc(S["sp_made"], 1)

            def turned_low(y, target, hi):
                dve.wait_ge(S["turn_hi"], y + 1)
                dve.tensor_tensor(target, ps[:, 6 + y % 2, 0:N], hi.bitcast(F32), ALU.subtract).then_inc(S["turn_lo"], 1)

            def column_low(g, j):
                dve.wait_ge(S["w_hi"], g * KT + (j + 1))
                b = 2 + 2 * (j % 2)
                dve.tensor_tensor(wlo[j % RING][:, :, :],
                                  ps[:, b:b + 2, :].rearrange("p b (k n) -> p (b k) n", n=P),
                                  whi[j % RING][:, :, :].bitcast(F32), ALU.subtract).then_inc(S["w_lo"], 1)

            def row_low(t, slot):
                dve.wait_ge(S["w_hi"], t + 1)
                dve.tensor_tensor(wlo_row[slot], raw[slot][:, :], whi_row[slot].bitcast(F32), ALU.subtract)\
                   .then_inc(S["w_lo"], 1)

            for f in range(KT):
                turned_low(Y_H0 + f, acts[:, 0, 1, f, :], acts[:, 0, 0, f, :])
            column_low(0, 0)
            column_low(0, 1)

            def eight_tiles(g, a):
                for j in range(KT):
                    column_low(g, j + 2)
                    dve.wait_ge(S["out_hi"], g * KT + (j + 1))
                    dve.scalar_tensor_tensor(acts[:, a, 1, j, :], ps[:, j % 2, 0:N], bcol[:, bass.ds(g * KT + j, 1)],
                                             acts[:, a, 0, j, :].bitcast(F32), ALU.add, ALU.subtract)\
                       .then_inc(S["out_lo"], 1)

            with dve.Fori(0, 3) as g:
                eight_tiles(g, g + 1)
            with dve.Fori(3, 6) as g:
                eight_tiles(g, g - 3)
            for m in range(NT):
                dve.wait_ge(S["v_turned"], 2 * m + 2)
                dve.tensor_copy(v_rows[:, 1, m, :], ps[:, 4:6, :].rearrange("p b n -> p (b n)")).then_inc(S["v_lo"], 1)

            dve.wait_ge(S["mask_made"], 2)

            def score_max(i, o):
                for nt in range(NT):
                    dve.wait_ge(S["scores_ready"], (i * 4 + o) * NT + (nt + 1))
                    need(dve, S["probs_turned"], (i * 4 + (o - 1)) * NT)
                    hold(dve)
                    dve.tensor_tensor_reduce(sc[:, o % 2, nt, :], ps[:, nt, 0:N], mask[:, nt, :], SCALE, -3e38,
                                             ALU.add, ALU.max, rmax[:, o % 2, nt:nt + 1]).then_inc(S["scores_read"], 1)
                dve.wait_ge(S["scores_read"], (i * 4 + (o + 1)) * NT)
                dve.tensor_scalar(nmax[:, o % 2, :], rmax[:, o % 2, :], -1.0, None, ALU.mult).then_inc(S["max_ready"], 1)

            def head(i, o):
                if not is_head(i, o, H - 1):
                    score_max(i, o + 1)
                for m in range(NT):
                    dve.wait_ge(S["pt_hi"], (i * 4 + o) * NT + (m + 1))
                    dve.tensor_tensor(pt[1][:, o % 2, m, :], ps[:, NT + m, 0:N], pt[0][:, o % 2, m, :].bitcast(F32),
                                      ALU.subtract).then_inc(S["pt_lo"], 1)
                if not is_head(i, o, H - 1):
                    invert_sum(i, o + 1)
                if not is_head(i, o, 0):
                    head_out(i, o - 1)

            def invert_sum(i, o):
                dve.wait_ge(S["exp_ready"], (i * 4 + (o + 1)) * NT)
                dve.reciprocal(rinv[:, o % 2, :], rsum[:, o % 2, :]).then_inc(S["sum_inverted"], 1)

            def head_out(i, o):
                r = DH * (o % 2)
                dve.wait_ge(S["head_hi"], i * 4 + (o + 1))
                dve.tensor_tensor(acts[r:r + DH, 0, 1, i * 2 + o // 2, :], ps[r:r + DH, 6 + o % 2, 0:N],
                                  acts[r:r + DH, 0, 0, i * 2 + o // 2, :].bitcast(F32), ALU.subtract)\
                   .then_inc(S["head_lo"], 1)

            score_max(0, 0)
            invert_sum(0, 0)
            head(0, 0)
            with dve.Fori(0, 3) as i:
                for o in range(1, 5):
                    head(i, o)
            for o in range(1, 4):
                head(3, o)
            head_out(3, 3)

            def add_y(j):
                dve.wait_ge(S["y_turned"], j + 1)
                dve.tensor_tensor(xres[:, :, P * j:P * j + P], xres[:, :, P * j:P * j + P],
                                  ps[:, 6 + j % 2, 0:N].rearrange("p (t n) -> p t n", t=NT), ALU.add)\
                   .then_inc(S["y_added"], 1)

            dve.wait_ge(S["x_in"], 32)
            for j in range(KT):
                if j + 2 < KT:
                    column_low(6, j + 2)
                else:
                    row_low(T_WO + j + 2, (j + 2) % RING)
                if 1 <= j <= NT:
                    link(dve.tensor_reduce(mask[:, j - 1, :],
                                           counts16[:, :, :].rearrange("p (r t) n -> p t n r", t=NT)[:, j - 1],
                                           AX.X, ALU.add))
                    dve.tensor_copy(total_r[:, j - 1, :], mask[:, j - 1, :]).then_inc(S["total_made"], 1)
                if j:
                    add_y(j - 1)
            add_y(KT - 1)
            dve.wait_ge(S["y_added"], KT)

            def layer_norm(n):
                for nt in range(NT):
                    norm_stats(nt)
                for nt in range(NT):
                    norm_shift(n, nt)

            def read_sums(q, k):
                dve.wait_ge(S["agg_ready"], q * (KT + 1) + (k + 2))
                need(dve, S["mean_lo"], q * KT + k)
                dve.tensor_tensor(mean_f[:, k % 2, :], ps[:, 7 - k % 2, 0:N], inv[:, :], ALU.mult)\
                   .then_inc(S["agg_read"], 1)

            def read_counts(q, n):
                dve.wait_ge(S["agg_ready"], q * (KT + 1) + 1)
                dve.tensor_scalar(cnt[:, :], ps[:, 6, 0:N], 1.0, None, ALU.max).then_inc(S["agg_read"], 1)
                dve.wait_ge(S["agg_read"], q * (KT + 1) + 1)
                dve.reciprocal(inv[:, :], cnt[:, :]).then_inc(S["inv_made"], 1)
                dve.wait_ge(S["inv_made"], q + 1)

            def own_product(n, t0, q):
                for k in range(KT):
                    row_low(t0 + k + 2, (k + 2) % RING)
                    if k + 2 < KT:
                        turned_low((Y_H1, Y_H2, Y_MID)[n] + k + 2, h_t[1][:, k + 2, :], h_t[0][:, k + 2, :])
                read_counts(q, n)
                read_sums(q, 0)

            def relation(q, t0, last):
                for k in range(KT):
                    if not isinstance(t0, int) or t0 + k + 2 < T_END:
                        row_low(t0 + (k + 2), (k + 2) % RING)
                    if k < KT - 1:
                        read_sums(q, k + 1)
                if not last:
                    read_counts(q + 1, 0)
                    read_sums(q + 1, 0)

            def sum_of(n, t_last, nt):
                if nt < NT - 1:
                    dve.wait_ge(S["sum_ready"], (NT - 1) * n + nt + 1)
                else:
                    dve.wait_ge(S["w_used"], t_last + 1 + W_CREDIT)

            layer_norm(1)
            turned_low(Y_H1, h_t[1][:, 0, :], h_t[0][:, 0, :])
            turned_low(Y_H1 + 1, h_t[1][:, 1, :], h_t[0][:, 1, :])
            own_product(0, T_ROOT, 0)
            with dve.Fori(0, R - 1) as r:
                relation(r, T_REL + r * KT, False)
            relation(R - 1, T_REL + (R - 1) * KT, True)

            def add_bias(n, t_last, target, done):
                for nt in range(NT):
                    sum_of(n, t_last, nt)
                    for f in range(2):
                        half = slice(HALF * f, HALF * f + HALF)
                        ins = dve.tensor_tensor(target[:, nt, half], ps[:, 2 * nt + f, :], brow[:, half], ALU.add)
                        ins.then_inc(S[done], 1)

            dve.wait_ge(S["brow_in"], 16)
            add_bias(0, T_GX - 1, u, "u_ready")
            for k in range(KT):
                row_low(T_GX + k + 2, (k + 2) % RING)
                turned_low(Y_U + k, u_t[1][:, k, :], u_t[0][:, k, :])
            for k in range(KT):
                row_low(T_GU + k + 2, (k + 2) % RING)
            for nt in range(NT):
                sum_of(1, T_S0 - 1, nt)
                dve.wait_ge(S["gate_sum"], nt + 1)
                for f in range(2):
                    half = slice(HALF * f, HALF * f + HALF)
                    dve.tensor_tensor(h[:, nt, half], ps[:, 2 * nt + f, :], u[:, nt, half], ALU.mult)\
                       .then_inc(S["gate_product"], 1)
            for nt in range(NT):
                dve.wait_ge(S["x_gated"], nt + 1)
                norm_stats(nt)
            for nt in range(NT):
                norm_shift(2, nt)
            turned_low(Y_H2, h_t[1][:, 0, :], h_t[0][:, 0, :])
            turned_low(Y_H2 + 1, h_t[1][:, 1, :], h_t[0][:, 1, :])
            own_product(1, T_S0, R)
            relation(R, T_N0, True)
            dve.wait_ge(S["brow_in"], 16 * 3)
            add_bias(2, T_S1 - 1, h, "mid_ready")
            turned_low(Y_MID, h_t[1][:, 0, :], h_t[0][:, 0, :])
            turned_low(Y_MID + 1, h_t[1][:, 1, :], h_t[0][:, 1, :])
            own_product(2, T_S1, R + 1)
            dve.wait_ge(S["w3_hi"], 1)
            dve.tensor_tensor(w3[1][:, :, :], sparse_w[:, :, :], w3[0][:, :, :].bitcast(F32), ALU.subtract)\
               .then_inc(S["w3_lo"], 1)
            relation(R + 1, T_N1, True)
            dve.wait_ge(S["x_based"], NT)
            for nt in range(NT):
                sum_of(3, T_END - 1, nt)
                for f in range(2):
                    half = slice(HALF * f, HALF * f + HALF)
                    dve.tensor_tensor(xres[:, nt, half], xres[:, nt, half], ps[:, 2 * nt + f, :], ALU.add)\
                       .then_inc(S["x_done"], 1)
                dve.wait_ge(S["x_done"], 2 * nt + 2)
                norm_stats(nt)
            for nt in range(NT):
                norm_shift(3, nt)
            for f in range(NT):
                turned_low(Y_H3 + f, h_t[1][:, f, :], h_t[0][:, f, :])
            for nt in range(NT):
                dve.wait_ge(S["out_psum"], nt + 1)
                dve.wait_ge(S["out_based"], nt + 1)
                dve.tensor_tensor(u[:, nt, 0:N], u[:, nt, 0:N], ps[:, nt, 0:N], ALU.add).then_inc(S["out_done"], 1)

        @block.gpsimd
        def _(pool):
            link = Chain(pool, S["pool_chain"])
            pool.memset(ident[:, :], 0.0).then_inc(S["ident_made"], 1)
            pool.wait_ge(S["ident_made"], 1)
            pool.affine_select(out=ident[:, :], in_=ident[:, :], compare_op=ALU.not_equal, fill=1.0, base=0,
                               pattern=[[-1, P]], channel_multiplier=1).then_inc(S["ident_made"], 1)
            pool.iota(iota[:, :], pattern=[[1, R * N]], base=0, channel_multiplier=0).then_inc(S["iota_made"], 1)
            pool.memset(later[:, :], 1.0).then_inc(S["later_made"], 1)
            pool.wait_ge(S["later_made"], 1)
            pool.affine_select(out=later[:, :], in_=later[:, :], compare_op=ALU.is_gt, fill=0.0, base=0,
                               pattern=[[1, P]], channel_multiplier=-1).then_inc(S["later_made"], 1)
            pool.iota(chunk_exp[:, :], pattern=[[EXP_STEP, EC]], base=EXP_BASE + 127, channel_multiplier=0)\
                .then_inc(S["exp_made"], 1)

            pool.wait_ge(S["mask_decoded"], 2)
            types = key_row[:, 0:NT * N]
            empty = key_i[:, 1, 0:NT * N].bitcast(F32)
            flat = mask[:, :, :].rearrange("p t n -> p (t n)")
            pool.wait_ge(S["sp_made"], 1)
            term = iota[:, 0:2 * NT * N].bitcast(F32)
            link(pool.tensor_scalar(flat, types, 0.0, sp[:, 5, 3:4], ALU.is_equal, ALU.mult))
            for t in range(1, 5):
                link(pool.tensor_scalar(term, types, float(t), sp[:, 5, t - 1:t], ALU.is_equal, ALU.mult))
                link(pool.tensor_tensor(flat, flat, term, ALU.add))
            link(pool.tensor_scalar(empty, empty, 0.0, MASKED, ALU.is_equal, ALU.mult))
            link(pool.affine_select(out=empty.rearrange("p (t n) -> p t n", t=NT),
                                    in_=empty.rearrange("p (t n) -> p t n", t=NT),
                                    compare_op=ALU.not_equal, fill=0.0, base=0,
                                    pattern=[[-P, NT], [1, N]], channel_multiplier=-1))
            link(pool.tensor_tensor(flat, flat, empty, ALU.add))
            pool.tensor_scalar(flat, flat, 1.0 / SCALE, None, ALU.mult).then_inc(S["mask_made"], 1)

            def stage_q(i, o):
                r0 = DH * (o % 2)
                need(pool, S["scores_ready"], (i * 4 + (o - 1)) * NT)
                for a in range(2):
                    pool.tensor_copy(q_st[a][r0:r0 + DH, o % 2, :], acts[r0:r0 + DH, 0, a, i * 2 + o // 2, :])\
                        .then_inc(S["q_staged"], 1)
                    pool.wait_ge(S["q_staged"], i * 8 + (2 * o + a + 1))

            def stage_v(i, o):
                pool.wait_ge(S["pv_done"], i * 4 + (2 * o - 2 + O_CREDIT))
                for a in range(2):
                    pool.tensor_copy(v_st[a][:, o % 2, :, :], v_rows[:, a, :, bass.ds((i * 2 + o) * P, P)])\
                        .then_inc(S["v_staged"], 1)
                pool.wait_ge(S["v_staged"], i * 4 + (2 * o + 2))

            def normalise(i, o):
                pool.wait_ge(S["sum_inverted"], i * 4 + (o + 1))
                hold(pool)
                for nt in range(NT):
                    ins = pool.tensor_scalar(sc[:, o % 2, nt, :], sc[:, o % 2, nt, :], rinv[:, o % 2, nt:nt + 1],
                                             None, ALU.mult)
                ins.then_inc(S["probs_ready"], 1)
                pool.wait_ge(S["probs_ready"], i * 4 + (o + 1))

            pool.wait_ge(S["v_lo"], NT)
            pool.wait_ge(S["v_hi"], NT)
            for a in range(2):
                for o in range(2):
                    r0 = DH * (1 - o)
                    link(pool.memset(q_st[a][r0:r0 + DH, o, :].bitcast(F32), 0.0))
            stage_q(0, 0)
            stage_q(0, 1)
            stage_v(0, 0)
            normalise(0, 0)
            stage_q(0, 2)
            normalise(0, 1)
            with pool.Fori(0, 3) as i:
                for o in range(1, 5):
                    stage_q(i, o + 2)
                    if o % 2:
                        stage_v(i, (o + 1) // 2)
                    normalise(i, o + 1)
            stage_q(3, 3)
            stage_v(3, 1)
            normalise(3, 2)
            normalise(3, 3)

            def row_parts(n):
                for nt in range(NT):
                    pool.wait_ge(S["row_hi"], NT * n + nt + 1)
                    pool.tensor_tensor(h_row[1][:, nt, :], h[:, nt, :], h_row[0][:, nt, :].bitcast(F32), ALU.subtract)\
                        .then_inc(S["row_lo"], 1)

            def mean_low(q, k):
                pool.wait_ge(S["mean_hi"], q * KT + (k + 1))
                pool.tensor_tensor(mean[1][:, k % 2, :], mean_f[:, k % 2, :], mean[0][:, k % 2, :].bitcast(F32),
                                   ALU.subtract).then_inc(S["mean_lo"], 1)

            row_parts(0)
            mean_low(0, 0)
            with pool.Fori(0, R - 1) as r:
                for k in range(KT):
                    mean_low(r, k + 1)
            for k in range(1, KT):
                mean_low(R - 1, k)
            pool.wait_ge(S["brow_in"], 16 * 2)
            for nt in range(NT):
                pool.wait_ge(S["u_tanh"], nt + 1)
                link(pool.tensor_tensor(u[:, nt, :], u[:, nt, :], h[:, nt, :], ALU.subtract))
                link(pool.tensor_tensor(xres[:, nt, :], xres[:, nt, :], h[:, nt, :], ALU.add))
                link(pool.tensor_tensor(h[:, nt, :], u[:, nt, :], brow[:, :], ALU.mult))
                pool.tensor_tensor(xres[:, nt, :], xres[:, nt, :], h[:, nt, :], ALU.add).then_inc(S["gate_sum"], 1)
            pool.wait_ge(S["gate_sum"], NT)
            for nt in range(NT):
                pool.wait_ge(S["gate_product"], 2 * nt + 2)
                pool.tensor_tensor(xres[:, nt, :], xres[:, nt, :], h[:, nt, :], ALU.add).then_inc(S["x_gated"], 1)
            row_parts(1)
            for k in range(KT):
                mean_low(R, k)
            row_parts(2)
            pool.wait_ge(S["brow_in"], 16 * 4)
            for nt in range(NT):
                pool.tensor_tensor(xres[:, nt, :], xres[:, nt, :], brow[:, :], ALU.add).then_inc(S["x_based"], 1)
            for k in range(KT):
                mean_low(R + 1, k)
            pool.wait_ge(S["brow_in"], 16 * 5)
            for nt in range(NT):
                pool.wait_ge(S["x_done"], 2 * nt + 2)
                pool.tensor_tensor(u[:, nt, :], xres[:, nt, :], brow[:, :], ALU.add).then_inc(S["out_based"], 1)


_INS = ["x", "src", "dst", "edge_type_5", "edge_type_8", "edge_weight", "L0_gnn_edge_type_weights",
        "L0_gnn_wq", "L0_gnn_bq", "L0_gnn_wk", "L0_gnn_bk", "L0_gnn_wv", "L0_gnn_bv", "L0_gnn_wiq",
        "L0_gnn_biq", "L0_gnn_wik", "L0_gnn_bik", "L0_gnn_wiv", "L0_gnn_biv", "L0_gnn_wo", "L0_gnn_bo",
        "L1_gnn_weight", "L1_gnn_root", "L1_gnn_bias", "L1_gnn_w_gate", "L1_gnn_b_gate",
        "L2_gnn_W_self0", "L2_gnn_W_neigh0", "L2_gnn_b0", "L2_gnn_W_self1", "L2_gnn_W_neigh1",
        "L2_gnn_b1", "L3_gnn_bias"]


def kernel(**inputs):
    import numpy as _np
    import concourse.bacc as _bacc
    from concourse import mybir as _mybir
    from concourse.bass_utils import run_bass_kernel_spmd as _run

    nc = _bacc.Bacc("TRN2", target_bir_lowering=False, num_devices=1)
    arrays, args = {}, []
    for name in _INS:
        a = _np.ascontiguousarray(inputs[name])
        arrays[f"in_{name}"] = a
        args.append(nc.dram_tensor(f"in_{name}", a.shape, _mybir.dt.from_np(a.dtype), kind="ExternalInput").ap())
    a = inputs["x"]
    args.append(nc.dram_tensor("out_0", a.shape, _mybir.dt.float32, kind="ExternalOutput").ap())
    build(nc, *args)
    r = _run(nc, [arrays], core_ids=[0])
    return r.results[0]["out_0"]
```

```python
from contextlib import ExitStack

import concourse.bass as bass
from concourse import mybir

ALU = mybir.AluOpType
ACT = mybir.ActivationFunctionType
AX = mybir.AxisListType
F32 = mybir.dt.float32
F32R = mybir.dt.float32r
BF16 = mybir.dt.bfloat16
I32 = mybir.dt.int32
I16 = mybir.dt.int16
U16 = mybir.dt.uint16

P = 128
RING = 4
EPS = 1e-5
MASKED = -1e30


def need(eng, sem, value):
    if not (isinstance(value, int) and value <= 0):
        eng.wait_ge(sem, value)


class Chain:

    def __init__(self, eng, sem):
        self.eng, self.sem, self.n = eng, sem, 0

    def __call__(self, instruction):
        self.n = self.n + 1
        instruction.then_inc(self.sem, 1)
        self.eng.wait_ge(self.sem, self.n)


def build(nc, x, src, dst, et5, et8, ew, etw, wq, bq, wk, bk, wv, bv, wiq, biq, wik, bik, wiv, biv,
          wo, bo, rel_w, root, bias1, w_gate, b_gate, w_self0, w_neigh0, b0, w_self1, w_neigh1, b1,
          bias3, out):
    N, D = x.shape
    E = src.shape[0]
    R = rel_w.shape[0]
    H = 16
    DH = D // H
    NT = N // P
    KT = D // P
    EC = E // P
    HALF = D // 2
    SCALE = float(DH) ** -0.5
    CELLS = R * NT
    DIGIT = 3
    EXP_STEP, EXP_BASE = 5, -120
    assert N == NT * P and D == KT * P and E == EC * P and DH == 64 and DIGIT * R <= 24
    assert EXP_BASE + EXP_STEP * EC <= 127

    ctx = ExitStack()
    with ctx:
        def sb(name, shape, dt, scope=ctx):
            return scope.enter_context(nc.sbuf_tensor(name, shape, dt))

        def sem(name):
            return ctx.enter_context(nc.semaphore(name))

        xres = sb("xres", [P, NT, D], F32)
        ident = sb("ident", [P, P], F32)
        ones_r = sb("ones_r", [P, P], F32R)
        counts16 = sb("counts16", [P, CELLS, N], U16)
        total_r = sb("total_r", [P, NT, N], F32R)
        sparse_w = sb("sparse_w", [P, NT, N], F32)
        mask = sb("mask", [P, NT, N], F32)
        iota = sb("iota", [P, N], I16)
        e_col = sb("e_col", [P, 7, EC], F32)
        digit_sum = sb("digit_sum", [P, R + 3], F32)
        no_digits = sb("no_digits", [P, 1], I32)
        brow = sb("brow", [P, D], F32)
        bcol = sb("bcol", [P, 7 * KT], F32)
        b_in = sb("b_in", [7 * KT, P], F32)
        stats = sb("stats", [P, NT, 2, 6], F32)
        mv = sb("mv", [P, NT, 2], F32)
        std = sb("std", [P, NT, 1], F32)
        rstd = sb("rstd", [P, NT, 1], F32)
        shift = sb("shift", [P, NT, 1], F32)
        epsc = sb("epsc", [P, 1], F32)
        raw = [sb(f"raw{i}", [P, D], F32) for i in range(RING)]
        whi = [sb(f"whi{i}", [P, KT, P], F32R) for i in range(RING)]
        wlo = [sb(f"wlo{i}", [P, KT, P], F32R) for i in range(RING)]
        whi_row = [w[:, :, :].rearrange("p k n -> p (k n)") for w in whi]
        wlo_row = [w[:, :, :].rearrange("p k n -> p (k n)") for w in wlo]

        graph_base = nc.sbuf_base
        with ExitStack() as scope:
            hot_src = sb("hot_src", [P, 2, N], BF16, scope)
            hot_rel = sb("hot_rel", [P, 2, N], BF16, scope)
            hot_w = sb("hot_w", [P, 2, 3, N], BF16, scope)
            e_in = sb("e_in", [EC, 4, P], I32, scope)
            e_w = sb("e_w", [EC, P], F32, scope)
            e_row = sb("e_row", [EC, 7, P], F32, scope)
            later = sb("later", [P, P], F32, scope)
            same = sb("same", [P, 2, P], F32, scope)
            rel_exp = sb("rel_exp", [P, 2, EC], I32, scope)
            w_bf = sb("w_bf", [P, 3, EC], BF16, scope)
            w_part = sb("w_part", [P, 3, EC], F32, scope)
            w_rest = sb("w_rest", [P, 2, EC], F32, scope)
            left_over = 2 * KT * N * 4 - (nc.sbuf_base - graph_base)
            assert left_over > 0
            sb("left_over", [P, left_over // 4], F32, scope)
            hot_dst = sb("hot_dst", [P, EC, N], BF16, scope)
            h0 = sb("h0", [P, NT, D], F32, scope)
            hot_val = sb("hot_val", [P, 2, N], BF16, scope)
            dup = sb("dup", [P, EC], F32, scope)
            live = sb("live", [P, EC], F32, scope)
            chunk_exp = sb("chunk_exp", [P, EC], I32, scope)
            chunk_val = sb("chunk_val", [P, EC], I32, scope)
            edge_val = sb("edge_val", [P, EC], F32, scope)
            etw_b = sb("etw_b", [P, 4], F32, scope)
            key_i = sb("key_i", [P, 2, E // 4], I32, scope)
            key_row = sb("key_row", [P, 2, E // 4], F32, scope)
            sp = sb("sp", [P, 6, 4], F32, scope)
            packed, codes = [key_i[:, i, 0:NT * N] for i in range(2)]
            digits = [key_row[:, i, 0:NT * N].bitcast(I32) for i in range(2)]

        with ExitStack() as scope:
            acts = sb("acts", [P, 4, 2, KT, N], F32R, scope)
        with ExitStack() as scope:
            sb("places_0_1", [P, 2, 2, KT, N], F32R, scope)
            pt = [sb(f"pt_{s}", [P, 2, NT, N], F32R, scope) for s in ("hi", "lo")]
            q_st = sb("q_st", [P, 2, 2, N], F32R, scope)
            sb("place_3", [P, 2, KT, N], F32R, scope)
            v_st = sb("v_st", [P, 2, 2, NT, P], F32R, scope)
            nmax = sb("nmax", [P, 2, NT], F32, scope)
            rsum = sb("rsum", [P, 2, NT], F32, scope)
            rinv = sb("rinv", [P, 2, NT], F32, scope)
        v_rows = acts[:, 3, :, :, :].rearrange("p s k n -> p s (k n)").rearrange(
            "p s (t d) -> p s t d", t=NT)
        sc = xres[:, :, :].rearrange("p t d -> p (t d)")[:, 0:2 * NT * N].rearrange(
            "p (b t n) -> p b t n", b=2, t=NT)
        y_t = brow[:, 0:2 * N].rearrange("p (b n) -> p b n", b=2)

        with ExitStack() as scope:
            h = sb("h", [P, NT, D], F32, scope)
            h_row = [sb(f"h_row_{s}", [P, NT, D], F32R, scope) for s in ("hi", "lo")]
            h_t = [sb(f"h_t_{s}", [P, KT, N], F32R, scope) for s in ("hi", "lo")]
            mean_f = sb("mean_f", [P, 2, N], F32, scope)
            mean = [sb(f"mean_{s}", [P, 2, N], F32R, scope) for s in ("hi", "lo")]
            rel_r = sb("rel_r", [P, NT, N], F32R, scope)
            cnt = sb("cnt", [P, N], F32, scope)
            inv = sb("inv", [P, N], F32, scope)
            u = sb("u", [P, NT, D], F32, scope)
            w3 = [sb(f"w3_{s}", [P, NT, N], F32R, scope) for s in ("hi", "lo")]
        nc_scope = ExitStack()
        with nc_scope as scope:
            any_dst = sb("any_dst", [P, EC, N], BF16, scope)
            any_rel = sb("any_rel", [P, 4, N], BF16, scope)
        u_t = [a[:, :, :].rearrange("p t d -> p (t d)").rearrange("p (k n) -> p k n", k=KT)
               for a in h_row]

        ps = ctx.enter_context(nc.psum_tensor("ps", [P, 8, 512], F32))

        names = """x_in edges_in key_rows_in etw_in bcol_in brow_in out_stored
            iota_made ident_made later_made exp_made ones_made
            edge_rows edges_turned edge_cols keys_made hots_made hots_used packed_made digits_made
            digits_kept check_ready check_summed check_made counts_final
            any_dst_made any_rel_made any_rel_used any_counts_read any_key_moved
            hot_val_made hot_val_used mask_decoded sparse_kept sp_max sp_exp sp_ln mask_made total_made
            var_ready std_ready shift_ready h_ready
            turned turn_hi turn_lo
            weight_turned w_hi w_lo w_used out_hi out_lo
            v_turned v_hi v_lo
            q_cleared scores_ready scores_read exp_ready sum_inverted
            probs_by_pool probs_by_vec probs_turned pt_hi pt_lo pv_done head_hi head_lo
            y_evacuated y_turned y_added
            row_hi row_lo rel_ready agg_ready agg_read mean_hi mean_lo
            u_ready u_tanh gate_sum gate_product x_gated
            mid_ready x_based x_done w3_hi w3_lo out_based out_psum out_done
            vec_chain pool_chain act_chain sum_ready inv_made sp_made dup_found held_vec held_pool""".split()
        S = {n: sem(n) for n in names}
        raw_in = [sem(f"raw_in{i}") for i in range(RING)]
        q_staged = [sem(f"q_staged_{s}") for s in ("even", "odd")]
        v_staged = [sem(f"v_staged_{s}") for s in ("even", "odd")]

        T_WO = 6 * KT
        T_ROOT = 7 * KT
        T_REL = T_ROOT + KT
        T_GX = T_REL + R * KT
        T_GU = T_GX + KT
        T_S0 = T_GU + KT
        T_N0 = T_S0 + KT
        T_S1 = T_N0 + KT
        T_N1 = T_S1 + KT
        T_END = T_N1 + KT
        W_CREDIT = RING
        O_CREDIT = 2
        PV_CREDIT = 3
        M_CREDIT = 2
        Y_H0, Y_H1 = 0, KT
        Y_U, Y_H2 = 2 * KT, 3 * KT
        Y_MID, Y_H3 = 4 * KT, 5 * KT
        SRC, DST, KEY, REL_KEY, TYPE, REL, WEIGHT = range(7)
        QUARTER = EC // 4

        def use_of_slot(g, j):
            return (g * (KT // RING) + (j // RING + 1)) * 16

        def hold(eng):
            eng.sem_inc(S["held_vec"] if eng is nc.vector else S["held_pool"], 1)

        def exists(i, o):
            return not isinstance(i, int) or i * 4 + o < H

        def is_head(i, o, n):
            return isinstance(i, int) and i * 4 + o == n

        block = ctx.enter_context(nc.Block())

        @block.sync
        def _(sp_):
            sp_.dma_start(e_in[:, 0, :], src.rearrange("(c p) -> c p", p=P)).then_inc(S["edges_in"], 16)
            sp_.dma_start(e_in[:, 1, :], dst.rearrange("(c p) -> c p", p=P)).then_inc(S["edges_in"], 16)
            sp_.dma_start(e_in[:, 2, :], et5.rearrange("(c p) -> c p", p=P)).then_inc(S["edges_in"], 16)
            sp_.dma_start(e_in[:, 3, :], et8.rearrange("(c p) -> c p", p=P)).then_inc(S["edges_in"], 16)
            sp_.dma_start(e_w[:, :], ew.rearrange("(c p) -> c p", p=P)).then_inc(S["edges_in"], 16)
            sp_.dma_start(xres[:, :, :], x.rearrange("(t p) d -> p t d", p=P)).then_inc(S["x_in"], 16)

            def load(t0, rows_of, n, looped=True):
                def four(i4, i):
                    for s in range(RING):
                        t = t0 + i4 + s
                        if t0 >= T_ROOT + RING:
                            sp_.wait_ge(S["w_lo"], t - RING + 1)
                        elif t0 >= RING:
                            sp_.wait_ge(S["weight_turned"], t - RING + 1)
                        sp_.dma_start(raw[s][:, :], rows_of(i4 + s)).then_inc(raw_in[s], 16)
                if n == 1 or not looped:
                    for i in range(n):
                        four(RING * i, i)
                else:
                    with sp_.Fori(0, n) as i:
                        four(i * RING, i)

            def rows(w):
                return lambda i: w[bass.ds(i * P, P), :]

            load(0, rows(wq), 1)
            load(RING, lambda i: wq[bass.ds((i + RING) * P, P), :], 1)
            for g, w in enumerate((wk, wv, wiq, wik, wiv)):
                load((g + 1) * KT, rows(w), KT // RING)
            load(T_WO, rows(wo), 1)

            def stage_q(i, o):
                r0 = DH * (o % 2)
                need(sp_, S["scores_ready"], (i * 4 + (o - 1)) * NT)
                sp_.dma_start(q_st[r0:r0 + DH, :, o % 2, :].bitcast(F32),
                              acts[r0:r0 + DH, 0, :, i * 2 + o // 2, :].bitcast(F32))\
                   .then_inc(q_staged[o % 2], 16)

            def stage_v(i, o):
                sp_.wait_ge(S["pv_done"], i * 4 + (2 * o - 3 + 1 + PV_CREDIT))
                sp_.dma_start(v_st[:, o % 2, :, :, :].bitcast(F32),
                              v_rows[:, :, :, bass.ds((i * 2 + o) * P, P)].bitcast(F32))\
                   .then_inc(v_staged[o % 2], 16)

            sp_.wait_ge(S["q_cleared"], 4)
            sp_.wait_ge(S["v_hi"], NT)
            sp_.wait_ge(S["v_lo"], NT)
            stage_q(0, 0)
            stage_q(0, 1)
            with sp_.Fori(0, 3) as i:
                for o in range(2, 6):
                    stage_q(i, o)
                    if o % 2 == 0:
                        stage_v(i, o // 2 - 1)
            for o in range(2, 4):
                stage_q(3, o)
                stage_v(3, o - 2)
            load(T_WO + RING, lambda i: wo[bass.ds((i + RING) * P, P), :], 1)
            load(T_ROOT, rows(root), 1)
            load(T_ROOT + RING, lambda i: root[bass.ds((i + RING) * P, P), :], 1)
            load(T_REL, rows(rel_w.rearrange("r k n -> (r k) n")), R * KT // RING)
            load(T_GX, lambda i: w_gate[bass.ds(i * P + D, P), :], KT // RING)
            load(T_GU, rows(w_gate), KT // RING)
            for t0, w in ((T_S0, w_self0), (T_N0, w_neigh0), (T_S1, w_self1), (T_N1, w_neigh1)):
                load(t0, rows(w), KT // RING)
            for nt in range(NT):
                sp_.wait_ge(S["out_based"], nt + 1)
                sp_.dma_start(out.rearrange("(t p) d -> p t d", p=P)[:, nt, N:D],
                              u[:, nt, N:D]).then_inc(S["out_stored"], 16)
            for nt in range(NT):
                sp_.wait_ge(S["out_done"], nt + 1)
                sp_.dma_start(out.rearrange("(t p) d -> p t d", p=P)[:, nt, 0:N],
                              u[:, nt, 0:N]).then_inc(S["out_stored"], 16)
            sp_.wait_ge(S["out_stored"], 16 * 2 * NT)

        @block.tensor
        def _(pe):
            pe.wait_ge(S["ident_made"], 2)
            pe.wait_ge(S["edge_rows"], 1)
            for f in range(7):
                mm = pe.transpose(ps[:, 0, EC * f:EC * f + EC], e_row[:, f, :], ident[0:EC, 0:EC])
            mm.then_inc(S["edges_turned"], 1)
            pe.wait_ge(S["bcol_in"], 16 * 7)
            pe.transpose(ps[:, 1, 0:7 * KT], b_in[:, :], ident[0:7 * KT, 0:7 * KT]).then_inc(S["edges_turned"], 1)
            pe.wait_ge(S["edge_cols"], 2)

            def count_chunks(c0, first, last):
                for j in range(2):
                    c = c0 + j
                    pe.wait_ge(S["hots_made"], c + 1)
                    for s in range(NT):
                        pe.matmul(ps[:, s, 0:N], hot_src[:, j, P * s:P * s + P], hot_rel[:, j, :],
                                  start=first and j == 0, stop=last and j == 1)
                        for w in range(3):
                            mm = pe.matmul(ps[:, NT + s, 0:N], hot_dst[:, c, P * s:P * s + P],
                                           hot_w[:, j, w, :], start=first and j == 0 and w == 0,
                                           stop=last and j == 1 and w == 2)
                    mm.then_inc(S["hots_used"], 1)

            count_chunks(0, True, False)
            with pe.Fori(1, EC // 2 - 1) as c2:
                count_chunks(c2 * 2, False, False)
            count_chunks(EC - 2, False, True)

            def turn(y, source, f):
                need(pe, S["turn_lo"], y - 1)
                for nt in range(NT):
                    mm = pe.transpose(ps[:, 6 + y % 2, P * nt:P * nt + P],
                                      source[:, nt, P * f:P * f + P], ident[:, :])
                mm.then_inc(S["turned"], 1)

            def turn_weight(g, j):
                pe.wait_ge(raw_in[j % RING], use_of_slot(g, j))
                need(pe, S["w_lo"], g * KT + (j - 1))
                for k in range(KT):
                    mm = pe.transpose(ps[:, 2 + 2 * (j % 2) + k // 4, P * (k % 4):P * (k % 4) + P],
                                      raw[j % RING][:, P * k:P * k + P], ident[:, :])
                mm.then_inc(S["weight_turned"], 1)

            def column_tile(g, j, a):
                pe.wait_ge(S["w_lo"], g * KT + (j + 1))
                i = 0
                for k in range(KT):
                    for stationary, moving in ((whi, 0), (whi, 1), (wlo, 0)):
                        mm = pe.matmul(ps[:, j % 2, 0:N], stationary[j % RING][:, k, :],
                                       acts[:, a, moving, k, :], start=i == 0, stop=i == 3 * KT - 1)
                        i += 1
                mm.then_inc(S["w_used"], 1)

            pe.wait_ge(S["h_ready"], NT)
            for f in range(KT):
                turn(Y_H0 + f, h0, f)

            def mask_chunks(c0, first, last):
                for j in range(2):
                    c = c0 + j
                    pe.wait_ge(S["hot_val_made"], c + 1)
                    for s in range(NT):
                        mm = pe.matmul(ps[:, 5 + s, 0:N], hot_val[:, j, P * s:P * s + P], hot_dst[:, c, :],
                                       start=first and j == 0, stop=last and j == 1)
                    mm.then_inc(S["hot_val_used"], 1)

            pe.wait_ge(S["sparse_kept"], 1)
            pe.wait_ge(S["turn_lo"], Y_H0 + KT)
            mask_chunks(0, True, False)
            with pe.Fori(1, EC // 2 - 1) as c2:
                mask_chunks(c2 * 2, False, False)
            mask_chunks(EC - 2, False, True)

            pe.wait_ge(S["packed_made"], 1)
            turn_weight(0, 0)
            pe.wait_ge(S["mask_decoded"], 1)
            turn_weight(0, 1)

            def eight_tiles(g, a):
                for j in range(KT):
                    turn_weight(g, j + 2)
                    pe.wait_ge(S["out_lo"], g * KT + (j - 1 + O_CREDIT))
                    column_tile(g, j, a)

            with pe.Fori(0, 3) as g:
                eight_tiles(g, 0)
            pe.wait_ge(S["check_ready"], 1)
            pe.matmul(ps[:, 7, 0:1], ones_r[:, :].bitcast(F32), digit_sum[:, R + 2:R + 3], start=True, stop=True)\
              .then_inc(S["check_summed"], 1)
            pe.wait_ge(S["out_lo"], O_CREDIT + 3 * KT)
            with pe.Fori(3, 6) as g:
                eight_tiles(g, g - 2)

            pe.wait_ge(S["out_lo"], O_CREDIT + 6 * KT)
            pe.wait_ge(S["w_lo"], T_WO + 2)
            for m in range(NT):
                for s in range(2):
                    need(pe, (S["v_hi"], S["v_lo"])[s], m)
                    for f in range(KT):
                        mm = pe.transpose(ps[:, 2 + 2 * s + f // 4, P * (f % 4):P * (f % 4) + P],
                                          acts[:, 2, s, f, P * m:P * m + P].bitcast(F32), ident[:, :])
                    mm.then_inc(S["v_turned"], 1)
            pe.wait_ge(S["v_hi"], NT)
            pe.wait_ge(S["v_lo"], NT)

            def scores(i, o):
                pe.wait_ge(q_staged[o % 2], i * 32 + 16 * (o // 2 + 1))
                for nt in range(NT):
                    need(pe, S["scores_read"], (i * 4 + (o - 1)) * NT + (nt + 1))
                    for n, (a, c) in enumerate(((0, 0), (0, 1), (1, 0))):
                        mm = pe.matmul(ps[:, nt, 0:N], q_st[:, a, o % 2, P * nt:P * nt + P],
                                       acts[:, 1, c, i * 2 + o // 2, :], start=n == 0, stop=n == 2)
                    mm.then_inc(S["scores_ready"], 1)

            def turn_probs(i, o):
                pe.wait_ge(S["probs_by_pool"], (i * 4 + (o + 1)) * (NT - 1))
                pe.wait_ge(S["probs_by_vec"], i * 4 + (o + 1))
                for m in range(NT):
                    need(pe, S["pt_lo"], (i * 4 + (o - 1)) * NT + (m + 1))
                    for nt in range(NT):
                        mm = pe.transpose(ps[:, NT + m, P * nt:P * nt + P],
                                          sc[:, o % 2, nt, P * m:P * m + P], ident[:, :])
                    mm.then_inc(S["probs_turned"], 1)

            def weigh_values(i, o):
                pe.wait_ge(S["pt_lo"], (i * 4 + (o + 1)) * NT)
                if o % 2 == 0:
                    pe.wait_ge(v_staged[o // 2 % 2], i * 16 + 16 * (o // 2 // 2 + 1))
                pe.wait_ge(S["head_lo"], i * 4 + (o - 1 + O_CREDIT))
                n = 0
                for m in range(NT):
                    for a, c in ((0, 0), (0, 1), (1, 0)):
                        mm = pe.matmul(ps[:, 6 + o % 2, 0:N], v_st[:, o // 2 % 2, a, m, :],
                                       pt[c][:, o % 2, m, :], start=n == 0, stop=n == 3 * NT - 1)
                        n += 1
                mm.then_inc(S["pv_done"], 1)

            def head(i, o):
                turn_probs(i, o)
                if exists(i, o + 2):
                    scores(i, o + 2)
                if not is_head(i, o, 0):
                    weigh_values(i, o - 1)

            scores(0, 0)
            scores(0, 1)
            head(0, 0)
            with pe.Fori(0, 3) as i:
                for o in range(1, 5):
                    head(i, o)
            for o in range(1, 4):
                head(3, o)
            weigh_values(3, 3)

            pe.wait_ge(S["head_lo"], O_CREDIT + H)
            pe.wait_ge(S["scores_read"], H * NT)

            def turn_y(j):
                pe.wait_ge(S["y_evacuated"], j + 1)
                need(pe, S["y_added"], j - 1)
                for nt in range(NT):
                    mm = pe.transpose(ps[:, 6 + j % 2, P * nt:P * nt + P],
                                      y_t[:, j % 2, P * nt:P * nt + P], ident[:, :])
                mm.then_inc(S["y_turned"], 1)

            for j in range(KT):
                if j + 2 < KT:
                    turn_weight(6, j + 2)
                need(pe, S["y_evacuated"], j - 1)
                column_tile(6, j, 0)
                if j:
                    turn_y(j - 1)
            turn_y(KT - 1)

            def any_chunks(r, c0, first, last):
                for j in range(4):
                    c = c0 + j
                    pe.wait_ge(S["any_rel_made"], r * EC + (c + 1))
                    for s in range(NT):
                        mm = pe.matmul(ps[:, s, 0:N], any_rel[:, j, P * s:P * s + P], any_dst[:, c, :],
                                       start=first and j == 0, stop=last and j == 3)
                    mm.then_inc(S["any_rel_used"], 1)

            pe.wait_ge(S["check_made"], 1)
            with pe.If(pe.value_load(no_digits[0:1, 0:1], min_val=0, max_val=1) > 0):
                pe.wait_ge(S["any_dst_made"], EC)
                with pe.Fori(0, R) as r:
                    pe.wait_ge(S["any_counts_read"], r + 1)
                    any_chunks(r, 0, True, False)
                    with pe.Fori(1, EC // 4 - 1) as c4:
                        any_chunks(r, c4 * 4, False, False)
                    any_chunks(r, EC - 4, False, True)

            def row_block(t, slot, stationary, k, first=False, last=False, bank_free=None):
                pe.wait_ge(S["w_lo"], t + 1)
                for nt in range(NT):
                    if bank_free:
                        bank_free(nt)
                    for a, weight in ((0, whi_row), (0, wlo_row), (1, whi_row)):
                        for f in range(2):
                            mm = pe.matmul(ps[:, 2 * nt + f, :], stationary[a][:, k, P * nt:P * nt + P],
                                           weight[slot][:, HALF * f:HALF * f + HALF],
                                           start=first and a == 0 and weight is whi_row,
                                           stop=last and a == 1, skip_group_check=True)
                    if last and nt < NT - 1:
                        mm.then_inc(S["sum_ready"], 1)
                mm.then_inc(S["w_used"], 1)

            def start_relation(q, edges, a6):
                a6()
                for s in range(NT):
                    mm = pe.matmul(ps[:, 6, 0:N], ones_r[:, :], edges[:, s, :], start=s == 0, stop=s == NT - 1)
                mm.then_inc(S["agg_ready"], 1)
                sum_edges(q, edges, 0)

            def sum_edges(q, edges, k):
                if k:
                    pe.wait_ge(S["agg_read"], q * (KT + 1) + k)
                i = 0
                for s in range(NT):
                    for a in range(2):
                        mm = pe.matmul(ps[:, 7 - k % 2, 0:N], h_row[a][:, s, P * k:P * k + P],
                                       edges[:, s, :], start=i == 0, stop=i == 2 * NT - 1)
                        i += 1
                mm.then_inc(S["agg_ready"], 1)

            def aggregated(q, k):
                pe.wait_ge(S["mean_hi"], q * KT + (k + 1))
                pe.wait_ge(S["mean_lo"], q * KT + (k + 2))

            def own_product(t0, y0, source, q, edges, first_free=None):
                for k in range(KT):
                    if k == KT - 1:
                        pe.wait_ge(S["row_lo"], (q - R + 1) * NT + NT if q >= R else NT)
                        if q == 0:
                            pe.wait_ge(S["rel_ready"], 1)
                        start_relation(q, edges, lambda: pe.wait_ge(S["turn_lo"], y0 + KT))
                    pe.wait_ge(S["turn_lo"], y0 + k + 1)
                    row_block(t0 + k, k % RING, h_t, k, first=k == 0,
                              bank_free=first_free if k == 0 else None)
                    if k + 2 < KT:
                        turn(y0 + k + 2, source, k + 2)

            def relation(q, t0, edges, last):
                for k in range(KT):
                    if k < KT - 1:
                        sum_edges(q, edges, k + 1)
                    elif not last:
                        pe.wait_ge(S["rel_ready"], q + 2)
                        start_relation(q + 1, edges, lambda: pe.wait_ge(S["agg_read"], (q + 1) * (KT + 1)))
                    aggregated(q, k)
                    row_block(t0 + k, k % RING, [m_pair(k, a) for a in range(2)], 0, last=last and k == KT - 1)

            def m_pair(k, a):
                return mean[a][:, k % 2:k % 2 + 1, :]

            def begin(q):
                y0 = (Y_H1, Y_H2, Y_MID)[q]
                pe.wait_ge(S["h_ready"], NT * (q + 2))
                if q == 0:
                    pe.wait_ge(S["y_added"], KT)
                else:
                    pe.wait_ge(S["agg_read"], (KT + 1) * (R + q - 1))
                turn(y0, h, 0)
                turn(y0 + 1, h, 1)
                return y0

            y0 = begin(0)
            own_product(T_ROOT, y0, h, 0, rel_r)
            with pe.Fori(0, R - 1) as r:
                relation(r, T_REL + r * KT, rel_r, False)
            relation(R - 1, T_REL + (R - 1) * KT, rel_r, True)

            pe.wait_ge(S["agg_read"], R * (KT + 1))
            for k in range(KT):
                row_block(T_GX + k, k % RING, h_t, k, first=k == 0,
                          bank_free=(lambda nt: pe.wait_ge(S["u_ready"], 2 * nt + 2)) if k == 0 else None)
                turn(Y_U + k, u, k)
            for k in range(KT):
                pe.wait_ge(S["turn_lo"], Y_U + k + 1)
                row_block(T_GU + k, k % RING, u_t, k, last=k == KT - 1)

            y0 = begin(1)
            own_product(T_S0, y0, h, R, total_r)
            relation(R, T_N0, total_r, True)
            y0 = begin(2)
            own_product(T_S1, y0, h, R + 1, total_r)
            relation(R + 1, T_N1, total_r, True)

            pe.wait_ge(S["h_ready"], NT * 5)
            pe.wait_ge(S["agg_read"], (KT + 1) * (R + 2))
            for f in range(NT):
                turn(Y_H3 + f, h, f)
            pe.wait_ge(S["turn_lo"], Y_H3 + NT)
            pe.wait_ge(S["w3_lo"], 1)
            for nt in range(NT):
                i = 0
                for k in range(NT):
                    for a, w in ((0, 0), (0, 1), (1, 0)):
                        mm = pe.matmul(ps[:, nt, 0:N], h_t[a][:, k, P * nt:P * nt + P], w3[w][:, k, :],
                                       start=i == 0, stop=i == 3 * NT - 1)
                        i += 1
                mm.then_inc(S["out_psum"], 1)

        @block.scalar
        def _(act):
            link = Chain(act, S["act_chain"])
            act.dma_start(etw_b[:, :], etw.partition_broadcast(P)).then_inc(S["etw_in"], 16)
            for g, b in enumerate((bq, bk, bv, biq, bik, biv, bo)):
                act.dma_start(b_in[KT * g:KT * g + KT, :], b.rearrange("(j p) -> j p", p=P)).then_inc(S["bcol_in"], 16)

            def key_rows(q):
                act.dma_start(key_i[:, 0, :], src[q * (E // 4):(q + 1) * (E // 4)].partition_broadcast(P))\
                   .then_inc(S["key_rows_in"], 16)
                act.dma_start(key_i[:, 1, :], dst[q * (E // 4):(q + 1) * (E // 4)].partition_broadcast(P))\
                   .then_inc(S["key_rows_in"], 16)

            key_rows(0)
            act.wait_ge(S["sp_max"], 1)
            act.activation(sp[:, 3, :], sp[:, 2, :], ACT.Exp, scale=-1.0).then_inc(S["sp_exp"], 1)
            act.wait_ge(S["sp_exp"], 1)
            act.activation(sp[:, 4, :], sp[:, 3, :], ACT.Ln, bias=1.0).then_inc(S["sp_ln"], 1)

            def layer_norm(n, target):
                for nt in range(NT):
                    act.wait_ge(S["var_ready"], NT * n + nt + 1)
                    act.activation(std[:, nt, :], mv[:, nt, 1:2], ACT.Sqrt, bias=epsc[:, 0:1]).then_inc(S["std_ready"], 1)
                for nt in range(NT):
                    act.wait_ge(S["shift_ready"], NT * n + nt + 1)
                    act.activation(target[:, nt, :], xres[:, nt, :], ACT.Relu, bias=shift[:, nt, :],
                                   scale=rstd[:, nt, :]).then_inc(S["h_ready"], 1)

            for q in range(1, 4):
                act.wait_ge(S["keys_made"], q)
                key_rows(q)
            layer_norm(0, h0)
            act.wait_ge(S["hots_used"], EC + M_CREDIT)
            act.activation(sparse_w[:, :, :], ps[:, NT:2 * NT, 0:N], ACT.Copy).then_inc(S["sparse_kept"], 1)

            def turned_high(y, target):
                act.wait_ge(S["turned"], y + 1)
                act.activation(target, ps[:, 6 + y % 2, 0:N], ACT.Copy).then_inc(S["turn_hi"], 1)

            def column_high(g, j):
                act.wait_ge(S["weight_turned"], g * KT + (j + 1))
                act.wait_ge(S["w_used"], g * KT + (j + 1))
                b = 2 + 2 * (j % 2)
                act.activation(whi[j % RING][:, :, :],
                               ps[:, b:b + 2, :].rearrange("p b (k n) -> p (b k) n", n=P), ACT.Copy)\
                   .then_inc(S["w_hi"], 1)

            def row_high(t, slot, use):
                act.wait_ge(raw_in[slot], use)
                act.wait_ge(S["w_used"], t + 1)
                act.activation(whi_row[slot], raw[slot][:, :], ACT.Copy).then_inc(S["w_hi"], 1)

            def row_high_at(t):
                row_high(t, t % RING, 16 * (t // RING + 1))

            for f in range(KT):
                turned_high(Y_H0 + f, acts[:, 0, 0, f, :])
            for r in range(R):
                act.wait_ge(S["digits_made"], r + 1)
                act.activation(counts16[:, NT * r:NT * r + NT, :].rearrange("p t n -> p (t n)"), digits[r % 2],
                               ACT.Copy, accum_out=digit_sum[:, r:r + 1]).then_inc(S["digits_kept"], 1)
            column_high(0, 0)
            column_high(0, 1)

            def eight_tiles(g, a):
                for j in range(KT):
                    column_high(g, j + 2)
                    act.wait_ge(S["w_used"], g * KT + (j + 1 + W_CREDIT))
                    act.activation(acts[:, a, 0, j, :], ps[:, j % 2, 0:N], ACT.Identity,
                                   bias=bcol[:, bass.ds(g * KT + j, 1)]).then_inc(S["out_hi"], 1)

            with act.Fori(0, 3) as g:
                act.wait_ge(S["mask_made"], g // 2 + 1)
                eight_tiles(g, g + 1)
            with act.Fori(3, 6) as g:
                eight_tiles(g, g - 3)
            for m in range(NT):
                act.wait_ge(S["v_turned"], 2 * m + 1)
                act.activation(v_rows[:, 0, m, :], ps[:, 2:4, :].rearrange("p b n -> p (b n)"), ACT.Copy)\
                   .then_inc(S["v_hi"], 1)

            def exps(i, o):
                for nt in range(NT):
                    act.wait_ge(S["scores_read"], (i * 4 + o) * NT + (nt + 1))
                    act.activation(sc[:, o % 2, nt, :], sc[:, o % 2, nt, :], ACT.Exp, scale=-1.0,
                                   bias=nmax[:, o % 2, nt:nt + 1],
                                   accum_out=rsum[:, o % 2, nt:nt + 1]).then_inc(S["exp_ready"], 1)

            def head(i, o):
                for m in range(NT):
                    act.wait_ge(S["probs_turned"], (i * 4 + o) * NT + (m + 1))
                    act.wait_ge(S["pv_done"], i * 4 + (o - 1 + PV_CREDIT))
                    act.activation(pt[0][:, o % 2, m, :], ps[:, NT + m, 0:N], ACT.Copy).then_inc(S["pt_hi"], 1)
                if exists(i, o + 2):
                    exps(i, o + 2)
                if not is_head(i, o, 0):
                    head_out(i, o - 1)

            def head_out(i, o):
                r = DH * (o % 2)
                act.wait_ge(S["pv_done"], i * 4 + (o + 1 + PV_CREDIT))
                act.activation(acts[r:r + DH, 0, 0, i * 2 + o // 2, :], ps[r:r + DH, 6 + o % 2, 0:N], ACT.Copy)\
                   .then_inc(S["head_hi"], 1)

            exps(0, 0)
            exps(0, 1)
            head(0, 0)
            with act.Fori(0, 3) as i:
                for o in range(1, 5):
                    head(i, o)
            for o in range(1, 4):
                head(3, o)
            act.wait_ge(S["probs_turned"], H * NT)
            act.dma_start(xres[:, :, :], x.rearrange("(t p) d -> p t d", p=P)).then_inc(S["x_in"], 16)
            head_out(3, 3)

            for j in range(KT):
                if j + 2 < KT:
                    column_high(6, j + 2)
                else:
                    row_high_at(T_WO + j + 2)
                act.wait_ge(S["w_used"], T_WO + j + 1 + W_CREDIT)
                need(act, S["y_turned"], j - 1)
                act.activation(y_t[:, j % 2, :], ps[:, j % 2, 0:N], ACT.Identity,
                               bias=bcol[:, T_WO + j:T_WO + j + 1]).then_inc(S["y_evacuated"], 1)

            def bias_row(b, last_use, count):
                act.wait_ge(S[last_use], count)
                act.dma_start(brow[:, :], b.partition_broadcast(P)).then_inc(S["brow_in"], 16)

            def row_parts(n):
                for nt in range(NT):
                    act.wait_ge(S["h_ready"], NT * (n + 2))
                    if n == 1:
                        act.wait_ge(S["w_used"], T_S0 + W_CREDIT)
                    if n == 2:
                        act.wait_ge(S["agg_ready"], (KT + 1) * (R + 1))
                    act.activation(h_row[0][:, nt, :], h[:, nt, :], ACT.Copy).then_inc(S["row_hi"], 1)

            def mean_high(q, k):
                act.wait_ge(S["agg_read"], q * (KT + 1) + (k + 2))
                act.activation(mean[0][:, k % 2, :], mean_f[:, k % 2, :], ACT.Copy).then_inc(S["mean_hi"], 1)

            def relation_edges(r):
                act.wait_ge(S["counts_final"], 1)
                need(act, S["agg_ready"], r * (KT + 1))
                act.activation(rel_r[:, :, :], counts16[:, bass.ds(r * NT, NT), :], ACT.Copy)\
                   .then_inc(S["rel_ready"], 1)

            def own_product(n, t0, q):
                for k in range(KT):
                    row_high_at(t0 + k + 2)
                    if k + 2 < KT:
                        turned_high((Y_H1, Y_H2, Y_MID)[n] + k + 2, h_t[0][:, k + 2, :])
                    if k == 1:
                        row_parts(n)
                    if k == 3 and n == 0:
                        relation_edges(0)
                mean_high(q, 0)

            def relation(q, t0, last, more=True):
                for k in range(KT):
                    if isinstance(t0, int):
                        if t0 + k + 2 < T_END:
                            row_high_at(t0 + k + 2)
                    else:
                        row_high(t0 + (k + 2), (k + 2) % RING, use_of_slot(q + T_REL // KT, k + 2))
                    if k < KT - 1:
                        act.wait_ge(S["w_used"], t0 + (k + W_CREDIT))
                        mean_high(q, k + 1)
                    if k == KT - 2 and not last:
                        act.wait_ge(S["agg_ready"], q * (KT + 1) + (KT + 1))
                        act.activation(rel_r[:, :, :], counts16[:, bass.ds(q * NT + NT, NT), :], ACT.Copy)\
                           .then_inc(S["rel_ready"], 1)
                if not last:
                    act.wait_ge(S["w_used"], t0 + (KT - 1 + W_CREDIT))
                    mean_high(q + 1, 0)

            bias_row(bias1, "y_turned", KT)
            layer_norm(1, h)
            turned_high(Y_H1, h_t[0][:, 0, :])
            turned_high(Y_H1 + 1, h_t[0][:, 1, :])
            own_product(0, T_ROOT, 0)
            with act.Fori(0, R - 1) as r:
                relation(r, T_REL + r * KT, False)
            relation(R - 1, T_REL + (R - 1) * KT, True)
            for k in range(KT):
                row_high_at(T_GX + k + 2)
                turned_high(Y_U + k, u_t[0][:, k, :])
                if k == 1:
                    bias_row(b_gate, "u_ready", 2 * NT)
            for k in range(KT):
                row_high_at(T_GU + k + 2)
                if k < NT:
                    act.wait_ge(S["turned"], Y_U + KT)
                    act.activation(u[:, k, :], u[:, k, :], ACT.Tanh).then_inc(S["u_tanh"], 1)
            bias_row(b0, "gate_sum", NT)
            layer_norm(2, h)
            turned_high(Y_H2, h_t[0][:, 0, :])
            turned_high(Y_H2 + 1, h_t[0][:, 1, :])
            own_product(1, T_S0, R)
            relation(R, T_N0, True)
            for nt in range(NT):
                act.wait_ge(S["mid_ready"], 2 * nt + 2)
                act.activation(h[:, nt, :], h[:, nt, :], ACT.Relu).then_inc(S["h_ready"], 1)
            bias_row(b1, "mid_ready", 2 * NT)
            turned_high(Y_MID, h_t[0][:, 0, :])
            turned_high(Y_MID + 1, h_t[0][:, 1, :])
            own_product(2, T_S1, R + 1)
            act.activation(w3[0][:, :, :], sparse_w[:, :, :], ACT.Copy).then_inc(S["w3_hi"], 1)
            relation(R + 1, T_N1, True)
            bias_row(bias3, "x_based", NT)
            layer_norm(3, h)
            for f in range(NT):
                turned_high(Y_H3 + f, h_t[0][:, f, :])

        @block.vector
        def _(dve):
            link = Chain(dve, S["vec_chain"])
            dve.sem_inc(S["w_used"], W_CREDIT)
            dve.sem_inc(S["out_lo"], O_CREDIT)
            dve.sem_inc(S["head_lo"], O_CREDIT)
            dve.sem_inc(S["pv_done"], PV_CREDIT)
            for name in ("mask_made", "mean_lo", "any_counts_read"):
                dve.sem_inc(S[name], 1)
            for name in ("dup_found", "hots_used", "hot_val_used"):
                dve.sem_inc(S[name], M_CREDIT)
            dve.sem_inc(S["any_rel_used"], 4)
            dve.memset(epsc[:, :], EPS).then_inc(S["ones_made"], 1)
            dve.memset(same[:, 0, :], 1.0).then_inc(S["ones_made"], 1)
            dve.wait_ge(S["ones_made"], 2)
            dve.tensor_copy(ones_r[:, :], same[:, 0, :]).then_inc(S["ones_made"], 1)

            dve.wait_ge(S["edges_in"], 16 * 5)
            dve.tensor_copy(e_row[:, SRC, :], e_in[:, 0, :])
            dve.tensor_copy(e_row[:, DST, :], e_in[:, 1, :])
            dve.tensor_copy(e_row[:, TYPE, :], e_in[:, 2, :])
            dve.tensor_copy(e_row[:, WEIGHT, :], e_w[:, :])
            dve.scalar_tensor_tensor(e_row[:, KEY, :], e_in[:, 0, :], float(N), e_in[:, 1, :], ALU.mult, ALU.add)
            dve.tensor_copy(e_row[:, REL, :], e_in[:, 3, :])
            dve.scalar_tensor_tensor(e_row[:, REL_KEY, :], e_in[:, 3, :], float(N), e_in[:, 0, :], ALU.mult, ALU.add)\
               .then_inc(S["edge_rows"], 1)
            dve.wait_ge(S["etw_in"], 16)
            link(dve.tensor_scalar(sp[:, 0, :], etw_b[:, :], 0.0, None, ALU.max))
            link(dve.tensor_scalar(sp[:, 1, :], etw_b[:, :], -1.0, None, ALU.mult))
            dve.tensor_tensor(sp[:, 2, :], etw_b[:, :], sp[:, 1, :], ALU.max).then_inc(S["sp_max"], 1)

            def norm_stats(nt):
                for f in range(2):
                    ins = dve.bn_stats(stats[:, nt, f, :], xres[:, nt, HALF * f:HALF * f + HALF])
                    link(ins)
                dve.bn_aggr(mv[:, nt, :], stats[:, nt, :, :].rearrange("p a b -> p (a b)")).then_inc(S["var_ready"], 1)

            def norm_shift(n, nt):
                dve.wait_ge(S["std_ready"], NT * n + nt + 1)
                link(dve.reciprocal(rstd[:, nt, :], std[:, nt, :]))
                dve.scalar_tensor_tensor(shift[:, nt, :], mv[:, nt, 0:1], -1.0, rstd[:, nt, :], ALU.mult, ALU.mult)\
                   .then_inc(S["shift_ready"], 1)

            dve.wait_ge(S["edges_turned"], 2)
            dve.tensor_copy(e_col[:, :, :], ps[:, 0, 0:7 * EC].rearrange("p (f c) -> p f c", f=7))\
               .then_inc(S["edge_cols"], 1)
            dve.tensor_copy(bcol[:, :], ps[:, 1, 0:7 * KT]).then_inc(S["edge_cols"], 1)
            dve.wait_ge(S["edge_cols"], 2)
            link(dve.tensor_scalar(rel_exp[:, 0, :], e_col[:, REL, :], float(DIGIT), 127.0, ALU.mult, ALU.add))
            link(dve.tensor_scalar(rel_exp[:, 1, :], rel_exp[:, 0, :], 23, None, ALU.logical_shift_left))
            rel_place = rel_exp[:, 1, :].bitcast(F32)
            left = e_col[:, WEIGHT, :]
            for w in range(3):
                link(dve.tensor_copy(w_bf[:, w, :], left))
                link(dve.tensor_copy(w_part[:, w, :], w_bf[:, w, :]))
                if w < 2:
                    link(dve.tensor_tensor(w_rest[:, w, :], left, w_part[:, w, :], ALU.subtract))
                    left = w_rest[:, w, :]
            dve.wait_ge(S["iota_made"], 1)
            dve.wait_ge(S["later_made"], 2)

            def one_hots(c0):
                for j in range(2):
                    c = c0 + j
                    col = bass.ds(c, 1)
                    dve.wait_ge(S["hots_used"], c + (j * 0 + 1))
                    dve.tensor_scalar(hot_dst[:, c, :], iota[:, :], e_col[:, DST, col], None, ALU.is_equal)
                    dve.tensor_scalar(hot_rel[:, j, :], iota[:, :], e_col[:, DST, col], rel_place[:, col],
                                      ALU.is_equal, ALU.mult)
                    dve.tensor_scalar(hot_src[:, j, :], iota[:, :], e_col[:, SRC, col], None, ALU.is_equal)
                    for w in range(3):
                        ins = dve.tensor_scalar(hot_w[:, j, w, :], iota[:, :], e_col[:, SRC, col],
                                                w_part[:, w, col], ALU.is_equal, ALU.mult)
                    ins.then_inc(S["hots_made"], 1)

            def find_later(q, c2):
                for j in range(2):
                    c = c2 * 2 + (q * QUARTER + j)
                    dve.wait_ge(S["dup_found"], c + 1)
                    dve.scalar_tensor_tensor(same[:, j, :], key_row[:, q % 2, bass.ds((c2 * 2 + j) * P, P)],
                                             e_col[:, KEY, bass.ds(c, 1)], later[:, :], ALU.is_equal, ALU.mult,
                                             accum_out=dup[:, bass.ds(c, 1)]).then_inc(S["dup_found"], 1)

            for q in range(4):
                dve.wait_ge(S["key_rows_in"], q * 32 + 32)
                need(dve, S["dup_found"], (q - 1) * QUARTER + M_CREDIT if q > 1 else 0)
                dve.scalar_tensor_tensor(key_row[:, q % 2, :], key_i[:, 0, :], float(N), key_i[:, 1, :],
                                         ALU.mult, ALU.add).then_inc(S["keys_made"], 1)
                dve.wait_ge(S["keys_made"], q + 1)
                hold(dve)
                with dve.Fori(0, QUARTER // 2) as c2:
                    one_hots(c2 * 2 + q * QUARTER)
                    find_later(q, c2)
                if q < NT:
                    dve.wait_ge(S["x_in"], 16)
                    norm_stats(q)
            for nt in range(NT):
                norm_shift(0, nt)
            dve.wait_ge(S["exp_made"], 1)
            dve.wait_ge(S["dup_found"], EC + M_CREDIT)
            link(dve.tensor_scalar(live[:, :], dup[:, :], 0.0, None, ALU.is_equal))
            link(dve.tensor_scalar(chunk_val[:, :], chunk_exp[:, :], 23, None, ALU.logical_shift_left))
            link(dve.tensor_scalar(edge_val[:, :], e_col[:, TYPE, :], 0.125, 1.0, ALU.mult, ALU.add))
            link(dve.tensor_tensor(edge_val[:, :], edge_val[:, :], live[:, :], ALU.mult))
            link(dve.tensor_tensor(edge_val[:, :], edge_val[:, :], chunk_val[:, :].bitcast(F32), ALU.mult))

            def turned_low(y, target, hi):
                dve.wait_ge(S["turn_hi"], y + 1)
                dve.tensor_tensor(target, ps[:, 6 + y % 2, 0:N], hi.bitcast(F32), ALU.subtract).then_inc(S["turn_lo"], 1)

            dve.wait_ge(S["hots_used"], EC + M_CREDIT)
            dve.tensor_scalar(packed.rearrange("p (t n) -> p t n", t=NT), ps[:, 0:NT, 0:N], 2.0 ** 30, None,
                              ALU.min).then_inc(S["packed_made"], 1)
            for f in range(KT):
                turned_low(Y_H0 + f, acts[:, 0, 1, f, :], acts[:, 0, 0, f, :])
            dve.wait_ge(S["packed_made"], 1)
            for r in range(R):
                need(dve, S["digits_kept"], r - 1)
                if r < R - 1:
                    ins = dve.tensor_scalar(digits[r % 2], packed, DIGIT * r, 2 ** DIGIT - 1,
                                            ALU.logical_shift_right, ALU.bitwise_and)
                else:
                    ins = dve.tensor_scalar(digits[r % 2], packed, DIGIT * r, None,
                                            ALU.logical_shift_right)
                ins.then_inc(S["digits_made"], 1)
                with dve.Fori(r * EC // R // 2, (r + 1) * EC // R // 2) as c2:
                    for j in range(2):
                        dve.wait_ge(S["hot_val_used"], c2 * 2 + (j + 1))
                        col = bass.ds(c2 * 2 + j, 1)
                        dve.tensor_scalar(hot_val[:, j, :], iota[:, :], e_col[:, SRC, col], edge_val[:, col],
                                          ALU.is_equal, ALU.mult).then_inc(S["hot_val_made"], 1)
            dve.wait_ge(S["hot_val_used"], EC + M_CREDIT)
            types = packed
            dve.tensor_copy(codes.bitcast(F32).rearrange("p (t n) -> p t n", t=NT), ps[:, 5:5 + NT, 0:N])\
               .then_inc(S["mask_decoded"], 1)
            dve.wait_ge(S["mask_decoded"], 1)
            link(dve.tensor_scalar(types, codes, 20, 7, ALU.logical_shift_right, ALU.bitwise_and))
            dve.wait_ge(S["digits_kept"], R - 1)
            dve.tensor_copy(key_row[:, 0, 0:NT * N], types).then_inc(S["mask_decoded"], 1)
            dve.wait_ge(S["sp_ln"], 1)
            dve.tensor_tensor(sp[:, 5, :], sp[:, 0, :], sp[:, 4, :], ALU.add).then_inc(S["sp_made"], 1)

            def column_low(g, j):
                dve.wait_ge(S["w_hi"], g * KT + (j + 1))
                b = 2 + 2 * (j % 2)
                dve.tensor_tensor(wlo[j % RING][:, :, :],
                                  ps[:, b:b + 2, :].rearrange("p b (k n) -> p (b k) n", n=P),
                                  whi[j % RING][:, :, :].bitcast(F32), ALU.subtract).then_inc(S["w_lo"], 1)

            def row_low(t, slot):
                dve.wait_ge(S["w_hi"], t + 1)
                dve.tensor_tensor(wlo_row[slot], raw[slot][:, :], whi_row[slot].bitcast(F32), ALU.subtract)\
                   .then_inc(S["w_lo"], 1)

            column_low(0, 0)
            column_low(0, 1)
            dve.wait_ge(S["digits_kept"], R)
            link(dve.tensor_reduce(digit_sum[:, R:R + 1], digit_sum[:, 0:R], AX.X, ALU.add))
            link(dve.tensor_reduce(digit_sum[:, R + 1:R + 2], digits[(R - 1) % 2], AX.X, ALU.max))
            link(dve.tensor_scalar(digit_sum[:, R + 1:R + 2], digit_sum[:, R + 1:R + 2], float(2 ** DIGIT),
                                   float(2 * E), ALU.is_ge, ALU.mult))
            dve.tensor_tensor(digit_sum[:, R + 2:R + 3], digit_sum[:, R:R + 1], digit_sum[:, R + 1:R + 2], ALU.add)\
               .then_inc(S["check_ready"], 1)

            def eight_tiles(g, a):
                for j in range(KT):
                    column_low(g, j + 2)
                    dve.wait_ge(S["out_hi"], g * KT + (j + 1))
                    dve.scalar_tensor_tensor(acts[:, a, 1, j, :], ps[:, j % 2, 0:N], bcol[:, bass.ds(g * KT + j, 1)],
                                             acts[:, a, 0, j, :].bitcast(F32), ALU.add, ALU.subtract)\
                       .then_inc(S["out_lo"], 1)

            with dve.Fori(0, 3) as g:
                eight_tiles(g, g + 1)
            dve.wait_ge(S["check_summed"], 1)
            dve.tensor_scalar(no_digits[:, :], ps[:, 7, 0:1], float(E), None, ALU.not_equal).then_inc(S["check_made"], 1)
            with dve.Fori(3, 6) as g:
                eight_tiles(g, g - 3)
            for m in range(NT):
                dve.wait_ge(S["v_turned"], 2 * m + 2)
                dve.tensor_copy(v_rows[:, 1, m, :], ps[:, 4:6, :].rearrange("p b n -> p (b n)")).then_inc(S["v_lo"], 1)

            dve.wait_ge(S["mask_made"], 2)

            def score_max(i, o):
                for nt in range(NT):
                    dve.wait_ge(S["scores_ready"], (i * 4 + o) * NT + (nt + 1))
                    need(dve, S["probs_turned"], (i * 4 + (o - 1)) * NT)
                    hold(dve)
                    dve.tensor_tensor_reduce(sc[:, o % 2, nt, :], ps[:, nt, 0:N], mask[:, nt, :], -SCALE, 3e38,
                                             ALU.add, ALU.min, nmax[:, o % 2, nt:nt + 1]).then_inc(S["scores_read"], 1)

            def invert_sum(i, o, nt):
                dve.wait_ge(S["exp_ready"], (i * 4 + o) * NT + (nt + 1))
                dve.reciprocal(rinv[:, o % 2, nt:nt + 1], rsum[:, o % 2, nt:nt + 1]).then_inc(S["sum_inverted"], 1)

            def normalise(i, o):
                invert_sum(i, o, NT - 1)
                dve.wait_ge(S["sum_inverted"], (i * 4 + (o + 1)) * NT)
                dve.tensor_scalar(sc[:, o % 2, NT - 1, :], sc[:, o % 2, NT - 1, :], rinv[:, o % 2, NT - 1:NT],
                                  None, ALU.mult).then_inc(S["probs_by_vec"], 1)

            def head(i, o):
                if exists(i, o + 2):
                    score_max(i, o + 2)
                for m in range(NT):
                    if exists(i, o + 2) and m < NT - 1:
                        invert_sum(i, o + 2, m)
                    dve.wait_ge(S["pt_hi"], (i * 4 + o) * NT + (m + 1))
                    dve.tensor_tensor(pt[1][:, o % 2, m, :], ps[:, NT + m, 0:N], pt[0][:, o % 2, m, :].bitcast(F32),
                                      ALU.subtract).then_inc(S["pt_lo"], 1)
                if exists(i, o + 2):
                    normalise(i, o + 2)
                if not is_head(i, o, 0):
                    head_out(i, o - 1)

            def head_out(i, o):
                r = DH * (o % 2)
                dve.wait_ge(S["head_hi"], i * 4 + (o + 1))
                dve.tensor_tensor(acts[r:r + DH, 0, 1, i * 2 + o // 2, :], ps[r:r + DH, 6 + o % 2, 0:N],
                                  acts[r:r + DH, 0, 0, i * 2 + o // 2, :].bitcast(F32), ALU.subtract)\
                   .then_inc(S["head_lo"], 1)

            for o in range(2):
                score_max(0, o)
                for nt in range(NT - 1):
                    invert_sum(0, o, nt)
                normalise(0, o)
            head(0, 0)
            with dve.Fori(0, 3) as i:
                for o in range(1, 5):
                    head(i, o)
            for o in range(1, 4):
                head(3, o)
            head_out(3, 3)

            def add_y(j):
                dve.wait_ge(S["y_turned"], j + 1)
                dve.tensor_tensor(xres[:, :, P * j:P * j + P], xres[:, :, P * j:P * j + P],
                                  ps[:, 6 + j % 2, 0:N].rearrange("p (t n) -> p t n", t=NT), ALU.add)\
                   .then_inc(S["y_added"], 1)

            dve.wait_ge(S["x_in"], 32)
            for j in range(KT):
                if j + 2 < KT:
                    column_low(6, j + 2)
                else:
                    row_low(T_WO + j + 2, (j + 2) % RING)
                if j:
                    add_y(j - 1)
            add_y(KT - 1)
            dve.wait_ge(S["y_added"], KT)

            dve.wait_ge(S["check_made"], 1)
            with dve.If(dve.value_load(no_digits[0:1, 0:1], min_val=0, max_val=1) > 0):
                with dve.Fori(0, EC) as c:
                    dve.tensor_scalar(any_dst[:, c, :], iota[:, :], e_col[:, DST, bass.ds(c, 1)],
                                      None, ALU.is_equal).then_inc(S["any_dst_made"], 1)
                with dve.Fori(0, R) as r:
                    with dve.Fori(0, EC // 4) as c4:
                        for j in range(4):
                            dve.wait_ge(S["any_rel_used"], r * EC + (c4 * 4 + (j + 1)))
                            dve.tensor_scalar(any_rel[:, j, :], iota[:, :], e_col[:, REL_KEY, bass.ds(c4 * 4 + j, 1)],
                                              None, ALU.is_equal).then_inc(S["any_rel_made"], 1)
                    dve.wait_ge(S["any_rel_used"], r * EC + (EC + 4))
                    dve.tensor_copy(counts16[:, bass.ds(r * NT, NT), :], ps[:, 0:NT, 0:N])\
                       .then_inc(S["any_counts_read"], 1)
                    dve.tensor_scalar(e_col[:, REL_KEY, :], e_col[:, REL_KEY, :], -float(N), None, ALU.add)\
                       .then_inc(S["any_key_moved"], 1)
                    dve.wait_ge(S["any_key_moved"], r + 1)
                    hold(dve)
                dve.wait_ge(S["any_counts_read"], R + 1)
            dve.sem_inc(S["counts_final"], 1)

            def layer_norm(n):
                for nt in range(NT):
                    norm_stats(nt)
                for nt in range(NT):
                    norm_shift(n, nt)

            def read_sums(q, k):
                dve.wait_ge(S["agg_ready"], q * (KT + 1) + (k + 2))
                need(dve, S["mean_lo"], q * KT + k)
                dve.tensor_tensor(mean_f[:, k % 2, :], ps[:, 7 - k % 2, 0:N], inv[:, :], ALU.mult)\
                   .then_inc(S["agg_read"], 1)

            def read_counts(q, n):
                dve.wait_ge(S["agg_ready"], q * (KT + 1) + 1)
                dve.tensor_scalar(cnt[:, :], ps[:, 6, 0:N], 1.0, None, ALU.max).then_inc(S["agg_read"], 1)
                dve.wait_ge(S["agg_read"], q * (KT + 1) + 1)
                dve.reciprocal(inv[:, :], cnt[:, :]).then_inc(S["inv_made"], 1)
                dve.wait_ge(S["inv_made"], q + 1)

            def own_product(n, t0, q):
                for k in range(KT):
                    row_low(t0 + k + 2, (k + 2) % RING)
                    if k + 2 < KT:
                        turned_low((Y_H1, Y_H2, Y_MID)[n] + k + 2, h_t[1][:, k + 2, :], h_t[0][:, k + 2, :])
                read_counts(q, n)
                read_sums(q, 0)

            def relation(q, t0, last):
                for k in range(KT):
                    if not isinstance(t0, int) or t0 + k + 2 < T_END:
                        row_low(t0 + (k + 2), (k + 2) % RING)
                    if k < KT - 1:
                        read_sums(q, k + 1)
                if not last:
                    read_counts(q + 1, 0)
                    read_sums(q + 1, 0)

            def sum_of(n, t_last, nt):
                if nt < NT - 1:
                    dve.wait_ge(S["sum_ready"], (NT - 1) * n + nt + 1)
                else:
                    dve.wait_ge(S["w_used"], t_last + 1 + W_CREDIT)

            layer_norm(1)
            turned_low(Y_H1, h_t[1][:, 0, :], h_t[0][:, 0, :])
            turned_low(Y_H1 + 1, h_t[1][:, 1, :], h_t[0][:, 1, :])
            own_product(0, T_ROOT, 0)
            with dve.Fori(0, R - 1) as r:
                relation(r, T_REL + r * KT, False)
            relation(R - 1, T_REL + (R - 1) * KT, True)

            def add_bias(n, t_last, target, done):
                for nt in range(NT):
                    sum_of(n, t_last, nt)
                    for f in range(2):
                        half = slice(HALF * f, HALF * f + HALF)
                        ins = dve.tensor_tensor(target[:, nt, half], ps[:, 2 * nt + f, :], brow[:, half], ALU.add)
                        ins.then_inc(S[done], 1)

            dve.wait_ge(S["brow_in"], 16)
            add_bias(0, T_GX - 1, u, "u_ready")
            for k in range(KT):
                row_low(T_GX + k + 2, (k + 2) % RING)
                turned_low(Y_U + k, u_t[1][:, k, :], u_t[0][:, k, :])
                if k < NT:
                    link(dve.tensor_reduce(mask[:, k, :], counts16[:, :, :].rearrange(
                        "p (r t) n -> p t n r", t=NT)[:, k], AX.X, ALU.add))
                    dve.tensor_copy(total_r[:, k, :], mask[:, k, :]).then_inc(S["total_made"], 1)
            for k in range(KT):
                row_low(T_GU + k + 2, (k + 2) % RING)
            for nt in range(NT):
                sum_of(1, T_S0 - 1, nt)
                dve.wait_ge(S["gate_sum"], nt + 1)
                for f in range(2):
                    half = slice(HALF * f, HALF * f + HALF)
                    dve.tensor_tensor(h[:, nt, half], ps[:, 2 * nt + f, :], u[:, nt, half], ALU.mult)\
                       .then_inc(S["gate_product"], 1)
            for nt in range(NT):
                dve.wait_ge(S["x_gated"], nt + 1)
                norm_stats(nt)
            for nt in range(NT):
                norm_shift(2, nt)
            turned_low(Y_H2, h_t[1][:, 0, :], h_t[0][:, 0, :])
            turned_low(Y_H2 + 1, h_t[1][:, 1, :], h_t[0][:, 1, :])
            own_product(1, T_S0, R)
            relation(R, T_N0, True)
            dve.wait_ge(S["brow_in"], 16 * 3)
            add_bias(2, T_S1 - 1, h, "mid_ready")
            turned_low(Y_MID, h_t[1][:, 0, :], h_t[0][:, 0, :])
            turned_low(Y_MID + 1, h_t[1][:, 1, :], h_t[0][:, 1, :])
            own_product(2, T_S1, R + 1)
            dve.wait_ge(S["w3_hi"], 1)
            dve.tensor_tensor(w3[1][:, :, :], sparse_w[:, :, :], w3[0][:, :, :].bitcast(F32), ALU.subtract)\
               .then_inc(S["w3_lo"], 1)
            relation(R + 1, T_N1, True)
            dve.wait_ge(S["x_based"], NT)
            for nt in range(NT):
                sum_of(3, T_END - 1, nt)
                for f in range(2):
                    half = slice(HALF * f, HALF * f + HALF)
                    dve.tensor_tensor(xres[:, nt, half], xres[:, nt, half], ps[:, 2 * nt + f, :], ALU.add)\
                       .then_inc(S["x_done"], 1)
                dve.wait_ge(S["x_done"], 2 * nt + 2)
                norm_stats(nt)
            for nt in range(NT):
                norm_shift(3, nt)
            for f in range(NT):
                turned_low(Y_H3 + f, h_t[1][:, f, :], h_t[0][:, f, :])
            for nt in range(NT):
                dve.wait_ge(S["out_psum"], nt + 1)
                dve.wait_ge(S["out_based"], nt + 1)
                dve.tensor_tensor(u[:, nt, 0:N], u[:, nt, 0:N], ps[:, nt, 0:N], ALU.add).then_inc(S["out_done"], 1)

        @block.gpsimd
        def _(pool):
            link = Chain(pool, S["pool_chain"])
            pool.memset(ident[:, :], 0.0).then_inc(S["ident_made"], 1)
            pool.wait_ge(S["ident_made"], 1)
            pool.affine_select(out=ident[:, :], in_=ident[:, :], compare_op=ALU.not_equal, fill=1.0, base=0,
                               pattern=[[-1, P]], channel_multiplier=1).then_inc(S["ident_made"], 1)
            pool.iota(iota[:, :], pattern=[[1, N]], base=0, channel_multiplier=0).then_inc(S["iota_made"], 1)
            pool.memset(later[:, :], 1.0).then_inc(S["later_made"], 1)
            pool.wait_ge(S["later_made"], 1)
            pool.affine_select(out=later[:, :], in_=later[:, :], compare_op=ALU.is_gt, fill=0.0, base=0,
                               pattern=[[1, P]], channel_multiplier=-1).then_inc(S["later_made"], 1)
            pool.iota(chunk_exp[:, :], pattern=[[EXP_STEP, EC]], base=EXP_BASE + 127, channel_multiplier=0)\
                .then_inc(S["exp_made"], 1)

            pool.wait_ge(S["mask_decoded"], 2)
            types = key_row[:, 0, 0:NT * N]
            empty = key_i[:, 1, 0:NT * N].bitcast(F32)
            flat = mask[:, :, :].rearrange("p t n -> p (t n)")
            pool.wait_ge(S["sp_made"], 1)
            pool.wait_ge(S["check_ready"], 1)
            term = key_row[:, 1, 0:NT * N]
            link(pool.tensor_scalar(flat, types, 0.0, sp[:, 5, 3:4], ALU.is_equal, ALU.mult))
            for t in range(1, 5):
                link(pool.tensor_scalar(term, types, float(t), sp[:, 5, t - 1:t], ALU.is_equal, ALU.mult))
                link(pool.tensor_tensor(flat, flat, term, ALU.add))
            link(pool.tensor_scalar(empty, empty, 0.0, MASKED, ALU.is_equal, ALU.mult))
            link(pool.affine_select(out=empty.rearrange("p (t n) -> p t n", t=NT),
                                    in_=empty.rearrange("p (t n) -> p t n", t=NT),
                                    compare_op=ALU.not_equal, fill=0.0, base=0,
                                    pattern=[[-P, NT], [1, N]], channel_multiplier=-1))
            link(pool.tensor_tensor(flat, flat, empty, ALU.add))
            pool.tensor_scalar(flat, flat, 1.0 / SCALE, None, ALU.mult).then_inc(S["mask_made"], 1)

            pool.wait_ge(S["v_lo"], NT)
            pool.wait_ge(S["v_hi"], NT)
            for o in range(2):
                for a in range(2):
                    r0 = DH * (1 - o)
                    pool.memset(q_st[r0:r0 + DH, a, o, :].bitcast(F32), 0.0).then_inc(S["q_cleared"], 1)
                    pool.wait_ge(S["q_cleared"], 2 * o + a + 1)

            def normalise(i, o):
                for nt in range(NT - 1):
                    pool.wait_ge(S["sum_inverted"], (i * 4 + o) * NT + (nt + 1))
                    hold(pool)
                    pool.tensor_scalar(sc[:, o % 2, nt, :], sc[:, o % 2, nt, :], rinv[:, o % 2, nt:nt + 1],
                                       None, ALU.mult).then_inc(S["probs_by_pool"], 1)

            with pool.Fori(0, H // 4) as i:
                for o in range(4):
                    normalise(i, o)

            def row_parts(n):
                for nt in range(NT):
                    pool.wait_ge(S["row_hi"], NT * n + nt + 1)
                    pool.tensor_tensor(h_row[1][:, nt, :], h[:, nt, :], h_row[0][:, nt, :].bitcast(F32), ALU.subtract)\
                        .then_inc(S["row_lo"], 1)

            def mean_low(q, k):
                pool.wait_ge(S["mean_hi"], q * KT + (k + 1))
                pool.tensor_tensor(mean[1][:, k % 2, :], mean_f[:, k % 2, :], mean[0][:, k % 2, :].bitcast(F32),
                                   ALU.subtract).then_inc(S["mean_lo"], 1)

            row_parts(0)
            mean_low(0, 0)
            with pool.Fori(0, R - 1) as r:
                for k in range(KT):
                    mean_low(r, k + 1)
            for k in range(1, KT):
                mean_low(R - 1, k)
            pool.wait_ge(S["brow_in"], 16 * 2)
            for nt in range(NT):
                pool.wait_ge(S["u_tanh"], nt + 1)
                link(pool.tensor_tensor(u[:, nt, :], u[:, nt, :], h[:, nt, :], ALU.subtract))
                link(pool.tensor_tensor(xres[:, nt, :], xres[:, nt, :], h[:, nt, :], ALU.add))
                link(pool.tensor_tensor(h[:, nt, :], u[:, nt, :], brow[:, :], ALU.mult))
                pool.tensor_tensor(xres[:, nt, :], xres[:, nt, :], h[:, nt, :], ALU.add).then_inc(S["gate_sum"], 1)
            pool.wait_ge(S["gate_sum"], NT)
            for nt in range(NT):
                pool.wait_ge(S["gate_product"], 2 * nt + 2)
                pool.tensor_tensor(xres[:, nt, :], xres[:, nt, :], h[:, nt, :], ALU.add).then_inc(S["x_gated"], 1)
            row_parts(1)
            for k in range(KT):
                mean_low(R, k)
            row_parts(2)
            pool.wait_ge(S["brow_in"], 16 * 4)
            for nt in range(NT):
                pool.tensor_tensor(xres[:, nt, :], xres[:, nt, :], brow[:, :], ALU.add).then_inc(S["x_based"], 1)
            for k in range(KT):
                mean_low(R + 1, k)
            pool.wait_ge(S["brow_in"], 16 * 5)
            for nt in range(NT):
                pool.wait_ge(S["x_done"], 2 * nt + 2)
                pool.tensor_tensor(u[:, nt, :], xres[:, nt, :], brow[:, :], ALU.add).then_inc(S["out_based"], 1)


_INS = ["x", "src", "dst", "edge_type_5", "edge_type_8", "edge_weight", "L0_gnn_edge_type_weights",
        "L0_gnn_wq", "L0_gnn_bq", "L0_gnn_wk", "L0_gnn_bk", "L0_gnn_wv", "L0_gnn_bv", "L0_gnn_wiq",
        "L0_gnn_biq", "L0_gnn_wik", "L0_gnn_bik", "L0_gnn_wiv", "L0_gnn_biv", "L0_gnn_wo", "L0_gnn_bo",
        "L1_gnn_weight", "L1_gnn_root", "L1_gnn_bias", "L1_gnn_w_gate", "L1_gnn_b_gate",
        "L2_gnn_W_self0", "L2_gnn_W_neigh0", "L2_gnn_b0", "L2_gnn_W_self1", "L2_gnn_W_neigh1",
        "L2_gnn_b1", "L3_gnn_bias"]


def kernel(**inputs):
    import numpy as _np
    import concourse.bacc as _bacc
    from concourse import mybir as _mybir
    from concourse.bass_utils import run_bass_kernel_spmd as _run

    nc = _bacc.Bacc("TRN2", target_bir_lowering=False, num_devices=1)
    arrays, args = {}, []
    for name in _INS:
        a = _np.ascontiguousarray(inputs[name])
        arrays[f"in_{name}"] = a
        args.append(nc.dram_tensor(f"in_{name}", a.shape, _mybir.dt.from_np(a.dtype), kind="ExternalInput").ap())
    a = inputs["x"]
    args.append(nc.dram_tensor("out_0", a.shape, _mybir.dt.float32, kind="ExternalOutput").ap())
    build(nc, *args)
    r = _run(nc, [arrays], core_ids=[0])
    return r.results[0]["out_0"]
```

```python
from contextlib import ExitStack

import concourse.bass as bass
from concourse import mybir

ALU = mybir.AluOpType
ACT = mybir.ActivationFunctionType
AX = mybir.AxisListType
F32 = mybir.dt.float32
F32R = mybir.dt.float32r
BF16 = mybir.dt.bfloat16
I32 = mybir.dt.int32
I16 = mybir.dt.int16
U16 = mybir.dt.uint16

P = 128
RING = 4
EPS = 1e-5
MASKED = -1e30


def need(eng, sem, value):
    if not (isinstance(value, int) and value <= 0):
        eng.wait_ge(sem, value)


class Chain:

    def __init__(self, eng, sem):
        self.eng, self.sem, self.n = eng, sem, 0

    def __call__(self, instruction):
        self.n = self.n + 1
        instruction.then_inc(self.sem, 1)
        self.eng.wait_ge(self.sem, self.n)


def build(nc, x, src, dst, et5, et8, ew, etw, wq, bq, wk, bk, wv, bv, wiq, biq, wik, bik, wiv, biv,
          wo, bo, rel_w, root, bias1, w_gate, b_gate, w_self0, w_neigh0, b0, w_self1, w_neigh1, b1,
          bias3, out):
    N, D = x.shape
    E = src.shape[0]
    R = rel_w.shape[0]
    H = 16
    DH = D // H
    NT = N // P
    KT = D // P
    EC = E // P
    HALF = D // 2
    SCALE = float(DH) ** -0.5
    CELLS = R * NT
    DIGIT = 3
    EXP_STEP, EXP_BASE = 5, -120
    assert N == NT * P and D == KT * P and E == EC * P and DH == 64 and DIGIT * R <= 24
    assert EXP_BASE + EXP_STEP * EC <= 127

    ctx = ExitStack()
    with ctx:
        def sb(name, shape, dt, scope=ctx):
            return scope.enter_context(nc.sbuf_tensor(name, shape, dt))

        def sem(name):
            return ctx.enter_context(nc.semaphore(name))

        xres = sb("xres", [P, NT, D], F32)
        ident = sb("ident", [P, P], F32)
        ones_r = sb("ones_r", [P, P], F32R)
        counts16 = sb("counts16", [P, CELLS, N], U16)
        total_r = sb("total_r", [P, NT, N], F32R)
        sparse_w = sb("sparse_w", [P, NT, N], F32)
        mask = sb("mask", [P, NT, N], F32)
        iota = sb("iota", [P, N], I16)
        e_col = sb("e_col", [P, 7, EC], F32)
        digit_sum = sb("digit_sum", [P, R + 3], F32)
        no_digits = sb("no_digits", [P, 1], I32)
        brow = sb("brow", [P, D], F32)
        bcol = sb("bcol", [P, 7 * KT], F32)
        b_in = sb("b_in", [7 * KT, P], F32)
        stats = sb("stats", [P, NT, 2, 6], F32)
        mv = sb("mv", [P, NT, 2], F32)
        std = sb("std", [P, NT, 1], F32)
        rstd = sb("rstd", [P, NT, 1], F32)
        shift = sb("shift", [P, NT, 1], F32)
        epsc = sb("epsc", [P, 1], F32)
        raw = [sb(f"raw{i}", [P, D], F32) for i in range(RING)]
        whi = [sb(f"whi{i}", [P, KT, P], F32R) for i in range(RING)]
        wlo = [sb(f"wlo{i}", [P, KT, P], F32R) for i in range(RING)]
        whi_row = [w[:, :, :].rearrange("p k n -> p (k n)") for w in whi]
        wlo_row = [w[:, :, :].rearrange("p k n -> p (k n)") for w in wlo]

        graph_base = nc.sbuf_base
        with ExitStack() as scope:
            hot_src = sb("hot_src", [P, 4, N], BF16, scope)
            hot_rel = sb("hot_rel", [P, 4, N], BF16, scope)
            dst_r = sb("dst_r", [P, 2, N], F32R, scope)
            src_w = sb("src_w", [P, 2, 2, N], F32R, scope)
            e_in = sb("e_in", [EC, 4, P], I32, scope)
            e_w = sb("e_w", [EC, P], F32, scope)
            e_row = sb("e_row", [EC, 7, P], F32, scope)
            same = sb("same", [P, 2, P], F32, scope)
            rel_exp = sb("rel_exp", [P, 2, EC], I32, scope)
            w_hi = sb("w_hi", [P, EC], F32R, scope)
            w_lo = sb("w_lo", [P, EC], F32, scope)
            left_over = 2 * KT * N * 4 - (nc.sbuf_base - graph_base)
            assert left_over > 0
            sb("left_over", [P, left_over // 4], F32, scope)
            hot_dst = sb("hot_dst", [P, EC, N], BF16, scope)
            h0 = sb("h0", [P, NT, D], F32, scope)
            hot_val = sb("hot_val", [P, 3, N], BF16, scope)
            later = sb("later", [P, P], F32, scope)
            dup = sb("dup", [P, EC], F32, scope)
            live = sb("live", [P, EC], F32, scope)
            chunk_exp = sb("chunk_exp", [P, EC], I32, scope)
            chunk_val = sb("chunk_val", [P, EC], I32, scope)
            edge_val = sb("edge_val", [P, EC], F32, scope)
            etw_b = sb("etw_b", [P, 4], F32, scope)
            key_i = sb("key_i", [P, 2, E // 4], I32, scope)
            key_row = sb("key_row", [P, 2, E // 4], F32, scope)
            sp = sb("sp", [P, 6, 4], F32, scope)
            packed, codes = [key_i[:, i, 0:NT * N] for i in range(2)]
            digits = [key_row[:, i, 0:NT * N].bitcast(I32) for i in range(2)]

        with ExitStack() as scope:
            acts = sb("acts", [P, 4, 2, KT, N], F32R, scope)
        with ExitStack() as scope:
            sb("places_0_1", [P, 2, 2, KT, N], F32R, scope)
            pt = [sb(f"pt_{s}", [P, 2, NT, N], F32R, scope) for s in ("hi", "lo")]
            v_st = sb("v_st", [P, 2, 2, NT, P], F32R, scope)
            sb("place_3", [P, 2, KT, N], F32R, scope)
            q_st = sb("q_st", [P, 2, 2, N], F32R, scope)
            nmax = sb("nmax", [P, 2, NT], F32, scope)
            rsum = sb("rsum", [P, 2, NT], F32, scope)
            rinv = sb("rinv", [P, 2, NT], F32, scope)
        v_rows = acts[:, 3, :, :, :].rearrange("p s k n -> p s (k n)").rearrange(
            "p s (t d) -> p s t d", t=NT)
        sc = xres[:, :, :].rearrange("p t d -> p (t d)")[:, 0:2 * NT * N].rearrange(
            "p (b t n) -> p b t n", b=2, t=NT)
        y_t = brow[:, 0:2 * N].rearrange("p (b n) -> p b n", b=2)

        with ExitStack() as scope:
            h = sb("h", [P, NT, D], F32, scope)
            h_row = [sb(f"h_row_{s}", [P, NT, D], F32R, scope) for s in ("hi", "lo")]
            h_t = [sb(f"h_t_{s}", [P, KT, N], F32R, scope) for s in ("hi", "lo")]
            mean_f = sb("mean_f", [P, 2, N], F32, scope)
            mean = [sb(f"mean_{s}", [P, 2, N], F32R, scope) for s in ("hi", "lo")]
            rel_r = sb("rel_r", [P, NT, N], F32R, scope)
            cnt = sb("cnt", [P, N], F32, scope)
            inv = sb("inv", [P, N], F32, scope)
            u = sb("u", [P, NT, D], F32, scope)
            w3 = [sb(f"w3_{s}", [P, NT, N], F32R, scope) for s in ("hi", "lo")]
        with ExitStack() as scope:
            any_dst = sb("any_dst", [P, EC, N], BF16, scope)
            any_rel = sb("any_rel", [P, 4, N], BF16, scope)
        u_t = [a[:, :, :].rearrange("p t d -> p (t d)").rearrange("p (k n) -> p k n", k=KT)
               for a in h_row]

        ps = ctx.enter_context(nc.psum_tensor("ps", [P, 8, 512], F32))

        names = """x_in edges_in key_rows_in etw_in bcol_in brow_in out_stored
            iota_made ident_made later_made exp_made ones_made
            edge_rows edges_turned edge_cols keys_made hots_made hot_parts_made hot_dst_even_made
            hots_used packed_made digits_made digits_kept check_ready check_summed check_made counts_final
            any_dst_made any_rel_made any_rel_used any_counts_read any_key_moved
            hot_val_made hot_val_used mask_decoded sparse_kept sp_max sp_exp sp_ln mask_made total_made
            half_stats_made var_ready std_ready shift_ready h_ready
            turned turn_hi turn_lo
            weight_turned w_hi w_lo w_used out_hi out_lo
            v_turned v_hi v_lo
            q_cleared scores_ready scores_read exp_ready sum_inverted
            probs_by_pool probs_by_vec probs_turned pt_hi pt_lo pv_done head_hi head_lo
            y_evacuated y_turned y_added
            row_hi row_lo rel_ready agg_ready agg_read mean_hi mean_lo
            u_ready u_tanh gate_sum gate_product x_gated x_gated_last
            mid_ready x_based x_done w3_hi w3_lo out_based out_psum out_done
            vec_chain pool_chain sum_ready inv_made sp_made dup_found held_vec held_pool""".split()
        S = {n: sem(n) for n in names}
        raw_in = [sem(f"raw_in{i}") for i in range(RING)]
        q_staged = [sem(f"q_staged_{s}") for s in ("even", "odd")]
        v_staged = [sem(f"v_staged_{s}") for s in ("even", "odd")]

        T_WO = 6 * KT
        T_ROOT = 7 * KT
        T_REL = T_ROOT + KT
        T_GX = T_REL + R * KT
        T_GU = T_GX + KT
        T_S0 = T_GU + KT
        T_N0 = T_S0 + KT
        T_S1 = T_N0 + KT
        T_N1 = T_S1 + KT
        T_END = T_N1 + KT
        W_CREDIT = RING
        O_CREDIT = 2
        HOT_CREDIT = 4
        VAL_CREDIT = 3
        PV_CREDIT = 3
        M_CREDIT = 2
        Y_H0, Y_H1 = 0, KT
        Y_U, Y_H2 = 2 * KT, 3 * KT
        Y_MID, Y_H3 = 4 * KT, 5 * KT
        H_FIRST = (3, 7, 13, 21, 25)
        H_ALL = (4, 10, 16, 22, 25)
        SEGMENTS = [(0, 4, None, 0, None), (4, 8, None, 0, None), (8, 12, None, 0, 0), (12, 20, 0, 6, 1),
                    (20, 28, 1, 6, 2), (28, 36, 2, 6, 3), (36, EC, 3, 4, None)]
        SRC, DST, KEY, REL_KEY, TYPE, REL, WEIGHT = range(7)
        QUARTER = EC // 4

        def use_of_slot(g, j):
            return (g * (KT // RING) + (j // RING + 1)) * 16

        def hold(eng):
            eng.sem_inc(S["held_vec"] if eng is nc.vector else S["held_pool"], 1)

        def exists(i, o):
            return not isinstance(i, int) or i * 4 + o < H

        def is_head(i, o, n):
            return isinstance(i, int) and i * 4 + o == n

        block = ctx.enter_context(nc.Block())

        @block.sync
        def _(sp_):
            sp_.dma_start(e_in[:, 0, :], src.rearrange("(c p) -> c p", p=P)).then_inc(S["edges_in"], 16)
            sp_.dma_start(e_in[:, 1, :], dst.rearrange("(c p) -> c p", p=P)).then_inc(S["edges_in"], 16)
            sp_.dma_start(e_in[:, 2, :], et5.rearrange("(c p) -> c p", p=P)).then_inc(S["edges_in"], 16)
            sp_.dma_start(e_in[:, 3, :], et8.rearrange("(c p) -> c p", p=P)).then_inc(S["edges_in"], 16)
            sp_.dma_start(e_w[:, :], ew.rearrange("(c p) -> c p", p=P)).then_inc(S["edges_in"], 16)
            sp_.dma_start(xres[:, :, :], x.rearrange("(t p) d -> p t d", p=P)).then_inc(S["x_in"], 16)

            def load(t0, rows_of, n):
                def four(i4):
                    for s in range(RING):
                        t = t0 + i4 + s
                        if t0 >= T_ROOT + RING:
                            sp_.wait_ge(S["w_lo"], t - RING + 1)
                        elif t0 >= RING:
                            sp_.wait_ge(S["weight_turned"], t - RING + 1)
                        sp_.dma_start(raw[s][:, :], rows_of(i4 + s)).then_inc(raw_in[s], 16)
                if n == 1:
                    four(0)
                else:
                    with sp_.Fori(0, n) as i:
                        four(i * RING)

            def rows(w):
                return lambda i: w[bass.ds(i * P, P), :]

            load(0, rows(wq), 1)
            load(RING, lambda i: wq[bass.ds((i + RING) * P, P), :], 1)
            for g, w in enumerate((wk, wv, wiq, wik, wiv)):
                load((g + 1) * KT, rows(w), KT // RING)
            load(T_WO, rows(wo), 1)

            def stage_q(i, o):
                r0 = DH * (o % 2)
                need(sp_, S["scores_ready"], (i * 4 + (o - 1)) * NT)
                sp_.dma_start(q_st[r0:r0 + DH, :, o % 2, :].bitcast(F32),
                              acts[r0:r0 + DH, 0, :, i * 2 + o // 2, :].bitcast(F32))\
                   .then_inc(q_staged[o % 2], 16)

            def stage_v(i, o):
                sp_.wait_ge(S["pv_done"], i * 4 + (2 * o - 3 + 1 + PV_CREDIT))
                sp_.dma_start(v_st[:, o % 2, :, :, :].bitcast(F32),
                              v_rows[:, :, :, bass.ds((i * 2 + o) * P, P)].bitcast(F32))\
                   .then_inc(v_staged[o % 2], 16)

            sp_.wait_ge(S["q_cleared"], 4)
            sp_.wait_ge(S["out_lo"], O_CREDIT + 4 * KT)
            stage_q(0, 0)
            stage_q(0, 1)
            sp_.wait_ge(S["v_hi"], NT)
            sp_.wait_ge(S["v_lo"], NT)
            with sp_.Fori(0, 3) as i:
                for o in range(2, 6):
                    stage_q(i, o)
                    if o % 2 == 0:
                        stage_v(i, o // 2 - 1)
            for o in range(2, 4):
                stage_q(3, o)
                stage_v(3, o - 2)
            load(T_WO + RING, lambda i: wo[bass.ds((i + RING) * P, P), :], 1)
            load(T_ROOT, rows(root), 1)
            load(T_ROOT + RING, lambda i: root[bass.ds((i + RING) * P, P), :], 1)
            load(T_REL, rows(rel_w.rearrange("r k n -> (r k) n")), R * KT // RING)
            load(T_GX, lambda i: w_gate[bass.ds(i * P + D, P), :], KT // RING)
            load(T_GU, rows(w_gate), KT // RING)
            for t0, w in ((T_S0, w_self0), (T_N0, w_neigh0), (T_S1, w_self1), (T_N1, w_neigh1)):
                load(t0, rows(w), KT // RING)
            for nt in range(NT):
                sp_.wait_ge(S["out_based"], nt + 1)
                sp_.dma_start(out.rearrange("(t p) d -> p t d", p=P)[:, nt, N:D],
                              u[:, nt, N:D]).then_inc(S["out_stored"], 16)
            for nt in range(NT):
                sp_.wait_ge(S["out_done"], nt + 1)
                sp_.dma_start(out.rearrange("(t p) d -> p t d", p=P)[:, nt, 0:N],
                              u[:, nt, 0:N]).then_inc(S["out_stored"], 16)
            sp_.wait_ge(S["out_stored"], 16 * 2 * NT)

        @block.tensor
        def _(pe):
            pe.wait_ge(S["ident_made"], 2)
            pe.wait_ge(S["edge_rows"], 1)
            for f in range(7):
                mm = pe.transpose(ps[:, 0, EC * f:EC * f + EC], e_row[:, f, :], ident[0:EC, 0:EC])
            mm.then_inc(S["edges_turned"], 1)
            pe.wait_ge(S["edge_cols"], 1)

            def count_chunks(c0, half0, first, last):
                for j in range(4):
                    c = c0 + j
                    pe.wait_ge(S["hots_made"], c + 1)
                    for s in range(NT):
                        pe.matmul(ps[:, s, 0:N], hot_src[:, j, P * s:P * s + P], hot_rel[:, j, :],
                                  start=first and j == 0, stop=last and j == 3)
                    pe.wait_ge(S["hot_parts_made"], c + 1)
                    if j % 2 == 0:
                        pe.wait_ge(S["hot_dst_even_made"], half0 + (j // 2 + 1))
                    for s in range(NT):
                        for w in range(2):
                            mm = pe.matmul(ps[:, NT + s, 0:N], dst_r[:, j % 2, P * s:P * s + P],
                                           src_w[:, j % 2, w, :], start=first and j == 0 and w == 0,
                                           stop=last and j == 3 and w == 1)
                    mm.then_inc(S["hots_used"], 1)

            count_chunks(0, 0, True, False)
            with pe.Fori(1, EC // 4 - 1) as c4:
                count_chunks(c4 * 4, c4 * 2, False, False)
            count_chunks(EC - 4, EC // 2 - 2, False, True)
            pe.wait_ge(S["bcol_in"], 16 * 7)
            pe.transpose(ps[:, 7, 0:7 * KT], b_in[:, :], ident[0:7 * KT, 0:7 * KT]).then_inc(S["edges_turned"], 1)

            def turn(y, source, f):
                need(pe, S["turn_lo"], y - 1)
                for nt in range(NT):
                    mm = pe.transpose(ps[:, 6 + y % 2, P * nt:P * nt + P],
                                      source[:, nt, P * f:P * f + P], ident[:, :])
                mm.then_inc(S["turned"], 1)

            def turn_weight(g, j):
                pe.wait_ge(raw_in[j % RING], use_of_slot(g, j))
                need(pe, S["w_lo"], g * KT + (j - 1))
                for k in range(KT):
                    mm = pe.transpose(ps[:, 4 - 2 * (j % 2) + k // 4, P * (k % 4):P * (k % 4) + P],
                                      raw[j % RING][:, P * k:P * k + P], ident[:, :])
                mm.then_inc(S["weight_turned"], 1)

            def column_tile(g, j, a):
                pe.wait_ge(S["w_lo"], g * KT + (j + 1))
                i = 0
                for k in range(KT):
                    for stationary, moving in ((whi, 0), (whi, 1), (wlo, 0)):
                        mm = pe.matmul(ps[:, j % 2, 0:N], stationary[j % RING][:, k, :],
                                       acts[:, a, moving, k, :], start=i == 0, stop=i == 3 * KT - 1)
                        i += 1
                mm.then_inc(S["w_used"], 1)

            def mask_chunks(c0, first, last):
                for j in range(3):
                    c = c0 + j
                    pe.wait_ge(S["hot_val_made"], c + 1)
                    for s in range(NT):
                        mm = pe.matmul(ps[:, s, 0:N], hot_val[:, j, P * s:P * s + P], hot_dst[:, c, :],
                                       start=first and j == 0, stop=last and j == 2)
                    mm.then_inc(S["hot_val_used"], 1)

            pe.wait_ge(S["packed_made"], 1)
            pe.wait_ge(S["edge_cols"], 2)
            for r in range(KT):
                first, end = r * EC // KT, (r + 1) * EC // KT
                if r == KT - 1:
                    pe.wait_ge(S["sparse_kept"], 1)
                    turn_weight(0, 0)
                for c in range(first, end, 3):
                    mask_chunks(c, c == 0, c == EC - 3)
                if r == 0:
                    pe.wait_ge(S["h_ready"], H_ALL[0])
                turn(Y_H0 + r, h0, r)

            pe.wait_ge(S["mask_decoded"], 1)
            turn_weight(0, 1)
            pe.wait_ge(S["turn_lo"], Y_H0 + KT)

            def eight_tiles(g, a):
                for j in range(KT):
                    turn_weight(g, j + 2)
                    pe.wait_ge(S["out_lo"], g * KT + (j - 1 + O_CREDIT))
                    column_tile(g, j, a)

            with pe.Fori(0, 3) as g:
                eight_tiles(g, 0)
            pe.wait_ge(S["check_ready"], 1)
            pe.wait_ge(S["ones_made"], 3)
            pe.matmul(ps[:, 7, 0:1], ones_r[:, :].bitcast(F32), digit_sum[:, R + 2:R + 3], start=True, stop=True)\
              .then_inc(S["check_summed"], 1)
            with pe.Fori(3, 6) as g:
                eight_tiles(g, g - 2)

            def turn_v(m):
                for s in range(2):
                    need(pe, (S["v_hi"], S["v_lo"])[s], m)
                    for f in range(KT):
                        mm = pe.transpose(ps[:, 4 + 2 * s + f // 4, P * (f % 4):P * (f % 4) + P],
                                          acts[:, 2, s, f, P * m:P * m + P].bitcast(F32), ident[:, :])
                    mm.then_inc(S["v_turned"], 1)

            def scores(i, o):
                pe.wait_ge(q_staged[o % 2], i * 32 + 16 * (o // 2 + 1))
                for nt in range(NT):
                    need(pe, S["scores_read"], (i * 4 + (o - 1)) * NT + (nt + 1))
                    for n, (a, c) in enumerate(((0, 0), (0, 1), (1, 0))):
                        mm = pe.matmul(ps[:, nt, 0:N], q_st[:, a, o % 2, P * nt:P * nt + P],
                                       acts[:, 1, c, i * 2 + o // 2, :], start=n == 0, stop=n == 2)
                    mm.then_inc(S["scores_ready"], 1)

            def turn_probs(i, o):
                pe.wait_ge(S["probs_by_pool"], (i * 4 + (o + 1)) * (NT - 1))
                pe.wait_ge(S["probs_by_vec"], i * 4 + (o + 1))
                for m in range(NT):
                    need(pe, S["pt_lo"], (i * 4 + (o - 1)) * NT + (m + 1))
                    for nt in range(NT):
                        mm = pe.transpose(ps[:, NT + m, P * nt:P * nt + P],
                                          sc[:, o % 2, nt, P * m:P * m + P], ident[:, :])
                    mm.then_inc(S["probs_turned"], 1)

            def weigh_values(i, o):
                pe.wait_ge(S["pt_lo"], (i * 4 + (o + 1)) * NT)
                if o % 2 == 0:
                    pe.wait_ge(v_staged[o // 2 % 2], i * 16 + 16 * (o // 2 // 2 + 1))
                pe.wait_ge(S["head_lo"], i * 4 + (o - 1 + O_CREDIT))
                n = 0
                for m in range(NT):
                    for a, c in ((0, 0), (0, 1), (1, 0)):
                        mm = pe.matmul(ps[:, 6 + o % 2, 0:N], v_st[:, o // 2 % 2, a, m, :],
                                       pt[c][:, o % 2, m, :], start=n == 0, stop=n == 3 * NT - 1)
                        n += 1
                mm.then_inc(S["pv_done"], 1)

            def head(i, o):
                turn_probs(i, o)
                if exists(i, o + 2):
                    scores(i, o + 2)
                if not is_head(i, o, 0):
                    weigh_values(i, o - 1)

            pe.wait_ge(S["out_lo"], O_CREDIT + 6 * KT)
            pe.wait_ge(S["w_lo"], T_WO + 2)
            scores(0, 0)
            for m in range(NT):
                turn_v(m)
            scores(0, 1)
            pe.wait_ge(S["v_hi"], NT)
            pe.wait_ge(S["v_lo"], NT)
            head(0, 0)
            with pe.Fori(0, 3) as i:
                for o in range(1, 5):
                    head(i, o)
            for o in range(1, 4):
                head(3, o)
            weigh_values(3, 3)

            pe.wait_ge(S["head_lo"], O_CREDIT + H)
            pe.wait_ge(S["scores_read"], H * NT)

            def turn_y(j):
                pe.wait_ge(S["y_evacuated"], j + 1)
                need(pe, S["y_added"], j - 1)
                for nt in range(NT):
                    mm = pe.transpose(ps[:, 6 + j % 2, P * nt:P * nt + P],
                                      y_t[:, j % 2, P * nt:P * nt + P], ident[:, :])
                mm.then_inc(S["y_turned"], 1)

            for j in range(KT):
                if j + 2 < KT:
                    turn_weight(6, j + 2)
                need(pe, S["y_evacuated"], j - 1)
                column_tile(6, j, 0)
                if j:
                    turn_y(j - 1)
            turn_y(KT - 1)

            def any_chunks(r, c0, first, last):
                for j in range(4):
                    c = c0 + j
                    pe.wait_ge(S["any_rel_made"], r * EC + (c + 1))
                    for s in range(NT):
                        mm = pe.matmul(ps[:, s, 0:N], any_rel[:, j, P * s:P * s + P], any_dst[:, c, :],
                                       start=first and j == 0, stop=last and j == 3)
                    mm.then_inc(S["any_rel_used"], 1)

            pe.wait_ge(S["check_made"], 1)
            with pe.If(pe.value_load(no_digits[0:1, 0:1], min_val=0, max_val=1) > 0):
                pe.wait_ge(S["any_dst_made"], EC)
                with pe.Fori(0, R) as r:
                    pe.wait_ge(S["any_counts_read"], r + 1)
                    any_chunks(r, 0, True, False)
                    with pe.Fori(1, EC // 4 - 1) as c4:
                        any_chunks(r, c4 * 4, False, False)
                    any_chunks(r, EC - 4, False, True)

            def row_tile(t, slot, stationary, k, nt, first=False, last=False):
                for a, weight in ((0, whi_row), (0, wlo_row), (1, whi_row)):
                    for f in range(2):
                        mm = pe.matmul(ps[:, 2 * nt + f, :], stationary[a][:, k, P * nt:P * nt + P],
                                       weight[slot][:, HALF * f:HALF * f + HALF],
                                       start=first and a == 0 and weight is whi_row,
                                       stop=last and a == 1, skip_group_check=True)
                return mm

            def row_block(t, slot, stationary, k, first=False, bank_free=None):
                pe.wait_ge(S["w_lo"], t + 1)
                for nt in range(NT):
                    if bank_free:
                        bank_free(nt)
                    mm = row_tile(t, slot, stationary, k, nt, first)
                mm.then_inc(S["w_used"], 1)

            def last_two_blocks(t, one, two, two_ready):
                pe.wait_ge(S["w_lo"], t + 2)
                row_tile(t, (KT - 2) % RING, *one, 0)
                row_tile(t, (KT - 2) % RING, *one, 1)
                two_ready()
                for nt in range(NT):
                    if nt == NT - 1:
                        mm = row_tile(t, (KT - 2) % RING, *one, nt)
                        mm.then_inc(S["w_used"], 1)
                    mm = row_tile(t + 1, (KT - 1) % RING, *two, nt, last=True)
                    mm.then_inc(S["sum_ready" if nt < NT - 1 else "w_used"], 1)

            def start_relation(q, edges, a6):
                a6()
                for s in range(NT):
                    mm = pe.matmul(ps[:, 6, 0:N], ones_r[:, :], edges[:, s, :], start=s == 0, stop=s == NT - 1)
                mm.then_inc(S["agg_ready"], 1)
                sum_edges(q, edges, 0)

            def sum_edges(q, edges, k):
                if k:
                    pe.wait_ge(S["agg_read"], q * (KT + 1) + k)
                i = 0
                for s in range(NT):
                    for a in range(2):
                        mm = pe.matmul(ps[:, 7 - k % 2, 0:N], h_row[a][:, s, P * k:P * k + P],
                                       edges[:, s, :], start=i == 0, stop=i == 2 * NT - 1)
                        i += 1
                mm.then_inc(S["agg_ready"], 1)

            def aggregated(q, k):
                pe.wait_ge(S["mean_hi"], q * KT + (k + 1))
                pe.wait_ge(S["mean_lo"], q * KT + (k + 2))

            def own_product(t0, y0, source, q, edges, first_free=None):
                for k in range(KT):
                    if k == 2:
                        pe.wait_ge(S["h_ready"], H_ALL[max(q - R + 1, 0) + 1])
                    if k == KT - 1:
                        pe.wait_ge(S["row_lo"], (q - R + 1) * NT + NT if q >= R else NT)
                        if q == 0:
                            pe.wait_ge(S["rel_ready"], 1)
                        start_relation(q, edges, lambda: pe.wait_ge(S["turn_lo"], y0 + KT))
                    pe.wait_ge(S["turn_lo"], y0 + k + 1)
                    row_block(t0 + k, k % RING, h_t, k, first=k == 0,
                              bank_free=first_free if k == 0 else None)
                    if k + 2 < KT:
                        turn(y0 + k + 2, source, k + 2)

            def relation(q, t0, edges, last):
                for k in range(KT):
                    if k < KT - 1:
                        sum_edges(q, edges, k + 1)
                    elif not last:
                        pe.wait_ge(S["rel_ready"], q + 2)
                        start_relation(q + 1, edges, lambda: pe.wait_ge(S["agg_read"], (q + 1) * (KT + 1)))
                    if not last or k < KT - 1:
                        aggregated(q, k)
                    if not last or k < KT - 2:
                        row_block(t0 + k, k % RING, [m_pair(k, a) for a in range(2)], 0)
                if last:
                    last_two_blocks(t0 + KT - 2, *[([m_pair(k, a) for a in range(2)], 0)
                                                   for k in (KT - 2, KT - 1)],
                                    lambda: aggregated(q, KT - 1))

            def m_pair(k, a):
                return mean[a][:, k % 2:k % 2 + 1, :]

            def begin(q):
                y0 = (Y_H1, Y_H2, Y_MID)[q]
                pe.wait_ge(S["h_ready"], H_FIRST[q + 1])
                if q == 0:
                    pe.wait_ge(S["y_added"], KT)
                else:
                    pe.wait_ge(S["agg_read"], (KT + 1) * (R + q - 1))
                turn(y0, h, 0)
                turn(y0 + 1, h, 1)
                return y0

            y0 = begin(0)
            own_product(T_ROOT, y0, h, 0, rel_r)
            with pe.Fori(0, R - 1) as r:
                relation(r, T_REL + r * KT, rel_r, False)
            relation(R - 1, T_REL + (R - 1) * KT, rel_r, True)

            pe.wait_ge(S["agg_read"], R * (KT + 1))
            for k in range(KT):
                row_block(T_GX + k, k % RING, h_t, k, first=k == 0,
                          bank_free=(lambda nt: pe.wait_ge(S["u_ready"], 2 * nt + 2)) if k == 0 else None)
                turn(Y_U + k, u, k)
            for k in range(KT):
                pe.wait_ge(S["turn_lo"], Y_U + k + 1)
                if k < KT - 2:
                    row_block(T_GU + k, k % RING, u_t, k)
            last_two_blocks(T_GU + KT - 2, (u_t, KT - 2), (u_t, KT - 1), lambda: None)

            y0 = begin(1)
            pe.wait_ge(S["total_made"], NT)
            own_product(T_S0, y0, h, R, total_r)
            relation(R, T_N0, total_r, True)
            y0 = begin(2)
            own_product(T_S1, y0, h, R + 1, total_r)
            relation(R + 1, T_N1, total_r, True)

            pe.wait_ge(S["h_ready"], H_ALL[4])
            pe.wait_ge(S["agg_read"], (KT + 1) * (R + 2))
            for f in range(NT):
                turn(Y_H3 + f, h, f)
            pe.wait_ge(S["turn_lo"], Y_H3 + NT)
            pe.wait_ge(S["w3_lo"], 1)
            for nt in range(NT):
                i = 0
                for k in range(NT):
                    for a, w in ((0, 0), (0, 1), (1, 0)):
                        mm = pe.matmul(ps[:, nt, 0:N], h_t[a][:, k, P * nt:P * nt + P], w3[w][:, k, :],
                                       start=i == 0, stop=i == 3 * NT - 1)
                        i += 1
                mm.then_inc(S["out_psum"], 1)

        @block.scalar
        def _(act):
            act.wait_ge(S["ones_made"], 2)
            act.activation(ones_r[:, :], same[:, 0, :], ACT.Copy).then_inc(S["ones_made"], 1)
            act.wait_ge(S["edges_in"], 16 * 5)
            def key_rows(q):
                act.dma_start(key_i[:, 0, :], src[q * (E // 4):(q + 1) * (E // 4)].partition_broadcast(P))\
                   .then_inc(S["key_rows_in"], 16)
                act.dma_start(key_i[:, 1, :], dst[q * (E // 4):(q + 1) * (E // 4)].partition_broadcast(P))\
                   .then_inc(S["key_rows_in"], 16)

            key_rows(0)
            act.dma_start(etw_b[:, :], etw.partition_broadcast(P)).then_inc(S["etw_in"], 16)
            for g, b in enumerate((bq, bk, bv, biq, bik, biv, bo)):
                act.dma_start(b_in[KT * g:KT * g + KT, :], b.rearrange("(j p) -> j p", p=P)).then_inc(S["bcol_in"], 16)

            def norm_std(n, nt):
                act.wait_ge(S["var_ready"], NT * n + nt + 1)
                act.activation(std[:, nt, :], mv[:, nt, 1:2], ACT.Sqrt, bias=epsc[:, 0:1]).then_inc(S["std_ready"], 1)

            def norm_relu(n, nt, target, parts):
                act.wait_ge(S["shift_ready"], NT * n + nt + 1)
                for part in parts:
                    act.activation(target[:, nt, part], xres[:, nt, part], ACT.Relu, bias=shift[:, nt, :],
                                   scale=rstd[:, nt, :]).then_inc(S["h_ready"], 1)

            def turned_high(y, target):
                act.wait_ge(S["turned"], y + 1)
                act.activation(target, ps[:, 6 + y % 2, 0:N], ACT.Copy).then_inc(S["turn_hi"], 1)

            def layer_norm(n, target, parts, y0=None):
                norm_std(n, 0)
                norm_relu(n, 0, target, parts[:1])
                norm_std(n, 1)
                norm_std(n, 2)
                for nt in range(1, NT):
                    norm_relu(n, nt, target, parts[:1])
                if len(parts) > 1:
                    norm_relu(n, 0, target, parts[1:])
                    turned_high(y0, h_t[0][:, 0, :])
                    norm_relu(n, 1, target, parts[1:])
                    turned_high(y0 + 1, h_t[0][:, 1, :])
                    norm_relu(n, 2, target, parts[1:])

            HALVES = [slice(0, HALF), slice(HALF, D)]

            def sparse_parts(c4):
                for j in range(4):
                    c = c4 * 4 + j
                    act.wait_ge(S["hots_made"], c + 1)
                    act.wait_ge(S["hots_used"], c + (HOT_CREDIT - 1))
                    if j % 2:
                        act.activation(dst_r[:, 1, :], hot_dst[:, c, :], ACT.Copy)
                    act.activation(src_w[:, j % 2, 0, :], hot_src[:, j, :], ACT.Copy,
                                   scale=w_hi[:, bass.ds(c, 1)].bitcast(F32))
                    act.activation(src_w[:, j % 2, 1, :], hot_src[:, j, :], ACT.Copy, scale=w_lo[:, bass.ds(c, 1)])\
                       .then_inc(S["hot_parts_made"], 1)

            for seg, (c_first, c_end, _, _, keys) in enumerate(SEGMENTS):
                if c_end - c_first == 4:
                    sparse_parts(c_first // 4)
                else:
                    with act.Fori(c_first // 4, c_end // 4) as c4:
                        sparse_parts(c4)
                if keys in (0, 1, 2):
                    act.wait_ge(S["keys_made"], keys + 1)
                    key_rows(keys + 1)
                if keys == 3:
                    act.wait_ge(S["sp_max"], 1)
                    act.activation(sp[:, 3, :], sp[:, 2, :], ACT.Exp, scale=-1.0).then_inc(S["sp_exp"], 1)
                    act.wait_ge(S["sp_exp"], 1)
                    act.activation(sp[:, 4, :], sp[:, 3, :], ACT.Ln, bias=1.0).then_inc(S["sp_ln"], 1)
                    for nt in range(NT):
                        norm_std(0, nt)
            norm_relu(0, 0, h0, [slice(0, D)])
            act.wait_ge(S["hots_used"], EC + HOT_CREDIT)
            act.activation(sparse_w[:, :, :], ps[:, NT:2 * NT, 0:N], ACT.Copy).then_inc(S["sparse_kept"], 1)
            norm_relu(0, 1, h0, [slice(0, D)])
            norm_relu(0, 2, h0, [slice(0, HALF), slice(HALF, D)])

            def column_high(g, j):
                act.wait_ge(S["weight_turned"], g * KT + (j + 1))
                act.wait_ge(S["w_used"], g * KT + (j + 1))
                b = 4 - 2 * (j % 2)
                act.activation(whi[j % RING][:, :, :],
                               ps[:, b:b + 2, :].rearrange("p b (k n) -> p (b k) n", n=P), ACT.Copy)\
                   .then_inc(S["w_hi"], 1)

            def row_high(t, slot, use):
                act.wait_ge(raw_in[slot], use)
                act.wait_ge(S["w_used"], t + 1)
                act.activation(whi_row[slot], raw[slot][:, :], ACT.Copy).then_inc(S["w_hi"], 1)

            def row_high_at(t):
                row_high(t, t % RING, 16 * (t // RING + 1))

            for r in range(R):
                act.wait_ge(S["digits_made"], r + 1)
                act.activation(counts16[:, NT * r:NT * r + NT, :].rearrange("p t n -> p (t n)"), digits[r % 2],
                               ACT.Copy, accum_out=digit_sum[:, r:r + 1]).then_inc(S["digits_kept"], 1)
                turned_high(Y_H0 + r, acts[:, 0, 0, r, :])
            column_high(0, 0)
            column_high(0, 1)

            def eight_tiles(g, a):
                for j in range(KT):
                    column_high(g, j + 2)
                    act.wait_ge(S["w_used"], g * KT + (j + 1 + W_CREDIT))
                    act.activation(acts[:, a, 0, j, :], ps[:, j % 2, 0:N], ACT.Identity,
                                   bias=bcol[:, bass.ds(g * KT + j, 1)]).then_inc(S["out_hi"], 1)

            with act.Fori(0, 3) as g:
                act.wait_ge(S["mask_made"], g // 2 + 1)
                eight_tiles(g, g + 1)
            with act.Fori(3, 6) as g:
                eight_tiles(g, g - 3)

            def exps(i, o):
                for nt in range(NT):
                    act.wait_ge(S["scores_read"], (i * 4 + o) * NT + (nt + 1))
                    act.activation(sc[:, o % 2, nt, :], sc[:, o % 2, nt, :], ACT.Exp, scale=-1.0,
                                   bias=nmax[:, o % 2, nt:nt + 1],
                                   accum_out=rsum[:, o % 2, nt:nt + 1]).then_inc(S["exp_ready"], 1)

            def head(i, o):
                for m in range(NT):
                    act.wait_ge(S["probs_turned"], (i * 4 + o) * NT + (m + 1))
                    act.wait_ge(S["pv_done"], i * 4 + (o - 1 + PV_CREDIT))
                    act.activation(pt[0][:, o % 2, m, :], ps[:, NT + m, 0:N], ACT.Copy).then_inc(S["pt_hi"], 1)
                if exists(i, o + 2):
                    exps(i, o + 2)
                if not is_head(i, o, 0):
                    head_out(i, o - 1)

            def head_out(i, o):
                r = DH * (o % 2)
                act.wait_ge(S["pv_done"], i * 4 + (o + 1 + PV_CREDIT))
                act.activation(acts[r:r + DH, 0, 0, i * 2 + o // 2, :], ps[r:r + DH, 6 + o % 2, 0:N], ACT.Copy)\
                   .then_inc(S["head_hi"], 1)

            exps(0, 0)
            for m in range(NT):
                act.wait_ge(S["v_turned"], 2 * m + 1)
                act.activation(v_rows[:, 0, m, :], ps[:, 4:6, :].rearrange("p b n -> p (b n)"), ACT.Copy)\
                   .then_inc(S["v_hi"], 1)
            exps(0, 1)
            head(0, 0)
            with act.Fori(0, 3) as i:
                for o in range(1, 5):
                    head(i, o)
            for o in range(1, 4):
                head(3, o)
            act.wait_ge(S["probs_turned"], H * NT)
            act.dma_start(xres[:, :, :], x.rearrange("(t p) d -> p t d", p=P)).then_inc(S["x_in"], 16)
            head_out(3, 3)

            for j in range(KT):
                if j + 2 < KT:
                    column_high(6, j + 2)
                else:
                    row_high_at(T_WO + j + 2)
                act.wait_ge(S["w_used"], T_WO + j + 1 + W_CREDIT)
                need(act, S["y_turned"], j - 1)
                act.activation(y_t[:, j % 2, :], ps[:, j % 2, 0:N], ACT.Identity,
                               bias=bcol[:, T_WO + j:T_WO + j + 1]).then_inc(S["y_evacuated"], 1)

            def bias_row(b, last_use, count):
                act.wait_ge(S[last_use], count)
                act.dma_start(brow[:, :], b.partition_broadcast(P)).then_inc(S["brow_in"], 16)

            def row_parts(n):
                for nt in range(NT):
                    act.wait_ge(S["h_ready"], H_ALL[n + 1])
                    if n == 1:
                        act.wait_ge(S["w_used"], T_S0 + W_CREDIT)
                    if n == 2:
                        act.wait_ge(S["agg_ready"], (KT + 1) * (R + 1))
                    act.activation(h_row[0][:, nt, :], h[:, nt, :], ACT.Copy).then_inc(S["row_hi"], 1)

            def mean_high(q, k):
                act.wait_ge(S["agg_read"], q * (KT + 1) + (k + 2))
                act.activation(mean[0][:, k % 2, :], mean_f[:, k % 2, :], ACT.Copy).then_inc(S["mean_hi"], 1)

            def relation_edges(r):
                act.wait_ge(S["counts_final"], 1)
                need(act, S["agg_ready"], r * (KT + 1))
                act.activation(rel_r[:, :, :], counts16[:, bass.ds(r * NT, NT), :], ACT.Copy)\
                   .then_inc(S["rel_ready"], 1)

            def own_product(n, t0, q):
                for k in range(KT):
                    row_high_at(t0 + k + 2)
                    if k + 2 < KT:
                        turned_high((Y_H1, Y_H2, Y_MID)[n] + k + 2, h_t[0][:, k + 2, :])
                    if k == 1:
                        row_parts(n)
                    if k == 3 and n == 0:
                        relation_edges(0)
                mean_high(q, 0)

            def relation(q, t0, last, more=True):
                for k in range(KT):
                    if isinstance(t0, int):
                        if t0 + k + 2 < T_END:
                            row_high_at(t0 + k + 2)
                    else:
                        row_high(t0 + (k + 2), (k + 2) % RING, use_of_slot(q + T_REL // KT, k + 2))
                    if k < KT - 1:
                        act.wait_ge(S["w_used"], t0 + (k + W_CREDIT))
                        mean_high(q, k + 1)
                    if k == KT - 2 and not last:
                        act.wait_ge(S["agg_ready"], q * (KT + 1) + (KT + 1))
                        act.activation(rel_r[:, :, :], counts16[:, bass.ds(q * NT + NT, NT), :], ACT.Copy)\
                           .then_inc(S["rel_ready"], 1)
                if not last:
                    act.wait_ge(S["w_used"], t0 + (KT - 1 + W_CREDIT))
                    mean_high(q + 1, 0)

            bias_row(bias1, "y_turned", KT)
            layer_norm(1, h, HALVES, Y_H1)
            own_product(0, T_ROOT, 0)
            with act.Fori(0, R - 1) as r:
                relation(r, T_REL + r * KT, False)
            relation(R - 1, T_REL + (R - 1) * KT, True)
            for k in range(KT):
                row_high_at(T_GX + k + 2)
                turned_high(Y_U + k, u_t[0][:, k, :])
                if k == 1:
                    bias_row(b_gate, "u_ready", 2 * NT)
            for k in range(KT):
                row_high_at(T_GU + k + 2)
                if k < NT:
                    act.wait_ge(S["turned"], Y_U + KT)
                    act.activation(u[:, k, :], u[:, k, :], ACT.Tanh).then_inc(S["u_tanh"], 1)
            bias_row(b0, "gate_sum", NT)
            layer_norm(2, h, HALVES, Y_H2)
            own_product(1, T_S0, R)
            relation(R, T_N0, True)
            for nt in range(NT):
                for f in range(2):
                    half = slice(HALF * f, HALF * f + HALF)
                    act.wait_ge(S["mid_ready"], 2 * nt + f + 1)
                    act.activation(h[:, nt, half], h[:, nt, half], ACT.Relu).then_inc(S["h_ready"], 1)
            bias_row(b1, "mid_ready", 2 * NT)
            turned_high(Y_MID, h_t[0][:, 0, :])
            turned_high(Y_MID + 1, h_t[0][:, 1, :])
            own_product(2, T_S1, R + 1)
            act.activation(w3[0][:, :, :], sparse_w[:, :, :], ACT.Copy).then_inc(S["w3_hi"], 1)
            relation(R + 1, T_N1, True)
            bias_row(bias3, "x_based", NT)
            layer_norm(3, h, [slice(0, N)])
            for f in range(NT):
                turned_high(Y_H3 + f, h_t[0][:, f, :])

        @block.vector
        def _(dve):
            link = Chain(dve, S["vec_chain"])
            dve.sem_inc(S["w_used"], W_CREDIT)
            dve.sem_inc(S["out_lo"], O_CREDIT)
            dve.sem_inc(S["head_lo"], O_CREDIT)
            dve.sem_inc(S["pv_done"], PV_CREDIT)
            for name in ("mask_made", "mean_lo", "any_counts_read"):
                dve.sem_inc(S[name], 1)
            dve.sem_inc(S["hots_used"], HOT_CREDIT)
            dve.sem_inc(S["hot_val_used"], VAL_CREDIT)
            dve.sem_inc(S["dup_found"], M_CREDIT)
            dve.sem_inc(S["any_rel_used"], 4)
            dve.memset(epsc[:, :], EPS).then_inc(S["ones_made"], 1)
            dve.memset(same[:, 0, :], 1.0).then_inc(S["ones_made"], 1)

            dve.wait_ge(S["edges_in"], 16 * 5)
            dve.tensor_copy(e_row[:, SRC, :], e_in[:, 0, :])
            dve.tensor_copy(e_row[:, DST, :], e_in[:, 1, :])
            dve.tensor_copy(e_row[:, TYPE, :], e_in[:, 2, :])
            dve.tensor_copy(e_row[:, WEIGHT, :], e_w[:, :])
            dve.scalar_tensor_tensor(e_row[:, KEY, :], e_in[:, 0, :], float(N), e_in[:, 1, :], ALU.mult, ALU.add)
            dve.tensor_copy(e_row[:, REL, :], e_in[:, 3, :])
            dve.scalar_tensor_tensor(e_row[:, REL_KEY, :], e_in[:, 3, :], float(N), e_in[:, 0, :], ALU.mult, ALU.add)\
               .then_inc(S["edge_rows"], 1)
            def half_stats(nt, f):
                dve.bn_stats(stats[:, nt, f, :], xres[:, nt, HALF * f:HALF * f + HALF]).then_inc(S["half_stats_made"], 1)

            def var_of(n, nt):
                dve.wait_ge(S["half_stats_made"], 2 * NT * n + (NT + nt + 1 if n == 1 else 2 * nt + 2))
                dve.bn_aggr(mv[:, nt, :], stats[:, nt, :, :].rearrange("p a b -> p (a b)")).then_inc(S["var_ready"], 1)

            def norm_stats(n, nt):
                half_stats(nt, 0)
                half_stats(nt, 1)
                var_of(n, nt)

            def norm_shift(n, nt):
                dve.wait_ge(S["std_ready"], NT * n + nt + 1)
                link(dve.reciprocal(rstd[:, nt, :], std[:, nt, :]))
                dve.scalar_tensor_tensor(shift[:, nt, :], mv[:, nt, 0:1], -1.0, rstd[:, nt, :], ALU.mult, ALU.mult)\
                   .then_inc(S["shift_ready"], 1)

            def layer_norm(n, complete):
                complete(0, lambda: None)
                complete(1, lambda: norm_shift(n, 0))
                complete(2, lambda: None)
                norm_shift(n, 1)
                norm_shift(n, 2)

            dve.wait_ge(S["edges_turned"], 1)
            dve.tensor_copy(e_col[:, :, :], ps[:, 0, 0:7 * EC].rearrange("p (f c) -> p f c", f=7))\
               .then_inc(S["edge_cols"], 1)
            dve.wait_ge(S["edge_cols"], 1)
            link(dve.tensor_scalar(rel_exp[:, 0, :], e_col[:, REL, :], float(DIGIT), 127.0, ALU.mult, ALU.add))
            link(dve.tensor_scalar(rel_exp[:, 1, :], rel_exp[:, 0, :], 23, None, ALU.logical_shift_left))
            rel_place = rel_exp[:, 1, :].bitcast(F32)
            link(dve.tensor_copy(w_hi[:, :], e_col[:, WEIGHT, :]))
            link(dve.tensor_tensor(w_lo[:, :], e_col[:, WEIGHT, :], w_hi[:, :].bitcast(F32), ALU.subtract))
            dve.wait_ge(S["iota_made"], 1)
            dve.wait_ge(S["later_made"], 2)

            def one_hots(c0, after=lambda j: None):
                for j in range(4):
                    c = c0 + j
                    col = bass.ds(c, 1)
                    dve.wait_ge(S["hots_used"], c + 1)
                    dve.tensor_scalar(hot_dst[:, c, :], iota[:, :], e_col[:, DST, col], None, ALU.is_equal)
                    dve.tensor_scalar(hot_rel[:, j, :], iota[:, :], e_col[:, DST, col], rel_place[:, col],
                                      ALU.is_equal, ALU.mult)
                    dve.tensor_scalar(hot_src[:, j, :], iota[:, :], e_col[:, SRC, col], None, ALU.is_equal)\
                       .then_inc(S["hots_made"], 1)
                    after(j)

            def find_later(q, first, some):
                for j in some:
                    c = first + (q * QUARTER + j)
                    dve.wait_ge(S["dup_found"], c + 1)
                    dve.scalar_tensor_tensor(same[:, j % 2, :], key_row[:, q % 2, bass.ds((first + j) * P, P)],
                                             e_col[:, KEY, bass.ds(c, 1)], later[:, :], ALU.is_equal, ALU.mult,
                                             accum_out=dup[:, bass.ds(c, 1)]).then_inc(S["dup_found"], 1)

            for seg, (c_first, c_end, quarter, n, keys) in enumerate(SEGMENTS):
                if c_end - c_first == 4:
                    one_hots(c_first)
                else:
                    with dve.Fori(0, (c_end - c_first) // 4) as c4:
                        one_hots(c4 * 4 + c_first, lambda j: find_later(
                            quarter, c4 * n, range(j * n // 4, (j + 1) * n // 4)))
                if seg < NT:
                    dve.wait_ge(S["x_in"], 16)
                    norm_stats(0, seg)
                if keys is not None:
                    dve.wait_ge(S["key_rows_in"], keys * 32 + 32)
                    need(dve, S["dup_found"], (keys - 1) * QUARTER + M_CREDIT if keys > 1 else 0)
                    dve.scalar_tensor_tensor(key_row[:, keys % 2, :], key_i[:, 0, :], float(N), key_i[:, 1, :],
                                             ALU.mult, ALU.add).then_inc(S["keys_made"], 1)
                    dve.wait_ge(S["keys_made"], keys + 1)
                    hold(dve)
                if keys == 1:
                    dve.wait_ge(S["etw_in"], 16)
                    link(dve.tensor_scalar(sp[:, 0, :], etw_b[:, :], 0.0, None, ALU.max))
                    link(dve.tensor_scalar(sp[:, 1, :], etw_b[:, :], -1.0, None, ALU.mult))
                    dve.tensor_tensor(sp[:, 2, :], etw_b[:, :], sp[:, 1, :], ALU.max).then_inc(S["sp_max"], 1)
            for nt in range(NT):
                norm_shift(0, nt)
            dve.wait_ge(S["exp_made"], 1)
            dve.wait_ge(S["dup_found"], EC + M_CREDIT)
            link(dve.tensor_scalar(live[:, :], dup[:, :], 0.0, None, ALU.is_equal))
            link(dve.tensor_scalar(chunk_val[:, :], chunk_exp[:, :], 23, None, ALU.logical_shift_left))
            link(dve.tensor_scalar(edge_val[:, :], e_col[:, TYPE, :], 0.125, 1.0, ALU.mult, ALU.add))
            link(dve.tensor_tensor(edge_val[:, :], edge_val[:, :], live[:, :], ALU.mult))
            link(dve.tensor_tensor(edge_val[:, :], edge_val[:, :], chunk_val[:, :].bitcast(F32), ALU.mult))

            def turned_low(y, target, hi):
                dve.wait_ge(S["turn_hi"], y + 1)
                dve.tensor_tensor(target, ps[:, 6 + y % 2, 0:N], hi.bitcast(F32), ALU.subtract).then_inc(S["turn_lo"], 1)

            def code_rows(c0, c1):
                for c in range(c0, c1):
                    dve.wait_ge(S["hot_val_used"], c + 1)
                    dve.tensor_scalar(hot_val[:, c % 3, :], iota[:, :], e_col[:, SRC, c:c + 1], edge_val[:, c:c + 1],
                                      ALU.is_equal, ALU.mult).then_inc(S["hot_val_made"], 1)

            code_rows(0, 3)
            dve.wait_ge(S["hots_used"], EC + HOT_CREDIT)
            dve.tensor_scalar(packed.rearrange("p (t n) -> p t n", t=NT), ps[:, 0:NT, 0:N], 2.0 ** 30, None,
                              ALU.min).then_inc(S["packed_made"], 1)
            dve.wait_ge(S["edges_turned"], 2)
            dve.tensor_copy(bcol[:, :], ps[:, 7, 0:7 * KT]).then_inc(S["edge_cols"], 1)
            dve.wait_ge(S["packed_made"], 1)
            for r in range(R):
                need(dve, S["digits_kept"], r - 1)
                if r < R - 1:
                    ins = dve.tensor_scalar(digits[r % 2], packed, DIGIT * r, 2 ** DIGIT - 1,
                                            ALU.logical_shift_right, ALU.bitwise_and)
                else:
                    ins = dve.tensor_scalar(digits[r % 2], packed, DIGIT * r, None,
                                            ALU.logical_shift_right)
                ins.then_inc(S["digits_made"], 1)
                code_rows(max(r * EC // R, 3), r * EC // R + 4)
                if r:
                    turned_low(Y_H0 + r - 1, acts[:, 0, 1, r - 1, :], acts[:, 0, 0, r - 1, :])
                code_rows(r * EC // R + 4, (r + 1) * EC // R)
            def column_low(g, j):
                dve.wait_ge(S["w_hi"], g * KT + (j + 1))
                b = 4 - 2 * (j % 2)
                dve.tensor_tensor(wlo[j % RING][:, :, :],
                                  ps[:, b:b + 2, :].rearrange("p b (k n) -> p (b k) n", n=P),
                                  whi[j % RING][:, :, :].bitcast(F32), ALU.subtract).then_inc(S["w_lo"], 1)

            dve.wait_ge(S["hot_val_used"], EC + VAL_CREDIT)
            types = packed
            dve.tensor_copy(codes.bitcast(F32).rearrange("p (t n) -> p t n", t=NT), ps[:, 0:NT, 0:N])\
               .then_inc(S["mask_decoded"], 1)
            turned_low(Y_H0 + KT - 1, acts[:, 0, 1, KT - 1, :], acts[:, 0, 0, KT - 1, :])
            column_low(0, 0)
            column_low(0, 1)
            dve.wait_ge(S["mask_decoded"], 1)
            link(dve.tensor_scalar(types, codes, 20, 7, ALU.logical_shift_right, ALU.bitwise_and))
            dve.wait_ge(S["digits_kept"], R - 1)
            dve.tensor_copy(key_row[:, 0, 0:NT * N], types).then_inc(S["mask_decoded"], 1)
            dve.wait_ge(S["sp_ln"], 1)
            dve.tensor_tensor(sp[:, 5, :], sp[:, 0, :], sp[:, 4, :], ALU.add).then_inc(S["sp_made"], 1)

            def row_low(t, slot):
                dve.wait_ge(S["w_hi"], t + 1)
                dve.tensor_tensor(wlo_row[slot], raw[slot][:, :], whi_row[slot].bitcast(F32), ALU.subtract)\
                   .then_inc(S["w_lo"], 1)

            dve.wait_ge(S["digits_kept"], R)
            link(dve.tensor_reduce(digit_sum[:, R:R + 1], digit_sum[:, 0:R], AX.X, ALU.add))
            link(dve.tensor_reduce(digit_sum[:, R + 1:R + 2], digits[(R - 1) % 2], AX.X, ALU.max))
            link(dve.tensor_scalar(digit_sum[:, R + 1:R + 2], digit_sum[:, R + 1:R + 2], float(2 ** DIGIT),
                                   float(2 * E), ALU.is_ge, ALU.mult))
            dve.tensor_tensor(digit_sum[:, R + 2:R + 3], digit_sum[:, R:R + 1], digit_sum[:, R + 1:R + 2], ALU.add)\
               .then_inc(S["check_ready"], 1)

            def eight_tiles(g, a):
                for j in range(KT):
                    column_low(g, j + 2)
                    dve.wait_ge(S["out_hi"], g * KT + (j + 1))
                    dve.scalar_tensor_tensor(acts[:, a, 1, j, :], ps[:, j % 2, 0:N], bcol[:, bass.ds(g * KT + j, 1)],
                                             acts[:, a, 0, j, :].bitcast(F32), ALU.add, ALU.subtract)\
                       .then_inc(S["out_lo"], 1)

            with dve.Fori(0, 3) as g:
                eight_tiles(g, g + 1)
            dve.wait_ge(S["check_summed"], 1)
            dve.tensor_scalar(no_digits[:, :], ps[:, 7, 0:1], float(E), None, ALU.not_equal).then_inc(S["check_made"], 1)
            with dve.Fori(3, 6) as g:
                eight_tiles(g, g - 3)
            dve.wait_ge(S["mask_made"], 2)

            def score_max(i, o):
                for nt in range(NT):
                    dve.wait_ge(S["scores_ready"], (i * 4 + o) * NT + (nt + 1))
                    need(dve, S["probs_turned"], (i * 4 + (o - 1)) * NT)
                    hold(dve)
                    dve.tensor_tensor_reduce(sc[:, o % 2, nt, :], ps[:, nt, 0:N], mask[:, nt, :], -SCALE, 3e38,
                                             ALU.add, ALU.min, nmax[:, o % 2, nt:nt + 1]).then_inc(S["scores_read"], 1)

            def invert_sum(i, o, nt):
                dve.wait_ge(S["exp_ready"], (i * 4 + o) * NT + (nt + 1))
                dve.reciprocal(rinv[:, o % 2, nt:nt + 1], rsum[:, o % 2, nt:nt + 1]).then_inc(S["sum_inverted"], 1)

            def normalise(i, o):
                invert_sum(i, o, NT - 1)
                dve.wait_ge(S["sum_inverted"], (i * 4 + (o + 1)) * NT)
                dve.tensor_scalar(sc[:, o % 2, NT - 1, :], sc[:, o % 2, NT - 1, :], rinv[:, o % 2, NT - 1:NT],
                                  None, ALU.mult).then_inc(S["probs_by_vec"], 1)

            def head(i, o):
                for m in range(NT):
                    if m == 1 and exists(i, o + 2):
                        score_max(i, o + 2)
                        invert_sum(i, o + 2, 0)
                    if m == 2 and exists(i, o + 2):
                        invert_sum(i, o + 2, 1)
                    dve.wait_ge(S["pt_hi"], (i * 4 + o) * NT + (m + 1))
                    dve.tensor_tensor(pt[1][:, o % 2, m, :], ps[:, NT + m, 0:N], pt[0][:, o % 2, m, :].bitcast(F32),
                                      ALU.subtract).then_inc(S["pt_lo"], 1)
                if exists(i, o + 2):
                    normalise(i, o + 2)
                if not is_head(i, o, 0):
                    head_out(i, o - 1)

            def head_out(i, o):
                r = DH * (o % 2)
                dve.wait_ge(S["head_hi"], i * 4 + (o + 1))
                dve.tensor_tensor(acts[r:r + DH, 0, 1, i * 2 + o // 2, :], ps[r:r + DH, 6 + o % 2, 0:N],
                                  acts[r:r + DH, 0, 0, i * 2 + o // 2, :].bitcast(F32), ALU.subtract)\
                   .then_inc(S["head_lo"], 1)

            score_max(0, 0)
            for nt in range(NT - 1):
                invert_sum(0, 0, nt)
            normalise(0, 0)
            for m in range(NT):
                dve.wait_ge(S["v_turned"], 2 * m + 2)
                dve.tensor_copy(v_rows[:, 1, m, :], ps[:, 6:8, :].rearrange("p b n -> p (b n)")).then_inc(S["v_lo"], 1)
            score_max(0, 1)
            for nt in range(NT - 1):
                invert_sum(0, 1, nt)
            normalise(0, 1)
            head(0, 0)
            with dve.Fori(0, 3) as i:
                for o in range(1, 5):
                    head(i, o)
            for o in range(1, 4):
                head(3, o)
            head_out(3, 3)

            def add_y(j):
                dve.wait_ge(S["y_turned"], j + 1)
                dve.tensor_tensor(xres[:, :, P * j:P * j + P], xres[:, :, P * j:P * j + P],
                                  ps[:, 6 + j % 2, 0:N].rearrange("p (t n) -> p t n", t=NT), ALU.add)\
                   .then_inc(S["y_added"], 1)

            dve.wait_ge(S["check_made"], 1)
            again = dve.value_load(no_digits[0:1, 0:1], min_val=0, max_val=1)
            dve.wait_ge(S["x_in"], 32)
            for j in range(KT):
                if j + 2 < KT:
                    column_low(6, j + 2)
                else:
                    row_low(T_WO + j + 2, (j + 2) % RING)
                if j:
                    add_y(j - 1)
                if 4 < j:
                    dve.wait_ge(S["y_added"], KT // 2)
                    half_stats(j - 5, 0)
            add_y(KT - 1)
            dve.wait_ge(S["y_added"], KT)

            with dve.If(again > 0):
                with dve.Fori(0, EC) as c:
                    dve.tensor_scalar(any_dst[:, c, :], iota[:, :], e_col[:, DST, bass.ds(c, 1)],
                                      None, ALU.is_equal).then_inc(S["any_dst_made"], 1)
                with dve.Fori(0, R) as r:
                    with dve.Fori(0, EC // 4) as c4:
                        for j in range(4):
                            dve.wait_ge(S["any_rel_used"], r * EC + (c4 * 4 + (j + 1)))
                            dve.tensor_scalar(any_rel[:, j, :], iota[:, :], e_col[:, REL_KEY, bass.ds(c4 * 4 + j, 1)],
                                              None, ALU.is_equal).then_inc(S["any_rel_made"], 1)
                    dve.wait_ge(S["any_rel_used"], r * EC + (EC + 4))
                    dve.tensor_copy(counts16[:, bass.ds(r * NT, NT), :], ps[:, 0:NT, 0:N])\
                       .then_inc(S["any_counts_read"], 1)
                    dve.tensor_scalar(e_col[:, REL_KEY, :], e_col[:, REL_KEY, :], -float(N), None, ALU.add)\
                       .then_inc(S["any_key_moved"], 1)
                    dve.wait_ge(S["any_key_moved"], r + 1)
                    hold(dve)
                dve.wait_ge(S["any_counts_read"], R + 1)
            dve.sem_inc(S["counts_final"], 1)

            def read_sums(q, k):
                dve.wait_ge(S["agg_ready"], q * (KT + 1) + (k + 2))
                need(dve, S["mean_lo"], q * KT + k)
                dve.tensor_tensor(mean_f[:, k % 2, :], ps[:, 7 - k % 2, 0:N], inv[:, :], ALU.mult)\
                   .then_inc(S["agg_read"], 1)

            def read_counts(q):
                dve.wait_ge(S["agg_ready"], q * (KT + 1) + 1)
                dve.tensor_scalar(cnt[:, :], ps[:, 6, 0:N], 1.0, None, ALU.max).then_inc(S["agg_read"], 1)
                dve.wait_ge(S["agg_read"], q * (KT + 1) + 1)
                dve.reciprocal(inv[:, :], cnt[:, :]).then_inc(S["inv_made"], 1)
                dve.wait_ge(S["inv_made"], q + 1)

            def own_product(n, t0, q):
                for k in range(KT):
                    row_low(t0 + k + 2, (k + 2) % RING)
                    if k + 2 < KT:
                        turned_low((Y_H1, Y_H2, Y_MID)[n] + k + 2, h_t[1][:, k + 2, :], h_t[0][:, k + 2, :])
                read_counts(q)
                read_sums(q, 0)

            def relation(q, t0, last):
                for k in range(KT):
                    if not isinstance(t0, int) or t0 + k + 2 < T_END:
                        row_low(t0 + (k + 2), (k + 2) % RING)
                    if k < KT - 1:
                        read_sums(q, k + 1)
                if not last:
                    read_counts(q + 1)
                    read_sums(q + 1, 0)

            def sum_of(n, t_last, nt):
                if nt < NT - 1:
                    dve.wait_ge(S["sum_ready"], (NT - 1) * n + nt + 1)
                else:
                    dve.wait_ge(S["w_used"], t_last + 1 + W_CREDIT)

            def second_half(nt, meanwhile):
                half_stats(nt, 1)
                meanwhile()
                var_of(1, nt)

            layer_norm(1, second_half)
            turned_low(Y_H1, h_t[1][:, 0, :], h_t[0][:, 0, :])
            turned_low(Y_H1 + 1, h_t[1][:, 1, :], h_t[0][:, 1, :])
            own_product(0, T_ROOT, 0)
            with dve.Fori(0, R - 1) as r:
                relation(r, T_REL + r * KT, False)
            relation(R - 1, T_REL + (R - 1) * KT, True)

            def add_bias(n, t_last, target, done):
                for nt in range(NT):
                    sum_of(n, t_last, nt)
                    for f in range(2):
                        half = slice(HALF * f, HALF * f + HALF)
                        dve.tensor_tensor(target[:, nt, half], ps[:, 2 * nt + f, :], brow[:, half], ALU.add)\
                           .then_inc(S[done], 1)

            dve.wait_ge(S["brow_in"], 16)
            add_bias(0, T_GX - 1, u, "u_ready")
            for k in range(KT):
                row_low(T_GX + k + 2, (k + 2) % RING)
                turned_low(Y_U + k, u_t[1][:, k, :], u_t[0][:, k, :])
                if k < NT:
                    link(dve.tensor_reduce(mask[:, k, :], counts16[:, :, :].rearrange(
                        "p (r t) n -> p t n r", t=NT)[:, k], AX.X, ALU.add))
                    dve.tensor_copy(total_r[:, k, :], mask[:, k, :]).then_inc(S["total_made"], 1)
            for k in range(KT):
                row_low(T_GU + k + 2, (k + 2) % RING)
            def gated(nt):
                sum_of(1, T_S0 - 1, nt)
                dve.wait_ge(S["gate_sum"], nt + 1)
                for f in range(2):
                    half = slice(HALF * f, HALF * f + HALF)
                    dve.tensor_tensor(h[:, nt, half], ps[:, 2 * nt + f, :], u[:, nt, half], ALU.mult)\
                       .then_inc(S["gate_product"], 1)
                if nt < NT - 1:
                    return
                for f in range(2):
                    half = slice(HALF * f, HALF * f + HALF)
                    dve.wait_ge(S["gate_product"], 2 * nt + f + 1)
                    dve.tensor_tensor(xres[:, nt, half], xres[:, nt, half], h[:, nt, half], ALU.add)\
                       .then_inc(S["x_gated_last"], 1)

            def gated_stats(nt, meanwhile):
                for f in range(2):
                    if nt < NT - 1:
                        dve.wait_ge(S["x_gated"], nt + 1)
                    else:
                        dve.wait_ge(S["x_gated_last"], f + 1)
                    half_stats(nt, f)
                meanwhile()
                var_of(2, nt)

            for nt in range(NT):
                gated(nt)
            layer_norm(2, gated_stats)
            turned_low(Y_H2, h_t[1][:, 0, :], h_t[0][:, 0, :])
            turned_low(Y_H2 + 1, h_t[1][:, 1, :], h_t[0][:, 1, :])
            own_product(1, T_S0, R)
            relation(R, T_N0, True)
            dve.wait_ge(S["brow_in"], 16 * 3)
            add_bias(2, T_S1 - 1, h, "mid_ready")
            turned_low(Y_MID, h_t[1][:, 0, :], h_t[0][:, 0, :])
            turned_low(Y_MID + 1, h_t[1][:, 1, :], h_t[0][:, 1, :])
            own_product(2, T_S1, R + 1)
            dve.wait_ge(S["w3_hi"], 1)
            dve.tensor_tensor(w3[1][:, :, :], sparse_w[:, :, :], w3[0][:, :, :].bitcast(F32), ALU.subtract)\
               .then_inc(S["w3_lo"], 1)
            relation(R + 1, T_N1, True)
            dve.wait_ge(S["x_based"], NT)
            def summed(nt, meanwhile):
                sum_of(3, T_END - 1, nt)
                for f in range(2):
                    half = slice(HALF * f, HALF * f + HALF)
                    dve.tensor_tensor(xres[:, nt, half], xres[:, nt, half], ps[:, 2 * nt + f, :], ALU.add)\
                       .then_inc(S["x_done"], 1)
                meanwhile()
                for f in range(2):
                    dve.wait_ge(S["x_done"], 2 * nt + f + 1)
                    half_stats(nt, f)
                var_of(3, nt)

            layer_norm(3, summed)
            for f in range(NT):
                turned_low(Y_H3 + f, h_t[1][:, f, :], h_t[0][:, f, :])
            for nt in range(NT):
                dve.wait_ge(S["out_psum"], nt + 1)
                dve.wait_ge(S["out_based"], nt + 1)
                dve.tensor_tensor(u[:, nt, 0:N], u[:, nt, 0:N], ps[:, nt, 0:N], ALU.add).then_inc(S["out_done"], 1)

        @block.gpsimd
        def _(pool):
            link = Chain(pool, S["pool_chain"])
            pool.memset(ident[:, :], 0.0).then_inc(S["ident_made"], 1)
            pool.wait_ge(S["ident_made"], 1)
            pool.affine_select(out=ident[:, :], in_=ident[:, :], compare_op=ALU.not_equal, fill=1.0, base=0,
                               pattern=[[-1, P]], channel_multiplier=1).then_inc(S["ident_made"], 1)
            pool.iota(iota[:, :], pattern=[[1, N]], base=0, channel_multiplier=0).then_inc(S["iota_made"], 1)
            pool.memset(later[:, :], 1.0).then_inc(S["later_made"], 1)
            pool.wait_ge(S["later_made"], 1)
            pool.affine_select(out=later[:, :], in_=later[:, :], compare_op=ALU.is_gt, fill=0.0, base=0,
                               pattern=[[1, P]], channel_multiplier=-1).then_inc(S["later_made"], 1)
            pool.iota(chunk_exp[:, :], pattern=[[EXP_STEP, EC]], base=EXP_BASE + 127, channel_multiplier=0)\
                .then_inc(S["exp_made"], 1)

            with pool.Fori(0, EC // 2) as c2:
                pool.wait_ge(S["hots_made"], c2 * 2 + 1)
                pool.wait_ge(S["hots_used"], c2 * 2 + (HOT_CREDIT - 1))
                pool.tensor_copy(dst_r[:, 0, :], hot_dst[:, c2 * 2, :]).then_inc(S["hot_dst_even_made"], 1)

            pool.wait_ge(S["mask_decoded"], 2)
            types = key_row[:, 0, 0:NT * N]
            empty = key_i[:, 1, 0:NT * N].bitcast(F32)
            flat = mask[:, :, :].rearrange("p t n -> p (t n)")
            pool.wait_ge(S["sp_made"], 1)
            pool.wait_ge(S["check_ready"], 1)
            term = key_row[:, 1, 0:NT * N]
            link(pool.tensor_scalar(flat, types, 0.0, sp[:, 5, 3:4], ALU.is_equal, ALU.mult))
            for t in range(1, 5):
                link(pool.tensor_scalar(term, types, float(t), sp[:, 5, t - 1:t], ALU.is_equal, ALU.mult))
                link(pool.tensor_tensor(flat, flat, term, ALU.add))
            link(pool.tensor_scalar(empty, empty, 0.0, MASKED, ALU.is_equal, ALU.mult))
            link(pool.affine_select(out=empty.rearrange("p (t n) -> p t n", t=NT),
                                    in_=empty.rearrange("p (t n) -> p t n", t=NT),
                                    compare_op=ALU.not_equal, fill=0.0, base=0,
                                    pattern=[[-P, NT], [1, N]], channel_multiplier=-1))
            link(pool.tensor_tensor(flat, flat, empty, ALU.add))
            pool.tensor_scalar(flat, flat, 1.0 / SCALE, None, ALU.mult).then_inc(S["mask_made"], 1)

            pool.wait_ge(S["mask_made"], 2)
            for o in range(2):
                for a in range(2):
                    r0 = DH * (1 - o)
                    pool.memset(q_st[r0:r0 + DH, a, o, :].bitcast(F32), 0.0).then_inc(S["q_cleared"], 1)
                    pool.wait_ge(S["q_cleared"], 2 * o + a + 1)

            def normalise(i, o):
                for nt in range(NT - 1):
                    pool.wait_ge(S["sum_inverted"], (i * 4 + o) * NT + (nt + 1))
                    hold(pool)
                    pool.tensor_scalar(sc[:, o % 2, nt, :], sc[:, o % 2, nt, :], rinv[:, o % 2, nt:nt + 1],
                                       None, ALU.mult).then_inc(S["probs_by_pool"], 1)

            with pool.Fori(0, H // 4) as i:
                for o in range(4):
                    normalise(i, o)

            def row_parts(n):
                for nt in range(NT):
                    pool.wait_ge(S["row_hi"], NT * n + nt + 1)
                    pool.tensor_tensor(h_row[1][:, nt, :], h[:, nt, :], h_row[0][:, nt, :].bitcast(F32), ALU.subtract)\
                        .then_inc(S["row_lo"], 1)

            def mean_low(q, k):
                pool.wait_ge(S["mean_hi"], q * KT + (k + 1))
                pool.tensor_tensor(mean[1][:, k % 2, :], mean_f[:, k % 2, :], mean[0][:, k % 2, :].bitcast(F32),
                                   ALU.subtract).then_inc(S["mean_lo"], 1)

            row_parts(0)
            mean_low(0, 0)
            with pool.Fori(0, R - 1) as r:
                for k in range(KT):
                    mean_low(r, k + 1)
            for k in range(1, KT):
                mean_low(R - 1, k)
            for nt in range(NT):
                link(pool.tensor_tensor(xres[:, nt, :], xres[:, nt, :], h[:, nt, :], ALU.add))
            pool.wait_ge(S["brow_in"], 16 * 2)
            for nt in range(NT):
                pool.wait_ge(S["u_tanh"], nt + 1)
                link(pool.tensor_tensor(u[:, nt, :], u[:, nt, :], h[:, nt, :], ALU.subtract))
                link(pool.tensor_tensor(h[:, nt, :], u[:, nt, :], brow[:, :], ALU.mult))
                pool.tensor_tensor(xres[:, nt, :], xres[:, nt, :], h[:, nt, :], ALU.add).then_inc(S["gate_sum"], 1)
            pool.wait_ge(S["gate_sum"], NT)
            for nt in range(NT - 1):
                pool.wait_ge(S["gate_product"], 2 * nt + 2)
                pool.tensor_tensor(xres[:, nt, :], xres[:, nt, :], h[:, nt, :], ALU.add).then_inc(S["x_gated"], 1)
            row_parts(1)
            for k in range(KT):
                mean_low(R, k)
            row_parts(2)
            pool.wait_ge(S["brow_in"], 16 * 4)
            for nt in range(NT):
                pool.tensor_tensor(xres[:, nt, :], xres[:, nt, :], brow[:, :], ALU.add).then_inc(S["x_based"], 1)
            for k in range(KT):
                mean_low(R + 1, k)
            pool.wait_ge(S["brow_in"], 16 * 5)
            for nt in range(NT):
                pool.wait_ge(S["x_done"], 2 * nt + 2)
                pool.tensor_tensor(u[:, nt, :], xres[:, nt, :], brow[:, :], ALU.add).then_inc(S["out_based"], 1)


_INS = ["x", "src", "dst", "edge_type_5", "edge_type_8", "edge_weight", "L0_gnn_edge_type_weights",
        "L0_gnn_wq", "L0_gnn_bq", "L0_gnn_wk", "L0_gnn_bk", "L0_gnn_wv", "L0_gnn_bv", "L0_gnn_wiq",
        "L0_gnn_biq", "L0_gnn_wik", "L0_gnn_bik", "L0_gnn_wiv", "L0_gnn_biv", "L0_gnn_wo", "L0_gnn_bo",
        "L1_gnn_weight", "L1_gnn_root", "L1_gnn_bias", "L1_gnn_w_gate", "L1_gnn_b_gate",
        "L2_gnn_W_self0", "L2_gnn_W_neigh0", "L2_gnn_b0", "L2_gnn_W_self1", "L2_gnn_W_neigh1",
        "L2_gnn_b1", "L3_gnn_bias"]


def kernel(**inputs):
    import numpy as _np
    import concourse.bacc as _bacc
    from concourse import mybir as _mybir
    from concourse.bass_utils import run_bass_kernel_spmd as _run

    nc = _bacc.Bacc("TRN2", target_bir_lowering=False, num_devices=1)
    arrays, args = {}, []
    for name in _INS:
        a = _np.ascontiguousarray(inputs[name])
        arrays[f"in_{name}"] = a
        args.append(nc.dram_tensor(f"in_{name}", a.shape, _mybir.dt.from_np(a.dtype), kind="ExternalInput").ap())
    a = inputs["x"]
    args.append(nc.dram_tensor("out_0", a.shape, _mybir.dt.float32, kind="ExternalOutput").ap())
    build(nc, *args)
    r = _run(nc, [arrays], core_ids=[0])
    return r.results[0]["out_0"]
```
